# Optimizing a Trainium2 kernel written in Bass

```python
import numpy as np
import jax
import jax.numpy as jnp

def _softmax(x, axis=-1):
    return jax.nn.softmax(x, axis=axis)

def _gelu(x):
    return jax.nn.gelu(x, approximate=True)

def _silu(x):
    return jax.nn.silu(x)

def _sigmoid(x):
    return jax.nn.sigmoid(x)

def _layernorm(x, axis=-1, eps=1e-05):
    m = jnp.mean(x, axis=axis, keepdims=True)
    v = jnp.var(x, axis=axis, keepdims=True)
    return (x - m) / jnp.sqrt(v + eps)

def _scatter_add(tgt, idx, src, axis=0):
    return tgt.at[idx].add(src)

def _segment_sum(src, seg, n):
    return jax.ops.segment_sum(src, seg, n)
kernel_name = 'mk_flamingo_gated_d2_seqx_r2_8d3599'

def setup_inputs(seed: int=0):
    np.random.seed(seed)
    _w = jnp.asarray

    def _rec_inputs():
        import jax
        import jax.numpy as jnp
        _rk = jax.random.key(seed)
        x = -0.0002928 + 1 * jax.random.normal(jax.random.fold_in(_rk, 1), (8, 512, 512), jnp.float32)
        _lenS = 512 - jax.random.randint(jax.random.fold_in(_rk, 7), (8,), 0, max(1, 512 // 4) + 1, jnp.int32)
        _lenS2 = 77 - jax.random.randint(jax.random.fold_in(_rk, 8), (8,), 0, max(1, 77 // 4) + 1, jnp.int32)
        _ctx_1024P = jax.random.normal(jax.random.fold_in(_rk, 11), (8, 16, 512), jnp.float32)
        _ctx_1024c = jax.random.dirichlet(jax.random.fold_in(_rk, 511), 0.3 * jnp.ones((16,), jnp.float32), (8, 77))
        _ctx_1024t = jnp.einsum('bsk,bkd->bsd', _ctx_1024c, _ctx_1024P)
        _ctx_1024t = _ctx_1024t * jax.lax.rsqrt(jnp.mean(jnp.square(_ctx_1024t)) + 1e-12) * 0.953939
        ctx_1024 = -1.39393e-06 + 0.999914 * (_ctx_1024t + 0.3 * jax.random.normal(jax.random.fold_in(_rk, 611), (8, 77, 512), jnp.float32))
        _g = jax.random.normal(jax.random.fold_in(_rk, 9001), (2, 2), jnp.float32)
        _g = jnp.sign(_g) * jnp.maximum(jnp.abs(_g), 1.0) + (_g == 0) * 1.0
        g_xattn = _g[0]
        g_ffn = _g[1]
        return (x, ctx_1024, g_xattn, g_ffn)
    x, ctx_1024, g_xattn, g_ffn = _rec_inputs()

    def _L0_xattn_setup():
        import jax, jax.numpy as jnp
        import numpy as np
        DIM = 512
        NUM_HEADS = 16
        HEAD_DIM = DIM // NUM_HEADS
        key = jax.random.key(seed)
        ks = jax.random.split(key, 11)
        B, N, C = (2, 1024, DIM)
        s = 1.0 / np.sqrt(C)
        inp = {'q': jax.random.normal(ks[0], (B, N, C), jnp.float32), 'k': jax.random.normal(ks[1], (B, N, C), jnp.float32), 'v': jax.random.normal(ks[2], (B, N, C), jnp.float32), 'Wq': jax.random.normal(ks[3], (C, C), jnp.float32) * s, 'bq': jnp.zeros((C,), jnp.float32), 'Wk': jax.random.normal(ks[4], (C, C), jnp.float32) * s, 'bk': jnp.zeros((C,), jnp.float32), 'Wv': jax.random.normal(ks[5], (C, C), jnp.float32) * s, 'bv': jnp.zeros((C,), jnp.float32), 'Wo': jax.random.normal(ks[6], (C, C), jnp.float32) * s, 'bo': jnp.zeros((C,), jnp.float32)}
        return inp
    _L0_xattn_all = _L0_xattn_setup()
    _L0_xattn_in = {k: v for k, v in _L0_xattn_all.items() if k in ('Wq', 'bq', 'Wk', 'bk', 'Wv', 'bv', 'Wo', 'bo')}
    del _L0_xattn_all

    def _L0_ffn_setup():
        import jax, jax.numpy as jnp
        import numpy as np
        BEST_K = 2

        def _expert(xf, w1, w3, w2):
            return jax.nn.silu(xf @ w1) * (xf @ w3) @ w2
        key = jax.random.key(seed)
        ks = jax.random.split(key, 9)
        E, S_sh, D, H = (8, 2, 512, 256)
        B, S = (2, 1024)
        w = lambda k, shape: jax.random.normal(k, shape, dtype=jnp.float32) * 0.02
        return {'x': jax.random.normal(ks[0], (B, S, D), dtype=jnp.float32), 'router_w': w(ks[1], (D, E)), 'router_b': jnp.zeros((E,), dtype=jnp.float32), 'routed_w1': w(ks[2], (E, D, H)), 'routed_w3': w(ks[3], (E, D, H)), 'routed_w2': w(ks[4], (E, H, D)), 'shared_w1': w(ks[5], (S_sh, D, H)), 'shared_w3': w(ks[6], (S_sh, D, H)), 'shared_w2': w(ks[7], (S_sh, H, D))}
    _L0_ffn_all = _L0_ffn_setup()
    _L0_ffn_in = {k: v for k, v in _L0_ffn_all.items() if k in ('router_w', 'router_b', 'routed_w1', 'routed_w3', 'routed_w2', 'shared_w1', 'shared_w3', 'shared_w2')}
    del _L0_ffn_all

    def _L1_xattn_setup():
        import jax, jax.numpy as jnp
        import numpy as np
        key = jax.random.key(seed)
        k1, k2 = jax.random.split(key)
        hidden_states = jax.random.normal(k1, (8, 2048, 512), dtype=jnp.float32)
        visual_hidden_state = jax.random.normal(k2, (8, 512, 512), dtype=jnp.float32)
        return {'hidden_states': hidden_states, 'visual_hidden_state': visual_hidden_state}
    _L1_xattn_all = _L1_xattn_setup()
    _L1_xattn_in = {k: v for k, v in _L1_xattn_all.items() if k in ()}
    del _L1_xattn_all

    def _L1_ffn_setup():
        import jax, jax.numpy as jnp
        import numpy as np
        B, S, D_MODEL, D_HIDDEN = (4, 1024, 512, 2048)

        def act_quant(x):
            scale = 127.0 / jnp.clip(jnp.max(jnp.abs(x), axis=-1, keepdims=True), 1e-05)
            return jnp.clip(jnp.round(x * scale), -128, 127) / scale

        def weight_quant(w):
            scale = 1.0 / jnp.clip(jnp.mean(jnp.abs(w)), 1e-05)
            return jnp.clip(jnp.round(w * scale), -1, 1) / scale

        def bit_linear(x, w):
            xq = x + jax.lax.stop_gradient(act_quant(x) - x)
            wq = w + jax.lax.stop_gradient(weight_quant(w) - w)
            return jnp.einsum('bsd,hd->bsh', xq, wq)

        def depthwise_conv1d(x_bcl, w, b):
            y = jax.lax.conv_general_dilated(x_bcl, w, window_strides=(1,), padding=[(1, 1)], dimension_numbers=('NCH', 'OIH', 'NCH'), feature_group_count=x_bcl.shape[1])
            return y + b[None, :, None]
        key = jax.random.key(seed)
        ks = jax.random.split(key, 5)
        lim1 = 1.0 / np.sqrt(D_MODEL)
        lim2 = 1.0 / np.sqrt(D_HIDDEN)
        limc = 1.0 / np.sqrt(3.0)
        return {'x': jax.random.normal(ks[0], (B, S, D_MODEL), dtype=jnp.float32), 'w1': jax.random.uniform(ks[1], (D_HIDDEN, D_MODEL), jnp.float32, -lim1, lim1), 'conv_w': jax.random.uniform(ks[2], (D_HIDDEN, 1, 3), jnp.float32, -limc, limc), 'conv_b': jax.random.uniform(ks[3], (D_HIDDEN,), jnp.float32, -limc, limc), 'w2': jax.random.uniform(ks[4], (D_MODEL, D_HIDDEN), jnp.float32, -lim2, lim2)}
    _L1_ffn_all = _L1_ffn_setup()
    _L1_ffn_in = {k: v for k, v in _L1_ffn_all.items() if k in ('w1', 'conv_w', 'conv_b', 'w2')}
    del _L1_ffn_all
    return {'x': x, 'ctx_1024': ctx_1024, 'g_xattn': g_xattn, 'g_ffn': g_ffn, 'L0_xattn_Wq': _L0_xattn_in['Wq'], 'L0_xattn_bq': _L0_xattn_in['bq'], 'L0_xattn_Wk': _L0_xattn_in['Wk'], 'L0_xattn_bk': _L0_xattn_in['bk'], 'L0_xattn_Wv': _L0_xattn_in['Wv'], 'L0_xattn_bv': _L0_xattn_in['bv'], 'L0_xattn_Wo': _L0_xattn_in['Wo'], 'L0_xattn_bo': _L0_xattn_in['bo'], 'L0_ffn_router_w': _L0_ffn_in['router_w'], 'L0_ffn_router_b': _L0_ffn_in['router_b'], 'L0_ffn_routed_w1': _L0_ffn_in['routed_w1'], 'L0_ffn_routed_w3': _L0_ffn_in['routed_w3'], 'L0_ffn_routed_w2': _L0_ffn_in['routed_w2'], 'L0_ffn_shared_w1': _L0_ffn_in['shared_w1'], 'L0_ffn_shared_w3': _L0_ffn_in['shared_w3'], 'L0_ffn_shared_w2': _L0_ffn_in['shared_w2'], 'L1_ffn_w1': _L1_ffn_in['w1'], 'L1_ffn_conv_w': _L1_ffn_in['conv_w'], 'L1_ffn_conv_b': _L1_ffn_in['conv_b'], 'L1_ffn_w2': _L1_ffn_in['w2']}

def reference(x, ctx_1024, g_xattn, g_ffn, L0_xattn_Wq, L0_xattn_bq, L0_xattn_Wk, L0_xattn_bk, L0_xattn_Wv, L0_xattn_bv, L0_xattn_Wo, L0_xattn_bo, L0_ffn_router_w, L0_ffn_router_b, L0_ffn_routed_w1, L0_ffn_routed_w3, L0_ffn_routed_w2, L0_ffn_shared_w1, L0_ffn_shared_w3, L0_ffn_shared_w2, L1_ffn_w1, L1_ffn_conv_w, L1_ffn_conv_b, L1_ffn_w2):
    import jax
    import jax.numpy as jnp

    def _L0_xattn_ref(q, k, v, Wq, bq, Wk, bk, Wv, bv, Wo, bo):
        import jax, jax.numpy as jnp
        import numpy as np
        DIM = 512
        NUM_HEADS = 16
        HEAD_DIM = DIM // NUM_HEADS
        B, Nq, C = q.shape
        Nkv = k.shape[1]
        H, D = (NUM_HEADS, HEAD_DIM)
        qh = (q @ Wq.T + bq).reshape(B, Nq, H, D).transpose(0, 2, 1, 3)
        kh = (k @ Wk.T + bk).reshape(B, Nkv, H, D).transpose(0, 2, 1, 3)
        vh = (v @ Wv.T + bv).reshape(B, Nkv, H, D).transpose(0, 2, 1, 3)
        scale = D ** (-0.5)
        attn = jax.nn.softmax(jnp.einsum('bhqd,bhkd->bhqk', qh, kh) * scale, axis=-1)
        out = jnp.einsum('bhqk,bhkd->bhqd', attn, vh)
        out = out.transpose(0, 2, 1, 3).reshape(B, Nq, C)
        return out @ Wo.T + bo

    def _L0_ffn_ref(x, router_w, router_b, routed_w1, routed_w3, routed_w2, shared_w1, shared_w3, shared_w2):
        import jax, jax.numpy as jnp
        import numpy as np
        BEST_K = 2

        def _expert(xf, w1, w3, w2):
            return jax.nn.silu(xf @ w1) * (xf @ w3) @ w2
        B, S, D = x.shape
        T = B * S
        xf = x.reshape(T, D)
        logits = xf @ router_w + router_b
        topk_vals, topk_idx = jax.lax.top_k(logits, BEST_K)
        sparse = jnp.full_like(logits, -jnp.inf)
        sparse = sparse.at[jnp.arange(T)[:, None], topk_idx].set(topk_vals)
        gates = jax.nn.softmax(sparse, axis=-1)
        routed = jax.vmap(_expert, in_axes=(None, 0, 0, 0))(xf, routed_w1, routed_w3, routed_w2)
        routed_out = jnp.einsum('etd,te->td', routed, gates)
        shared_out = jax.vmap(_expert, in_axes=(None, 0, 0, 0))(xf, shared_w1, shared_w3, shared_w2).sum(axis=0)
        return (routed_out + shared_out).reshape(B, S, D)

    def _L1_xattn_ref(hidden_states, visual_hidden_state):
        import jax, jax.numpy as jnp
        import numpy as np
        fusion_scores = jnp.einsum('bsd,bvd->bsv', hidden_states, visual_hidden_state)
        fusion_probs = jax.nn.softmax(fusion_scores, axis=-1)
        fusion_output = jnp.einsum('bsv,bvd->bsd', fusion_probs, visual_hidden_state)
        return fusion_output

    def _L1_ffn_ref(x, w1, conv_w, conv_b, w2):
        import jax, jax.numpy as jnp
        import numpy as np
        B, S, D_MODEL, D_HIDDEN = (4, 1024, 512, 2048)

        def act_quant(x):
            scale = 127.0 / jnp.clip(jnp.max(jnp.abs(x), axis=-1, keepdims=True), 1e-05)
            return jnp.clip(jnp.round(x * scale), -128, 127) / scale

        def weight_quant(w):
            scale = 1.0 / jnp.clip(jnp.mean(jnp.abs(w)), 1e-05)
            return jnp.clip(jnp.round(w * scale), -1, 1) / scale

        def bit_linear(x, w):
            xq = x + jax.lax.stop_gradient(act_quant(x) - x)
            wq = w + jax.lax.stop_gradient(weight_quant(w) - w)
            return jnp.einsum('bsd,hd->bsh', xq, wq)

        def depthwise_conv1d(x_bcl, w, b):
            y = jax.lax.conv_general_dilated(x_bcl, w, window_strides=(1,), padding=[(1, 1)], dimension_numbers=('NCH', 'OIH', 'NCH'), feature_group_count=x_bcl.shape[1])
            return y + b[None, :, None]
        h = bit_linear(x, w1)
        h = depthwise_conv1d(h.transpose(0, 2, 1), conv_w, conv_b)
        h = h.transpose(0, 2, 1)
        h = jax.nn.silu(h)
        return bit_linear(h, w2)
    x = x + jnp.tanh(g_xattn[0]) * _L0_xattn_ref(_layernorm(x, axis=-1), ctx_1024, ctx_1024, L0_xattn_Wq, L0_xattn_bq, L0_xattn_Wk, L0_xattn_bk, L0_xattn_Wv, L0_xattn_bv, L0_xattn_Wo, L0_xattn_bo)
    x = x + jnp.tanh(g_ffn[0]) * _L0_ffn_ref(_layernorm(x, axis=-1), L0_ffn_router_w, L0_ffn_router_b, L0_ffn_routed_w1, L0_ffn_routed_w3, L0_ffn_routed_w2, L0_ffn_shared_w1, L0_ffn_shared_w3, L0_ffn_shared_w2)
    x = x + jnp.tanh(g_xattn[1]) * _L1_xattn_ref(_layernorm(x, axis=-1), ctx_1024)
    x = x + jnp.tanh(g_ffn[1]) * _L1_ffn_ref(_layernorm(x, axis=-1), L1_ffn_w1, L1_ffn_conv_w, L1_ffn_conv_b, L1_ffn_w2)
    return x

_drawn_inputs = setup_inputs


def setup_inputs(seed=0):
    import zlib

    import numpy as np

    out = dict(_drawn_inputs(seed))
    spreads = {'g_ffn': (-1.0, 0.6),
     'L0_xattn_bq': (0.0, 0.1),
     'L0_xattn_bk': (0.0, 0.8),
     'L0_xattn_bv': (0.0, 0.1),
     'L0_xattn_bo': (0.0, 0.1),
     'L0_ffn_router_b': (0.0, 0.49)}
    factors = {}
    for name, (base, spread) in spreads.items():
        noise = np.random.default_rng([zlib.crc32(name.encode()), seed]).standard_normal(out[name].shape)
        drawn = base * np.exp(spread * noise) if base else spread * noise
        out[name] = jnp.asarray(drawn.astype(out[name].dtype))
    for name, factor in factors.items():
        out[name] = (out[name] * factor).astype(out[name].dtype)
    return out
```

```python
from contextlib import ExitStack

import concourse.bass as bass
from concourse import mybir

F32 = mybir.dt.float32
FR = mybir.dt.float32r
BF16 = mybir.dt.bfloat16
I32 = mybir.dt.int32
U32 = mybir.dt.uint32
ALU = mybir.AluOpType
ACT = mybir.ActivationFunctionType
AX = mybir.AxisListType
ds = bass.ds

P = 128
MAGIC = 12582912.0
PASSES = ((0, 0), (0, 1), (1, 0))
EPS_LN = 1e-5
EPS_Q = 1e-5


class Program:
    pass


def flamingo(nc, x, ctx, ctxT, gates, wqT, wkT, wvT, woT, bq, bk, bv, bo, router_w, router_b,
             w13, w2e, w1T, conv_w, conv_b, w2T, out):
    B, C, D = ctx.shape
    T = x.shape[0]
    S = T // B
    KD = D // P
    NT = T // P
    TB = S // P
    HD = 32
    H = D // HD
    HG = P // HD
    NG = H // HG
    CP = C + C % 2
    E = router_w.shape[2]
    NE = w13.shape[0]
    NSH = NE - E
    HID = w13.shape[3] // 2
    KH = HID // P
    MIN_TILES = 3
    SHT = NSH * NT
    MAXT = 2 * NT + MIN_TILES * E
    DH = w1T.shape[2]
    KF = DH // P
    SCALE = float(HD) ** -0.5

    x1_d = nc.dram_tensor("x1_scratch", [T, D], F32)
    xn2_d = nc.dram_tensor("xn2_scratch", [T, D], F32)
    xs_d = nc.dram_tensor("slots_in_scratch", [MAXT * P, D], F32)
    ys_d = nc.dram_tensor("experts_out_scratch", [(SHT + MAXT) * P, D], F32)
    x3_d = nc.dram_tensor("x3_scratch", [T, D], F32)
    xd_d = nc.dram_tensor("xd_scratch", [T, D], F32)

    def tile_rows(t, first, n=1):
        if n == 1:
            return t[ds(first * P, P), :]
        return t[ds(first * P, n * P), :].rearrange("(n p) d -> p n d", p=P)

    with ExitStack() as top:
        def keep(name, shape, dt):
            return top.enter_context(nc.sbuf_tensor(name, shape, dt))

        ident = keep("ident", [P, P], F32)
        tg = keep("tanh_gates", [P, 4], F32)
        logits = keep("logits", [P, NT, E], F32)
        gate = keep("gate", [P, 2, NT], F32)
        slot = keep("slot", [P, 2, NT], U32)
        slot_y = keep("slot_y", [P, 2, NT], U32)

        passed_dve = top.enter_context(nc.semaphore("passed_dve"))
        passed_pool = top.enter_context(nc.semaphore("passed_pool"))

        n = Program()
        n.B = B
        n.C = C
        n.CP = CP
        n.D = D
        n.DH = DH
        n.E = E
        n.H = H
        n.HD = HD
        n.HG = HG
        n.HID = HID
        n.KD = KD
        n.KF = KF
        n.KH = KH
        n.MAXT = MAXT
        n.MIN_TILES = MIN_TILES
        n.NE = NE
        n.NG = NG
        n.NSH = NSH
        n.NT = NT
        n.S = S
        n.SCALE = SCALE
        n.SHT = SHT
        n.T = T
        n.TB = TB
        n.bk = bk
        n.bo = bo
        n.bq = bq
        n.bv = bv
        n.conv_b = conv_b
        n.conv_w = conv_w
        n.ctx = ctx
        n.ctxT = ctxT
        n.gate = gate
        n.gates = gates
        n.ident = ident
        n.logits = logits
        n.out = out
        n.passed_dve = passed_dve
        n.passed_pool = passed_pool
        n.router_b = router_b
        n.router_w = router_w
        n.slot = slot
        n.slot_y = slot_y
        n.tg = tg
        n.tile_rows = tile_rows
        n.w13 = w13
        n.w1T = w1T
        n.w2T = w2T
        n.w2e = w2e
        n.wkT = wkT
        n.woT = woT
        n.wqT = wqT
        n.wvT = wvT
        n.x = x
        n.x1_d = x1_d
        n.x3_d = x3_d
        n.xd_d = xd_d
        n.xn2_d = xn2_d
        n.xs_d = xs_d
        n.ys_d = ys_d

        attention(nc, n)
        experts(nc, n)
        fuse(nc, n)
        ffn(nc, n)


def hold(eng, sem, value, passed):
    eng.wait_ge(sem, value)
    eng.sem_inc(passed, 1)


def attention(nc, n):
    B, C, D, S, KD, NT, TB, HD, H, HG, NG, E = n.B, n.C, n.D, n.S, n.KD, n.NT, n.TB, n.HD, n.H, n.HG, n.NG, n.E
    ident, tg, logits = n.ident, n.tg, n.logits
    W2 = 2 * P
    NSTEP = n.T // W2
    GC = HG * C

    with ExitStack() as ctx:
        def sb(name, shape, dt, c=ctx):
            return c.enter_context(nc.sbuf_tensor(name, shape, dt))

        def sem(name, c=ctx):
            return c.enter_context(nc.semaphore(name))

        wq = sb("wq", [P, 2, KD, D], FR)
        wo = sb("wo", [P, 2, KD, D], FR)
        kc = sb("k_all", [P, B, NG, C], F32)
        vc = sb("v_all", [C, B, D], F32)
        kbd = sb("k_blocks", [P, 2, NG, GC], FR)
        vbd = sb("v_blocks", [C, 2, H, P], FR)
        bq_s = sb("bq_s", [P, NG], F32)
        bo_t = sb("bo_t", [P, D], F32)
        rw = sb("rw", [P, 2, KD, E], FR)
        rb = sb("rb", [P, E], F32)
        half = sb("minus_half", [P, 2], F32)
        eps = sb("eps", [P, 2], F32)

        with ExitStack() as c1:
            wraw = sb("wraw", [P, 4, KD, D], F32, c1)
            wkv = sb("wkv", [P, 2, 2, KD, D], FR, c1)
            craw = sb("craw", [P, KD, B * C], F32, c1)
            cts = sb("cts", [P, 2, KD, B * C], FR, c1)
            rraw = sb("rraw", [P, KD, E], F32, c1)
            bk_s = sb("bk_s", [P, NG], F32, c1)
            bv_s = sb("bv_s", [C, D], F32, c1)
            bo_s = sb("bo_s", [P, D], F32, c1)
            graw = sb("graw", [P, 4], F32, c1)
            kv_ps = [c1.enter_context(nc.psum_tensor(f"kv_ps{i}", [P, 512], F32)) for i in range(4)]
            ctx_in = sem("ctx_in", c1)
            small_in = sem("small_in", c1)
            w_in = [sem(f"w_in{i}", c1) for i in range(4)]
            hi_done = sem("hi_done", c1)
            lo_done = sem("lo_done", c1)
            cleared = sem("cleared", c1)
            id_done = sem("id_done", c1)
            tanh_done = sem("tanh_done", c1)
            kv_full = sem("kv_full", c1)
            kv_free = sem("kv_free", c1)
            block = c1.enter_context(nc.Block())
            srcs = [craw[:], wraw[:, 0], wraw[:, 1], wraw[:, 2], wraw[:, 3], rraw[:]]
            his = [cts[:, 0], wkv[:, 0, 0], wkv[:, 1, 0], wq[:, 0], wo[:, 0], rw[:, 0]]
            los = [cts[:, 1], wkv[:, 0, 1], wkv[:, 1, 1], wq[:, 1], wo[:, 1], rw[:, 1]]
            loaded = [(ctx_in, 16), (w_in[0], 16), (w_in[1], 16), (w_in[2], 16), (w_in[3], 16), (small_in, 112)]

            @block.sync
            def _(sp):
                sp.dma_start(craw[:], n.ctxT).then_inc(ctx_in, 16)
                for i, w in enumerate((n.wkT, n.wvT, n.wqT, n.woT)):
                    sp.dma_start(wraw[:, i], w).then_inc(w_in[i], 16)
                sp.dma_start(bq_s[:], n.bq).then_inc(small_in, 16)
                sp.dma_start(bk_s[:], n.bk).then_inc(small_in, 16)
                sp.dma_start(bv_s[:], n.bv.partition_broadcast(C)).then_inc(small_in, 16)
                sp.dma_start(bo_s[:], n.bo.partition_broadcast(P)).then_inc(small_in, 16)
                sp.dma_start(rb[:], n.router_b.partition_broadcast(P)).then_inc(small_in, 16)
                sp.dma_start(graw[:], n.gates.partition_broadcast(P)).then_inc(small_in, 16)
                sp.dma_start(rraw[:], n.router_w).then_inc(small_in, 16)

            @block.gpsimd
            def _(pool):
                pool.memset(half[:], -0.5)
                pool.memset(eps[:], EPS_LN)
                pool.memset(kbd[:].bitcast(F32), 0.0)
                pool.memset(vbd[:].bitcast(F32), 0.0)
                pool.memset(ident[:], 0.0).then_inc(cleared, 1)
                pool.wait_ge(cleared, 1)
                pool.affine_select(out=ident[:], in_=ident[:], compare_op=ALU.not_equal, fill=1.0, base=0,
                                   pattern=[[-1, P]], channel_multiplier=1).then_inc(id_done, 1)

            @block.scalar
            def _(act):
                for s, h, (q, v) in zip(srcs, his, loaded):
                    act.wait_ge(q, v)
                    act.activation(h, s, ACT.Copy).then_inc(hi_done, 1)
                act.activation(tg[:], graw[:], ACT.Tanh).then_inc(tanh_done, 1)

            @block.vector
            def _(dve):
                def lo(i):
                    dve.wait_ge(hi_done, i + 1)
                    dve.wait_ge(loaded[i][0], loaded[i][1])
                    dve.tensor_tensor(los[i], srcs[i], his[i].bitcast(F32), ALU.subtract).then_inc(lo_done, 1)

                for i in range(3):
                    lo(i)
                dve.wait_ge(small_in, 112)
                use = 0
                for half_b in range(2):
                    for m in range(NG):
                        dve.wait_ge(kv_full, use + 1)
                        bs = slice(half_b * B // 2, (half_b + 1) * B // 2)
                        dve.tensor_scalar(kc[:, bs, m, :],
                                          kv_ps[use % 4][:, 0:B // 2 * C].rearrange("p (b c) -> p b c", c=C),
                                          bk_s[:, m:m + 1], None, ALU.add).then_inc(kv_free, 1)
                        use += 1
                for b in range(B):
                    dve.wait_ge(kv_full, use + 1)
                    dve.tensor_tensor(vc[:, b], kv_ps[use % 4][0:C, :], bv_s[:], ALU.add).then_inc(kv_free, 1)
                    use += 1
                for i in range(3, 6):
                    lo(i)
                dve.wait_ge(tanh_done, 1)
                dve.tensor_scalar(bo_t[:], bo_s[:], tg[:, 0:1], None, ALU.mult)

            @block.tensor
            def _(pe):
                use = 0
                pe.wait_ge(lo_done, 2)
                N = B // 2 * C
                for half_b in range(2):
                    for m in range(NG):
                        if use >= 4:
                            pe.wait_ge(kv_free, use - 3)
                        for k in range(KD):
                            for pa, pb in PASSES:
                                mm = pe.matmul(kv_ps[use % 4][:, 0:N], wkv[:, 0, pa, k, m * P:(m + 1) * P],
                                               cts[:, pb, k, half_b * N:(half_b + 1) * N],
                                               start=(k == 0 and (pa, pb) == PASSES[0]),
                                               stop=(k == KD - 1 and (pa, pb) == PASSES[-1]))
                        mm.then_inc(kv_full, 1)
                        use += 1
                pe.wait_ge(lo_done, 3)
                for bb in range(B):
                    pe.wait_ge(kv_free, use - 3)
                    for k in range(KD):
                        for pa, pb in PASSES:
                            mm = pe.matmul(kv_ps[use % 4][0:C, :], cts[:, pa, k, bb * C:(bb + 1) * C],
                                           wkv[:, 1, pb, k, :],
                                           start=(k == 0 and (pa, pb) == PASSES[0]),
                                           stop=(k == KD - 1 and (pa, pb) == PASSES[-1]))
                    mm.then_inc(kv_full, 1)
                    use += 1

        xin = sb("xin", [P, 2, D], F32)
        xn = sb("xn", [P, 2, D], F32)
        xT = sb("xT", [P, 2, KD, W2], FR)
        qT = sb("qT", [P, 2, 2, NG, W2], FR)
        prob = sb("prob", [P, 2, H, C], F32)
        pT = sb("pT", [C, 2, H, W2], FR)
        oT = sb("oT", [P, 2, NG, W2], FR)
        xres = sb("xres", [P, 2, D], F32)
        x1 = sb("x1", [P, 2, D], F32)
        xn2 = sb("xn2", [P, 2, D], F32)
        x2T = sb("x2T", [P, 2, KD, W2], FR)
        st1 = sb("st1", [P, 2, 6], F32)
        mv1 = sb("mv1", [P, 2, 2], F32)
        ve1 = sb("ve1", [P, 2], F32)
        rs1 = sb("rs1", [P, 2], F32)
        st2 = sb("st2", [P, 2, 6], F32)
        mv2 = sb("mv2", [P, 2, 2], F32)
        ve2 = sb("ve2", [P, 2], F32)
        rs2 = sb("rs2", [P, 2], F32)
        mx = sb("mx", [P, 2, H], F32)
        sm = sb("sm", [P, 2, H], F32)
        ri = sb("ri", [P, 2, H], F32)
        s_ps = ctx.enter_context(nc.psum_tensor("s_ps", [P, NG, 512], F32))
        t_ps = ctx.enter_context(nc.psum_tensor("t_ps", [P, 2, 512], F32))
        m_ps = ctx.enter_context(nc.psum_tensor("m_ps", [P, 2, 512], F32))

        x_in = sem("x_in")
        xres_in = sem("xres_in")
        mv1_done = sem("mv1_done")
        mv2_done = sem("mv2_done")
        st_done = sem("st_done")
        rs_tmp = sem("rs_tmp")
        rs1_done = sem("rs1_done")
        rs2_done = sem("rs2_done")
        xn_done = sem("xn_done")
        xb_done = sem("xb_done")
        t_full = sem("t_full")
        t_hi = sem("t_hi")
        t_free = sem("t_free")
        m_full = sem("m_full")
        m_hi = sem("m_hi")
        m_free = sem("m_free")
        s_full = sem("s_full")
        s_sub = sem("s_sub")
        mx_done = sem("mx_done")
        e_done = sem("e_done")
        sum_done = sem("sum_done")
        ri_done = sem("ri_done")
        p_done = sem("p_done")
        bd_hi = sem("bd_hi")
        k_bd = sem("k_bd")
        v_bd = sem("v_bd")
        xn2_done = sem("xn2_done")
        x1_out = sem("x1_out")
        xn2_out = sem("xn2_out")


        def whole(eng, run):
            run(-1, -1, False, False, True)
            run(0, 0, True, False, True)
            run(1, 0, True, True, True)
            if B > 2:
                with eng.Fori(1, B - 1) as b:
                    run(b * 2, b, True, True, True, 0)
                    run(b * 2 + 1, b, True, True, True, 1)
            run(NSTEP - 2, B - 1, True, True, True)
            run(NSTEP - 1, B - 1, True, True, False)
            run(NSTEP, B, False, True, False)

        def before(s, first, front, back):
            if isinstance(s, int):
                return max(0, min(s + 1, NSTEP)) * front + max(0, s) * first + max(0, s - 1) * back
            return s * (front + first + back) + (front - back)

        def t_base(s):
            return before(s, 2 * NG, 2, 2)

        def m_base(s):
            return before(s, 0, 2, 6)

        def plan(mid, back, front):
            t = (["x0", "x1"] if front else []) + ([("p", 0, g) for g in range(NG)] if mid else []) \
                + (["n0", "n1"] if back else []) + ([("p", 1, g) for g in range(NG)] if mid else [])
            m = (["o0", "o1", "w0", "w1"] if back else []) + (["q0", "q1"] if front else []) \
                + (["r0", "r1"] if back else [])
            return {u: i for i, u in enumerate(t)}, {u: i for i, u in enumerate(m)}

        def kc_heads(q, b):
            return kc[q, ds(b, 1), :, :].rearrange("p o g c -> p (o g) c")

        def vbd_heads(part, i):
            return vbd[:, part].rearrange("c (g i) p -> c g i p", i=HG)[:, :, i, i * HD:(i + 1) * HD]

        def vc_heads(b, i):
            return vc[:, ds(b, 1), :].rearrange("c o (g i d) -> c (o g) i d", i=HG, d=HD)[:, :, i, :]

        assert NG == 4 and B >= 2
        block = ctx.enter_context(nc.Block())

        @block.sync
        def _(sp):
            def run(s, b, mid, back, front, par=None):
                par = s % 2 if par is None else par
                if front:
                    if not (isinstance(s, int) and s < 0):
                        sp.wait_ge(xn_done, (s + 1) * 2)
                    sp.dma_start(xin[:], tile_rows2(n.x, s + 1)).then_inc(x_in, 16)
                if back:
                    sp.dma_start(xres[:], tile_rows2(n.x, s - 1)).then_inc(xres_in, 16)
                    for j in range(2):
                        sp.wait_ge(m_free, m_base(s) + plan(mid, back, front)[1][f"w{j}"] + 1)
                        sp.dma_start(n.tile_rows(n.x1_d, (s - 1) * 2 + j), x1[:, j]).then_inc(x1_out, 16)
                    for j in range(2):
                        sp.wait_ge(xn2_done, (s - 1) * 2 + j + 1)
                        sp.dma_start(n.tile_rows(n.xn2_d, (s - 1) * 2 + j), xn2[:, j]).then_inc(xn2_out, 16)

            def tile_rows2(t, s):
                return n.tile_rows(t, s * 2, 2)

            whole(sp, run)
            sp.wait_ge(x1_out, 16 * NT)
            sp.wait_ge(xn2_out, 16 * NT)

        @block.gpsimd
        def _(pool):
            def rstd(mv_sem, count, mv, ve, rs, out_sem, tmp_count):
                pool.wait_ge(mv_sem, count)
                pool.tensor_tensor(ve[:], mv[:, :, 1], eps[:], ALU.add).then_inc(rs_tmp, 1)
                pool.wait_ge(rs_tmp, tmp_count)
                pool.tensor_tensor(rs[:], ve[:], half[:], ALU.pow).then_inc(out_sem, 1)

            def run(s, b, mid, back, front, par=None):
                par = s % 2 if par is None else par
                tmp = before(s, 0, 1, 1)
                if front:
                    rstd(mv1_done, s * 2 + 4, mv1, ve1, rs1, rs1_done, tmp + 1)
                if back:
                    pool.wait_ge(xres_in, s * 16)
                    for j in range(2):
                        pool.tensor_tensor(xres[:, j], xres[:, j], bo_t[:], ALU.add).then_inc(xb_done, 1)
                if mid:
                    normalise(s, 0)
                if back:
                    rstd(mv2_done, s * 2, mv2, ve2, rs2, rs2_done, tmp + (2 if front else 1))
                if mid:
                    normalise(s, 1)

            def normalise(s, j):
                pool.wait_ge(ri_done, s * 2 + j + 1)
                pool.tensor_tensor(prob[:, j], prob[:, j], ri[:, j].unsqueeze(2).to_broadcast([P, H, C]),
                                   ALU.mult).then_inc(p_done, 1)

            whole(pool, run)

        @block.scalar
        def _(act):
            def hi(full, count, done, dst, src):
                act.wait_ge(full, count)
                act.activation(dst, src, ACT.Copy).then_inc(done, 1)

            def run(s, b, mid, back, front, par=None):
                par = s % 2 if par is None else par
                tb, mb = t_base(s), m_base(s)
                t, m = plan(mid, back, front)

                def tcopy(u, dst, parts=P):
                    i = t[u]
                    act.wait_ge(t_full, tb + i + 1)
                    act.activation(dst, t_ps[0:parts, i % 2].rearrange("p (a b) -> p a b", b=P), ACT.Copy).then_inc(t_hi, 1)

                def exps(j):
                    for pair in range(2):
                        act.wait_ge(s_sub, s * 4 + 2 * j + pair + 1)
                        g = slice(pair * H // 2, (pair + 1) * H // 2)
                        act.activation(prob[:, j, g], prob[:, j, g], ACT.Exp, scale=n.SCALE).then_inc(e_done, 1)

                if mid and par == 0:
                    if not (isinstance(s, int) and s == 0):
                        act.wait_ge(s_full, s * 4)
                    for i in range(HG):
                        q = slice(i * HD, (i + 1) * HD)
                        act.activation(kbd[q, 0, :, i * C:(i + 1) * C], kc_heads(q, b),
                                       ACT.Copy).then_inc(bd_hi, 1)
                if mid:
                    exps(0)
                if back:
                    for i, u in enumerate(("o0", "o1")):
                        act.wait_ge(m_full, mb + m[u] + 1)
                        act.activation(oT[:, 0, 2 * i:2 * i + 2], m_ps[:, m[u] % 2].rearrange("p (a b) -> p a b", b=W2),
                                       ACT.Copy).then_inc(m_hi, 1)
                if mid and par == 0:
                    for i in range(HG):
                        act.activation(vbd_heads(0, i), vc_heads(b, i), ACT.Copy).then_inc(bd_hi, 1)
                if front:
                    for j in range(2):
                        tcopy(f"x{j}", xT[:, 0, :, j * P:(j + 1) * P])
                if mid:
                    exps(1)
                    for g in range(NG):
                        tcopy(("p", 0, g), pT[:, 0, g * HG:(g + 1) * HG, 0:P], C)
                if front:
                    for i in range(2):
                        u = f"q{i}"
                        act.wait_ge(m_full, mb + m[u] + 1)
                        for g in range(2):
                            act.activation(qT[:, 1 - par, 0, 2 * i + g], m_ps[:, m[u] % 2, g * W2:(g + 1) * W2],
                                           ACT.Identity, bias=bq_s[:, 2 * i + g:2 * i + g + 1]).then_inc(m_hi, 1)
                if back:
                    for j in range(2):
                        tcopy(f"n{j}", x2T[:, 0, :, j * P:(j + 1) * P])
                if mid:
                    for g in range(NG):
                        tcopy(("p", 1, g), pT[:, 0, g * HG:(g + 1) * HG, P:W2], C)

            whole(act, run)

        @block.vector
        def _(dve):
            def run(s, b, mid, back, front, par=None):
                par = s % 2 if par is None else par
                tb, mb = t_base(s), m_base(s)
                t, m = plan(mid, back, front)
                hb = before(s, 0, 4, 2)
                sb0 = before(s, 0, 2, 2)

                def tlow(u, dst, hi_ap, parts=P):
                    i = t[u]
                    dve.wait_ge(t_hi, tb + i + 1)
                    dve.tensor_tensor(dst, t_ps[0:parts, i % 2].rearrange("p (a b) -> p a b", b=P),
                                      hi_ap.bitcast(F32), ALU.subtract).then_inc(t_free, 1)

                def softmax_in(j):
                    for pair in range(2):
                        dve.wait_ge(s_full, s * 4 + 2 * j + pair + 1)
                        hs = slice(pair * H // 2, (pair + 1) * H // 2)
                        sc = s_ps[:, 2 * pair:2 * pair + 2, 0:GC].rearrange("p g (i c) -> p g i c", c=C)
                        mxp = mx[:, j, hs].rearrange("p (g i) -> p g i", i=HG)
                        dve.tensor_reduce(mxp, sc, AX.X, ALU.max).then_inc(mx_done, 1)
                        dve.wait_ge(mx_done, s * 4 + 2 * j + pair + 1)
                        dve.tensor_tensor(prob[:, j, hs].rearrange("p (g i) c -> p g i c", i=HG), sc,
                                          mxp.unsqueeze(3).to_broadcast([P, 2, HG, C]), ALU.subtract).then_inc(s_sub, 1)

                def softmax_sum(j):
                    dve.wait_ge(e_done, s * 4 + 2 * j + 2)
                    dve.tensor_reduce(sm[:, j], prob[:, j], AX.X, ALU.add).then_inc(sum_done, 1)
                    dve.wait_ge(sum_done, s * 2 + j + 1)
                    dve.reciprocal(ri[:, j], sm[:, j]).then_inc(ri_done, 1)

                def norm_stats(src_of, st, mv, done, base):
                    for j in range(2):
                        dve.bn_stats(st[:, j], src_of(j)).then_inc(st_done, 1)
                    for j in range(2):
                        hold(dve, st_done, base + j + 1, n.passed_dve)
                        dve.bn_aggr(mv[:, j], st[:, j]).then_inc(done, 1)

                if front:
                    dve.wait_ge(x_in, s * 16 + 32)
                    norm_stats(lambda j: xin[:, j], st1, mv1, mv1_done, sb0)
                if mid and par == 0:
                    for i in range(HG):
                        q = slice(i * HD, (i + 1) * HD)
                        dve.wait_ge(bd_hi, b * 2 * HG + i + 1)
                        hi = kbd[q, 0, :, i * C:(i + 1) * C].bitcast(F32)
                        dve.tensor_tensor(kbd[q, 1, :, i * C:(i + 1) * C],
                                          kc_heads(q, b), hi,
                                          ALU.subtract).then_inc(k_bd, 1)
                if mid:
                    softmax_in(0)
                if front:
                    dve.wait_ge(rs1_done, s + 2)
                    for j in range(2):
                        dve.tensor_scalar(xn[:, j], xin[:, j], mv1[:, j, 0:1], rs1[:, j:j + 1], ALU.subtract,
                                          ALU.mult).then_inc(xn_done, 1)
                if back:
                    for i, u in enumerate(("o0", "o1")):
                        dve.wait_ge(m_hi, hb + i + 1)
                        dve.tensor_tensor(oT[:, 1, 2 * i:2 * i + 2], m_ps[:, m[u] % 2].rearrange("p (a b) -> p a b", b=W2),
                                          oT[:, 0, 2 * i:2 * i + 2].bitcast(F32), ALU.subtract).then_inc(m_free, 1)
                if mid and par == 0:
                    for i in range(HG):
                        dve.wait_ge(bd_hi, b * 2 * HG + HG + i + 1)
                        dve.tensor_tensor(vbd_heads(1, i), vc_heads(b, i), vbd_heads(0, i).bitcast(F32),
                                          ALU.subtract).then_inc(v_bd, 1)
                if mid:
                    softmax_in(1)
                    softmax_sum(0)
                if front:
                    for j in range(2):
                        tlow(f"x{j}", xT[:, 1, :, j * P:(j + 1) * P], xT[:, 0, :, j * P:(j + 1) * P])
                if back:
                    dve.wait_ge(xb_done, s * 2)
                    if not (isinstance(s, int) and s <= 1):
                        dve.wait_ge(x1_out, (s - 1) * 32)
                    for j in range(2):
                        u = f"w{j}"
                        dve.wait_ge(m_full, mb + m[u] + 1)
                        dve.scalar_tensor_tensor(out=x1[:, j], in0=m_ps[:, m[u] % 2], scalar=tg[:, 0:1], in1=xres[:, j],
                                                 op0=ALU.mult, op1=ALU.add).then_inc(m_free, 1)
                    dve.wait_ge(m_free, mb + m["w1"] + 1)
                    norm_stats(lambda j: x1[:, j], st2, mv2, mv2_done, sb0 + (2 if front else 0))
                if mid:
                    softmax_sum(1)
                    for g in range(NG):
                        hs = slice(g * HG, (g + 1) * HG)
                        tlow(("p", 0, g), pT[:, 1, hs, 0:P], pT[:, 0, hs, 0:P], C)
                if back:
                    dve.wait_ge(rs2_done, s)
                    if not (isinstance(s, int) and s <= 1):
                        dve.wait_ge(xn2_out, (s - 1) * 32)
                    for j in range(2):
                        dve.tensor_scalar(xn2[:, j], x1[:, j], mv2[:, j, 0:1], rs2[:, j:j + 1], ALU.subtract,
                                          ALU.mult).then_inc(xn2_done, 1)
                if front:
                    for i in range(2):
                        u = f"q{i}"
                        for g in range(2):
                            dve.wait_ge(m_hi, hb + (2 if back else 0) + 2 * i + 2)
                            ins = dve.scalar_tensor_tensor(
                                out=qT[:, 1 - par, 1, 2 * i + g], in0=m_ps[:, m[u] % 2, g * W2:(g + 1) * W2],
                                scalar=bq_s[:, 2 * i + g:2 * i + g + 1], in1=qT[:, 1 - par, 0, 2 * i + g].bitcast(F32),
                                op0=ALU.add, op1=ALU.subtract)
                        ins.then_inc(m_free, 1)
                if back:
                    for j in range(2):
                        tlow(f"n{j}", x2T[:, 1, :, j * P:(j + 1) * P], x2T[:, 0, :, j * P:(j + 1) * P])
                    for j in range(2):
                        u = f"r{j}"
                        dve.wait_ge(m_full, mb + m[u] + 1)
                        dve.tensor_tensor(logits[:, ds((s - 1) * 2 + j, 1), :].rearrange("p o e -> p (o e)"),
                                          m_ps[:, m[u] % 2, 0:E], rb[:], ALU.add).then_inc(m_free, 1)
                if mid:
                    for g in range(NG):
                        hs = slice(g * HG, (g + 1) * HG)
                        tlow(("p", 1, g), pT[:, 1, hs, P:W2], pT[:, 0, hs, P:W2], C)

            whole(dve, run)

        @block.tensor
        def _(pe):
            def run(s, b, mid, back, front, par=None):
                par = s % 2 if par is None else par
                tb, mb = t_base(s), m_base(s)
                t, m = plan(mid, back, front)

                def t_room(u):
                    if not (isinstance(s, int) and tb + t[u] < 2):
                        pe.wait_ge(t_free, tb + t[u] - 1)

                def m_room(u):
                    if not (isinstance(s, int) and mb + m[u] < 2):
                        pe.wait_ge(m_free, mb + m[u] - 1)

                def scores(j):
                    for g in range(NG):
                        if g % 2 == 0 and not (isinstance(s, int) and s * 4 + 2 * j + g // 2 < 2):
                            pe.wait_ge(s_sub, s * 4 + 2 * j + g // 2 - 1)
                        for pa, pb in PASSES:
                            mm = pe.matmul(s_ps[:, g, 0:GC], qT[:, par, pa, g, j * P:(j + 1) * P], kbd[:, pb, g, :],
                                           start=((pa, pb) == PASSES[0]), stop=((pa, pb) == PASSES[-1]))
                        if g % 2:
                            mm.then_inc(s_full, 1)

                def prob_transposes(j):
                    pe.wait_ge(p_done, s * 2 + j + 1)
                    for g in range(NG):
                        t_room(("p", j, g))
                        for i in range(HG):
                            mm = pe.transpose(t_ps[0:C, t[("p", j, g)] % 2, i * P:(i + 1) * P], prob[:, j, g * HG + i, :],
                                              ident[:])
                        mm.then_inc(t_full, 1)

                if mid:
                    if par == 0:
                        pe.wait_ge(k_bd, b * HG + HG)
                    pe.wait_ge(m_free, mb)
                    scores(0)
                if back:
                    pe.wait_ge(t_free, tb)
                    pe.wait_ge(v_bd, (b - 1 if par == 0 else b) * HG + HG)
                    for i in range(2):
                        m_room(f"o{i}")
                        for g in range(2):
                            for h in range(HG):
                                hh = (2 * i + g) * HG + h
                                for pa, pb in PASSES:
                                    mm = pe.matmul(m_ps[:, m[f"o{i}"] % 2, g * W2:(g + 1) * W2], vbd[:, pa, hh, :],
                                                   pT[:, pb, hh, :], start=(h == 0 and (pa, pb) == PASSES[0]),
                                                   stop=(h == HG - 1 and (pa, pb) == PASSES[-1]))
                        mm.then_inc(m_full, 1)
                if mid:
                    scores(1)
                if front:
                    pe.wait_ge(xn_done, s * 2 + 4)
                    for j in range(2):
                        t_room(f"x{j}")
                        for k in range(KD):
                            mm = pe.transpose(t_ps[:, t[f"x{j}"] % 2, k * P:(k + 1) * P], xn[:, j, k * P:(k + 1) * P],
                                              ident[:])
                        mm.then_inc(t_full, 1)
                if back:
                    pe.wait_ge(m_free, mb + m["o1"] + 1)
                    for j in range(2):
                        m_room(f"w{j}")
                        for k in range(KD):
                            for pa, pb in PASSES:
                                mm = pe.matmul(m_ps[:, m[f"w{j}"] % 2], oT[:, pa, k, j * P:(j + 1) * P], wo[:, pb, k, :],
                                               start=(k == 0 and (pa, pb) == PASSES[0]),
                                               stop=(k == KD - 1 and (pa, pb) == PASSES[-1]))
                        mm.then_inc(m_full, 1)
                if mid:
                    prob_transposes(0)
                if front:
                    pe.wait_ge(t_free, tb + t["x1"] + 1)
                    for i in range(2):
                        m_room(f"q{i}")
                        for g in range(2):
                            mt = 2 * i + g
                            for k in range(KD):
                                for pa, pb in PASSES:
                                    mm = pe.matmul(m_ps[:, m[f"q{i}"] % 2, g * W2:(g + 1) * W2],
                                                   wq[:, pa, k, mt * P:(mt + 1) * P], xT[:, pb, k, :],
                                                   start=(k == 0 and (pa, pb) == PASSES[0]),
                                                   stop=(k == KD - 1 and (pa, pb) == PASSES[-1]))
                        mm.then_inc(m_full, 1)
                if back:
                    pe.wait_ge(xn2_done, s * 2)
                    for j in range(2):
                        t_room(f"n{j}")
                        for k in range(KD):
                            mm = pe.transpose(t_ps[:, t[f"n{j}"] % 2, k * P:(k + 1) * P], xn2[:, j, k * P:(k + 1) * P],
                                              ident[:])
                        mm.then_inc(t_full, 1)
                    pe.wait_ge(t_free, tb + t["n1"] + 1)
                    for j in range(2):
                        m_room(f"r{j}")
                        for k in range(KD):
                            for pa, pb in PASSES:
                                mm = pe.matmul(m_ps[:, m[f"r{j}"] % 2, 0:E], x2T[:, pa, k, j * P:(j + 1) * P], rw[:, pb, k, :],
                                               start=(k == 0 and (pa, pb) == PASSES[0]),
                                               stop=(k == KD - 1 and (pa, pb) == PASSES[-1]))
                        mm.then_inc(m_full, 1)
                if mid:
                    prob_transposes(1)

            whole(pe, run)


def experts(nc, n):
    NT, E, KD, D, KH, HID, NSH, NE = n.NT, n.E, n.KD, n.D, n.KH, n.HID, n.NSH, n.NE
    MT, SHT, MAXT = n.MIN_TILES, n.SHT, n.MAXT
    ident, logits, gate, slot, slot_y = n.ident, n.logits, n.gate, n.slot, n.slot_y
    WN = KD * 2 * HID + KH * D
    W1N = KD * 2 * HID

    with ExitStack() as ctx:
        def sb(name, shape, dt):
            return ctx.enter_context(nc.sbuf_tensor("e_" + name, shape, dt))

        def sem(name):
            return ctx.enter_context(nc.semaphore("e_" + name))

        def psum(name, shape, dt=F32):
            return ctx.enter_context(nc.psum_tensor("e_" + name, shape, dt))

        top8 = sb("top8", [P, NT, 8], F32)
        idx8 = sb("idx8", [P, NT, 8], U32)
        idx = sb("idx", [P, 2, NT], F32)
        iota_e = sb("iota_e", [P, E], F32)
        iota_t = sb("iota_t", [P, NT], F32)
        hot = sb("hot", [P, 2, NT, E], F32)
        chosen = sb("chosen", [P, NT, E], BF16)
        before = sb("before", [P, P], BF16)
        ones = sb("ones", [P, P], BF16)
        onesf = sb("onesf", [P, NT], F32)
        tot = sb("tot", [P, E, NT], F32)
        cum = sb("cum", [P, E, NT], F32)
        big = sb("big", [P, E, NT], F32)
        tiles = sb("tiles", [P, E], F32)
        tcum = sb("tcum", [P, E], F32)
        first = sb("first", [P, E + 1], F32)
        least = sb("least", [P, E + 1], F32)
        bounds = sb("bounds", [P, E + 1], I32)
        base = sb("base", [P, E, NT], F32)
        pos = sb("pos", [P, NT, E], F32)
        sel = sb("sel", [P, 2, NT, E], F32)
        posf = sb("posf", [P, 2, NT], F32)
        dif = sb("dif", [P, NT], F32)
        ex = sb("ex", [P, NT], F32)
        den = sb("den", [P, NT], F32)
        zero = sb("zero", [P, MT, D], F32)
        srow = sb("srow", [P, 2, D], F32)
        scol = sb("scol", [P, 2, 2], U32)
        wraw = sb("wraw", [P, WN], F32)
        w = sb("w", [P, 2, 2, WN], FR)
        xe = sb("xe", [P, D], F32)
        xeT = sb("xeT", [P, 2, KD, P], FR)
        sg = sb("sg", [P, HID], F32)
        hh = sb("hh", [P, HID], F32)
        hT = sb("hT", [P, 2, KH, P], FR)
        ye = sb("ye", [P, D], F32)
        r_ps = psum("r_ps", [P, 2, NT * E])
        x_ps = psum("x_ps", [P, KD, P])
        u_ps = psum("u_ps", [P, 2 * HID])
        h_ps = psum("h_ps", [P, KH, P])
        y_ps = psum("y_ps", [P, D])

        zero_set = sem("zero_set")
        consts = sem("consts")
        masks = sem("masks")
        route = sem("route")
        chosen_done = sem("chosen_done")
        counted = sem("counted")
        bounds_done = sem("bounds_done")
        dif_done = sem("dif_done")
        ex_done = sem("ex_done")
        slot_done = sem("slot_done")
        zeroed = sem("zeroed")
        srow_in = [sem("srow_in0"), sem("srow_in1")]
        scol_done = sem("scol_done")
        scattered = [sem("scattered0"), sem("scattered1")]
        w_in = sem("w_in")
        w_hi = sem("w_hi")
        w_ready = sem("w_ready")
        xe_in = sem("xe_in")
        x_full = sem("x_full")
        x_hi = sem("x_hi")
        x_lo = sem("x_lo")
        u_full = sem("u_full")
        sg_done = sem("sg_done")
        hh_done = sem("hh_done")
        h_full = sem("h_full")
        h_hi = sem("h_hi")
        h_lo = sem("h_lo")
        y_full = sem("y_full")
        y_copied = sem("y_copied")
        y_out = sem("y_out")

        def bound(eng, e):
            return eng.value_load(bounds[0:1, e:e + 1], min_val=0, max_val=MAXT - MT * E) + (SHT + MT * e)

        block = ctx.enter_context(nc.Block())

        @block.sync
        def _(sp):
            def load(src, g, row_tile, first_load=False):
                if not first_load:
                    sp.wait_ge(x_full, g)
                sp.dma_start(xe[:], n.tile_rows(src, row_tile)).then_inc(xe_in, 16)

            load(n.xn2_d, 0, 0, True)
            with sp.Fori(1, NT) as g:
                load(n.xn2_d, g, g)
            for i in range(1, NSH):
                with sp.Fori(i * NT, (i + 1) * NT) as g:
                    load(n.xn2_d, g, g - i * NT)
            sp.wait_ge(bounds_done, 1)
            for par in range(2):
                sp.wait_ge(scattered[par], NT // 2 * 32)
            end = bound(sp, E)
            with sp.Fori(SHT, end) as g:
                load(n.xs_d, g, g - SHT)

        @block.gpsimd
        def _(pool):
            def fetch(e):
                pool.dma_start(wraw[:, 0:W1N].rearrange("p (k f) -> p k f", k=KD), n.w13[ds(e, 1)].rearrange("o p k f -> p (o k) f")).then_inc(w_in, 16)
                pool.dma_start(wraw[:, W1N:WN].rearrange("p (k f) -> p k f", k=KH), n.w2e[ds(e, 1)].rearrange("o p k f -> p (o k) f")).then_inc(w_in, 16)

            def split(e, par):
                pool.wait_ge(w_in, e * 32 + 32)
                pool.tensor_copy(w[:, par, 0], wraw[:]).then_inc(w_hi, 1)
                pool.wait_ge(w_hi, e + 1)
                pool.tensor_tensor(w[:, par, 1], wraw[:], w[:, par, 0].bitcast(F32), ALU.subtract).then_inc(w_ready, 1)
                pool.wait_ge(w_ready, e + 1)

            fetch(0)
            pool.memset(zero[:], 0.0).then_inc(zero_set, 1)
            pool.memset(onesf[:], 1.0)
            pool.memset(ones[:], 1.0)
            pool.iota(iota_e[:], pattern=[[1, E]], base=0, channel_multiplier=0, allow_small_or_imprecise_dtypes=True)
            pool.iota(least[:], pattern=[[MT, E + 1]], base=0, channel_multiplier=0, allow_small_or_imprecise_dtypes=True)
            pool.iota(iota_t[:], pattern=[[P, NT]], base=0, channel_multiplier=0, allow_small_or_imprecise_dtypes=True)
            pool.memset(before[:], 1.0).then_inc(masks, 1)
            pool.wait_ge(masks, 1)
            pool.affine_select(out=before[:], in_=before[:], compare_op=ALU.is_gt, fill=0.0, base=0,
                               pattern=[[1, P]], channel_multiplier=-1).then_inc(consts, 1)
            split(0, 0)
            fetch(1)
            split(1, 1)
            fetch(2)
            pool.wait_ge(bounds_done, 1)
            for e in range(E):
                end = bound(pool, e + 1)
                pool.dma_start(n.xs_d[ds((end - (SHT + MT)) * P, MT * P), :].rearrange("(n p) d -> p n d", p=P),
                               zero[:]).then_inc(zeroed, 16)
            pool.wait_ge(slot_done, 1)
            pool.wait_ge(zeroed, 16 * E)

            def stage(t, par, used):
                if used is not None:
                    pool.wait_ge(scattered[par], used)
                pool.dma_start(srow[:, par], n.tile_rows(n.xn2_d, t)).then_inc(srow_in[par], 16)
                pool.tensor_copy(scol[:, par], slot[:, :, ds(t, 1)].rearrange("p s o -> p (s o)")).then_inc(scol_done, 1)

            def send(i, par, count):
                hold(pool, srow_in[par], i * 16 + 16, n.passed_pool)
                hold(pool, scol_done, count, n.passed_pool)
                for s in range(2):
                    pool.indirect_dma_start(out=n.xs_d[:, :], out_offset=bass.IndirectOffsetOnAxis(ap=scol[:, par, s:s + 1], axis=0),
                                            in_=srow[:, par], in_offset=None).then_inc(scattered[par], 16)

            for par in range(2):
                stage(par, par, None)
            for par in range(2):
                send(0, par, par + 1)
            with pool.Fori(1, NT // 2) as i:
                for par in range(2):
                    stage(i * 2 + par, par, i * 32)
                for par in range(2):
                    send(i, par, i * 2 + par + 1)
            for e in range(2, NE):
                hold(pool, y_full, (e - 1) * NT if e <= NSH else bound(pool, e - 1 - NSH), n.passed_pool)
                split(e, e % 2)
                if e + 1 < NE:
                    fetch(e + 1)

        @block.scalar
        def _(act):
            act.wait_ge(dif_done, 1)
            act.activation(ex[:], dif[:], ACT.Exp).then_inc(ex_done, 1)

            def slot_of(g, lead, last):
                act.wait_ge(u_full, g + 1)
                act.activation(sg[:], u_ps[:, 0:HID], ACT.Silu).then_inc(sg_done, 1)
                if not last:
                    x_high(g + 1)
                if lead:
                    y_copy(g - 1)
                act.wait_ge(h_full, g + 1)
                act.activation(hT[:, 0], h_ps[:], ACT.Copy).then_inc(h_hi, 1)

            def x_high(g):
                act.wait_ge(x_full, g + 1)
                act.activation(xeT[:, 0], x_ps[:], ACT.Copy).then_inc(x_hi, 1)

            def y_copy(g):
                act.wait_ge(y_full, g + 1)
                if not (isinstance(g, int) and g == 0):
                    act.wait_ge(y_out, g * 16)
                act.activation(ye[:], y_ps[:], ACT.Copy).then_inc(y_copied, 1)
                act.wait_ge(y_copied, g + 1)
                act.dma_start(n.tile_rows(n.ys_d, g), ye[:]).then_inc(y_out, 16)

            x_high(0)
            slot_of(0, False, False)
            act.wait_ge(bounds_done, 1)
            end = bound(act, E)
            with act.Fori(1, end - 1) as g:
                slot_of(g, True, False)
            slot_of(end - 1, True, True)
            y_copy(end - 1)
            act.wait_ge(zero_set, 1)
            with act.Fori(end, SHT + MAXT) as g:
                act.dma_start(n.tile_rows(n.ys_d, g), zero[:, 0]).then_inc(y_out, 16)
            act.wait_ge(y_out, (SHT + MAXT) * 16)

        @block.vector
        def _(dve):
            steps = [0]

            def then(ins):
                steps[0] += 1
                ins.then_inc(route, 1)
                dve.wait_ge(route, steps[0])

            for t in range(NT):
                ins = dve.max(top8[:, t], logits[:, t])
            then(ins)
            for t in range(NT):
                ins = dve.max_index(idx8[:, t], top8[:, t], logits[:, t])
            then(ins)
            dve.tensor_tensor(dif[:], top8[:, :, 1], top8[:, :, 0], ALU.subtract).then_inc(dif_done, 1)
            then(dve.tensor_copy(idx[:], idx8[:, :, 0:2].rearrange("p t s -> p s t")))
            dve.wait_ge(consts, 1)
            for s in range(2):
                ins = dve.tensor_tensor(hot[:, s], idx[:, s].unsqueeze(2).to_broadcast([P, NT, E]),
                                        iota_e[:].unsqueeze(1).to_broadcast([P, NT, E]), ALU.is_equal)
            then(ins)
            dve.tensor_tensor(chosen[:], hot[:, 0], hot[:, 1], ALU.add).then_inc(chosen_done, 1)
            dve.wait_ge(counted, 1)
            then(dve.tensor_copy(tot[:], r_ps[:, 1].rearrange("p (t e) -> p e t", e=E)))
            for e in range(E):
                ins = dve.tensor_tensor_scan(cum[:, e], onesf[:], tot[:, e], 0.0, ALU.mult, ALU.add)
            then(ins)
            then(dve.tensor_tensor(big[:], cum[:, :, NT - 1:NT].to_broadcast([P, E, NT]),
                                   iota_t[:].unsqueeze(1).to_broadcast([P, E, NT]), ALU.is_gt))
            then(dve.tensor_reduce(tiles[:], big[:], AX.X, ALU.add))
            then(dve.tensor_scalar(tiles[:], tiles[:], float(MT), None, ALU.max))
            then(dve.tensor_tensor_scan(tcum[:], onesf[:, 0:E], tiles[:], 0.0, ALU.mult, ALU.add))
            dve.tensor_tensor(first[:, 0:E], tcum[:], tiles[:], ALU.subtract)
            then(dve.tensor_copy(first[:, E:E + 1], tcum[:, E - 1:E]))
            dve.tensor_tensor(bounds[:], first[:], least[:], ALU.subtract).then_inc(bounds_done, 1)
            then(dve.tensor_tensor(base[:], cum[:], tot[:], ALU.subtract))
            then(dve.scalar_tensor_tensor(out=base[:], in0=first[:, 0:E].unsqueeze(2).to_broadcast([P, E, NT]),
                                          scalar=float(P), in1=base[:], op0=ALU.mult, op1=ALU.add))
            then(dve.tensor_tensor(pos[:], r_ps[:, 0].rearrange("p (t e) -> p t e", e=E),
                                   base[:].rearrange("p e t -> p t e"), ALU.add))
            for s in range(2):
                ins = dve.tensor_tensor(sel[:, s], hot[:, s], pos[:], ALU.mult)
            then(ins)
            then(dve.tensor_reduce(posf[:], sel[:], AX.X, ALU.add))
            dve.tensor_scalar(slot_y[:], posf[:], float(SHT * P), None, ALU.add)
            dve.tensor_copy(slot[:], posf[:]).then_inc(slot_done, 1)
            dve.wait_ge(ex_done, 1)
            then(dve.tensor_scalar(den[:], ex[:], 1.0, None, ALU.add))
            then(dve.reciprocal(gate[:, 0], den[:]))
            then(dve.tensor_tensor(gate[:, 1], gate[:, 0], ex[:], ALU.mult))

            def x_low(g):
                dve.wait_ge(x_hi, g + 1)
                dve.tensor_tensor(xeT[:, 1], x_ps[:], xeT[:, 0].bitcast(F32), ALU.subtract).then_inc(x_lo, 1)

            def slot_of(g, last):
                dve.wait_ge(sg_done, g + 1)
                dve.tensor_tensor(hh[:], u_ps[:, HID:2 * HID], sg[:], ALU.mult).then_inc(hh_done, 1)
                if not last:
                    x_low(g + 1)
                dve.wait_ge(h_hi, g + 1)
                dve.tensor_tensor(hT[:, 1], h_ps[:], hT[:, 0].bitcast(F32), ALU.subtract).then_inc(h_lo, 1)

            x_low(0)
            slot_of(0, False)
            dve.wait_ge(bounds_done, 1)
            end = bound(dve, E)
            with dve.Fori(1, end - 1) as g:
                slot_of(g, False)
            slot_of(end - 1, True)

        @block.tensor
        def _(pe):
            pe.wait_ge(consts, 1)
            pe.wait_ge(chosen_done, 1)
            for i, m in enumerate((before, ones)):
                mm = pe.matmul(r_ps[:, i], m[:], chosen[:].rearrange("p t e -> p (t e)"), start=True, stop=True)
            mm.then_inc(counted, 1)

            def x_transposes(g):
                pe.wait_ge(xe_in, g * 16 + 16)
                for k in range(KD):
                    mm = pe.transpose(x_ps[:, k], xe[:, k * P:(k + 1) * P], ident[:])
                mm.then_inc(x_full, 1)

            def up(g, par):
                pe.wait_ge(x_lo, g + 1)
                for k in range(KD):
                    for pa, pb in PASSES:
                        mm = pe.matmul(u_ps[:], xeT[:, pa, k], w[:, par, pb, k * 2 * HID:(k + 1) * 2 * HID],
                                       start=(k == 0 and (pa, pb) == PASSES[0]),
                                       stop=(k == KD - 1 and (pa, pb) == PASSES[-1]))
                mm.then_inc(u_full, 1)

            def down(g, par):
                pe.wait_ge(h_lo, g + 1)
                if not (isinstance(g, int) and g == 0):
                    pe.wait_ge(y_copied, g)
                for k in range(KH):
                    for pa, pb in PASSES:
                        mm = pe.matmul(y_ps[:], hT[:, pa, k], w[:, par, pb, W1N + k * D:W1N + (k + 1) * D],
                                       start=(k == 0 and (pa, pb) == PASSES[0]),
                                       stop=(k == KH - 1 and (pa, pb) == PASSES[-1]))
                mm.then_inc(y_full, 1)

            def h_transposes(g):
                pe.wait_ge(hh_done, g + 1)
                for k in range(KH):
                    mm = pe.transpose(h_ps[:, k], hh[:, k * P:(k + 1) * P], ident[:])
                mm.then_inc(h_full, 1)

            def slot_of(g, par, before_par=None, last=False):
                up(g, par)
                if not last:
                    x_transposes(g + 1)
                if before_par is not None:
                    down(g - 1, before_par)
                h_transposes(g)

            x_transposes(0)
            for e in range(NE):
                par = e % 2
                pe.wait_ge(w_ready, e + 1)
                if e < NSH:
                    lo, hi = e * NT, (e + 1) * NT
                else:
                    if e == NSH:
                        pe.wait_ge(bounds_done, 1)
                    lo, hi = bound(pe, e - NSH), bound(pe, e - NSH + 1)
                slot_of(lo, par, 1 - par if e else None)
                final = e == NE - 1
                with pe.Fori(lo + 1, hi - 1 if final else hi) as g:
                    slot_of(g, par, par)
                if final:
                    slot_of(hi - 1, par, par, True)
                    down(hi - 1, par)


def fuse(nc, n):
    B, C, CP, D, KD, NT, TB = n.B, n.C, n.CP, n.D, n.KD, n.NT, n.TB
    ident, tg, gate, slot_y = n.ident, n.tg, n.gate, n.slot_y

    with ExitStack() as ctx:
        def sb(name, shape, dt=F32):
            return ctx.enter_context(nc.sbuf_tensor(name, shape, dt))

        def sem(name):
            return ctx.enter_context(nc.semaphore(name))

        def psum(name, shape):
            return ctx.enter_context(nc.psum_tensor(name, shape, F32))

        x1 = sb("f_x1", [P, 2, TB, D])
        sh0 = sb("sh0", [P, 2, TB, D])
        sh1 = sb("sh1", [P, 2, TB, D])
        y1 = sb("y1", [P, 2, TB, D])
        y2 = sb("y2", [P, 2, TB, D])
        ycol = sb("ycol", [P, 2, 2, TB], U32)
        gcol = sb("gcol", [P, 2, 2, TB])
        craw = sb("f_craw", [C, 2, D])
        ctraw = sb("f_ctraw", [P, 2, KD, C])
        cx = sb("cx", [C, 2, 2, D], FR)
        cxT = sb("cxT", [P, 2, 2, KD, CP], FR)
        xn = sb("f_xn", [P, TB, D])
        xT = sb("f_xT", [P, 2, TB, KD, P], FR)
        pr = sb("pr", [P, TB, C])
        prT = sb("prT", [C, 2, TB, P], FR)
        x3 = sb("x3", [P, TB, D])
        xq = sb("xq", [P, TB, D])
        xd = sb("xd", [P, TB, D])
        st = sb("f_st", [P, 2, TB, 6])
        mv = sb("f_mv", [P, 2, TB, 2])
        ve = sb("f_ve", [P, 2, TB])
        rs = sb("f_rs", [P, 2, TB])
        nmr = sb("nmr", [P, 2, TB])
        nm = sb("nm", [P, TB])
        su = sb("su", [P, TB])
        ri = sb("f_ri", [P, TB])
        rt = sb("rt", [P, TB])
        am = sb("am", [P, TB])
        ami = sb("ami", [P, TB])
        sc = sb("sc", [P, TB])
        dq = sb("dq", [P, TB])
        half = sb("f_half", [P, TB])
        eps = sb("f_eps", [P, TB])
        t_ps = psum("f_t_ps", [P, 2, KD, P])
        s_ps = psum("f_s_ps", [P, TB, P])
        p_ps = psum("f_p_ps", [P, TB, P])
        o_ps = psum("f_o_ps", [P, 2, D])

        ld_in = [sem("ld_in0"), sem("ld_in1")]
        y_in = [sem("y_in0"), sem("y_in1")]
        consts = sem("f_consts")
        ycol_done = sem("ycol_done")
        gcol_done = sem("gcol_done")
        sh_done = sem("sh_done")
        comb = sem("comb")
        st_done = sem("f_st_done")
        mv1_done = sem("f_mv1_done")
        mv2_done = sem("f_mv2_done")
        ve_done = sem("f_ve_done")
        rs1_done = sem("f_rs1_done")
        rs2_done = sem("f_rs2_done")
        nmr1_done = sem("nmr1_done")
        nmr2_done = sem("nmr2_done")
        xn_done = sem("f_xn_done")
        c_hi = sem("c_hi")
        c_lo = sem("c_lo")
        padded = sem("padded")
        t_full = sem("f_t_full")
        t_hi = sem("f_t_hi")
        t_lo = sem("f_t_lo")
        s_full = sem("f_s_full")
        nm_done = sem("nm_done")
        e_done = sem("f_e_done")
        p_full = sem("p_full")
        p_hi = sem("p_hi")
        p_lo = sem("p_lo")
        ri_done = sem("f_ri_done")
        rt_done = sem("rt_done")
        o_full = sem("o_full")
        x3_done = sem("x3_done")
        x4_done = sem("x4_done")
        am_done = sem("am_done")
        amc_done = sem("amc_done")
        ami_done = sem("ami_done")
        sc_done = sem("sc_done")
        q_done = sem("q_done")
        xd_done = sem("xd_done")
        x3_out = sem("x3_out")
        xd_out = sem("xd_out")

        def whole(eng, run):
            run(-1, False, True)
            run(0, True, True)
            with eng.Fori(1, B // 2) as i:
                run(i * 2 - 1, True, True, 1)
                run(i * 2, True, True, 0)
            run(B - 1, True, False)

        def half_of(s, par):
            return (s + 1) // 2

        assert B % 2 == 0 and B >= 4
        block = ctx.enter_context(nc.Block())

        @block.sync
        def _(sp):
            def load_x1(b, par):
                sp.dma_start(x1[:, par], n.tile_rows(n.x1_d, b * TB, TB)).then_inc(ld_in[par], 16)

            def load(b, par):
                sp.dma_start(sh0[:, par], n.tile_rows(n.ys_d, b * TB, TB)).then_inc(ld_in[par], 16)
                sp.dma_start(sh1[:, par], n.tile_rows(n.ys_d, b * TB + NT, TB)).then_inc(ld_in[par], 16)
                sp.dma_start(craw[:, par], n.ctx[ds(b, 1)].rearrange("o c d -> c (o d)")).then_inc(ld_in[par], 16)
                sp.dma_start(ctraw[:, par], n.ctxT[:, :, ds(b * C, C)]).then_inc(ld_in[par], 16)

            def run(s, mid, front, par=None):
                par = s % 2 if par is None else par
                if isinstance(s, int) and s < 0:
                    for b in range(2):
                        load(b, b)
                        load_x1(b, b)
                    return
                if not (isinstance(s, int) and s >= B - 2):
                    sp.wait_ge(c_lo, (s + 1) * 2)
                    load(s + 2, par)
                if mid:
                    sp.wait_ge(x3_done, (s + 1) * TB)
                    sp.dma_start(n.tile_rows(n.x3_d, s * TB, TB), x3[:]).then_inc(x3_out, 16)
                    if not (isinstance(s, int) and s >= B - 2):
                        load_x1(s + 2, par)
                    sp.wait_ge(xd_done, (s + 1) * TB)
                    sp.dma_start(n.tile_rows(n.xd_d, s * TB, TB), xd[:]).then_inc(xd_out, 16)

            def whole_sp():
                run(-1, False, True)
                run(0, True, True)
                if B > 4:
                    with sp.Fori(1, B // 2 - 1) as i:
                        run(i * 2 - 1, True, True, 1)
                        run(i * 2, True, True, 0)
                for s in range(B - 3, B):
                    run(s, True, True)

            whole_sp()
            sp.wait_ge(x3_out, B * 16)
            sp.wait_ge(xd_out, B * 16)

        @block.gpsimd
        def _(pool):
            def gather(b, par):
                pool.tensor_copy(ycol[:, par], slot_y[:, :, ds(b * TB, TB)]).then_inc(ycol_done, 1)
                hold(pool, ycol_done, b + 1, n.passed_pool)
                for i, y in enumerate((y1, y2)):
                    for j in range(TB):
                        pool.indirect_dma_start(out=y[:, par, j], out_offset=None, in_=n.ys_d[:, :],
                                                in_offset=bass.IndirectOffsetOnAxis(ap=ycol[:, par, i, j:j + 1], axis=0)
                                                ).then_inc(y_in[par], 16)

            def rstd(which, mv_sem, count, out_sem, ve_count):
                pool.wait_ge(mv_sem, count)
                pool.tensor_tensor(ve[:, which], mv[:, which, :, 1], eps[:], ALU.add).then_inc(ve_done, 1)
                pool.wait_ge(ve_done, ve_count)
                pool.tensor_tensor(rs[:, which], ve[:, which], half[:], ALU.pow).then_inc(out_sem, 1)

            def run(s, mid, front, par=None):
                par = s % 2 if par is None else par
                if front:
                    pool.wait_ge(ld_in[1 - par], half_of(s, par) * 80 + 80)
                    for j in range(TB):
                        pool.tensor_tensor(sh0[:, 1 - par, j], sh0[:, 1 - par, j], sh1[:, 1 - par, j],
                                           ALU.add).then_inc(sh_done, 1)
                if mid and gathers(s):
                    hold(pool, comb, (s + 1) * 3 * TB, n.passed_pool)
                    gather(s + 2, par)
                if mid:
                    rstd(1, mv2_done, (s + 1) * TB, rs2_done, s * 2 + 2)
                if front:
                    rstd(0, mv1_done, (s + 2) * TB, rs1_done, s * 2 + 3)

            def gathers(s):
                return not isinstance(s, int) or s < B - 2

            pool.memset(half[:], -0.5)
            pool.memset(eps[:], EPS_LN)
            pool.memset(cxT[:].bitcast(F32), 0.0).then_inc(padded, 1)
            gather(0, 0)
            gather(1, 1)
            run(-1, False, True)
            run(0, True, True)
            if B > 4:
                with pool.Fori(1, B // 2 - 1) as i:
                    run(i * 2 - 1, True, True, 1)
                    run(i * 2, True, True, 0)
            for s in range(B - 3, B):
                run(s, True, s < B - 1)

        @block.scalar
        def _(act):
            def run(s, mid, front, par=None):
                par = s % 2 if par is None else par
                if mid:
                    for j in range(TB):
                        act.wait_ge(t_full, s * TB + j + 1)
                        act.activation(xT[:, 0, j], t_ps[:, j % 2], ACT.Copy).then_inc(t_hi, 1)
                    act.wait_ge(nm_done, s + 1)
                    for j in range(TB):
                        act.activation(pr[:, j], s_ps[:, j, 0:C], ACT.Exp, bias=nm[:, j:j + 1],
                                       accum_out=su[:, j:j + 1]).then_inc(e_done, 1)
                    act.wait_ge(p_full, s + 1)
                    act.activation(prT[:, 0], p_ps[0:C], ACT.Copy).then_inc(p_hi, 1)
                if front:
                    o = 1 - par
                    act.wait_ge(ld_in[o], half_of(s, par) * 80 + 80)
                    act.wait_ge(padded, 1)
                    act.activation(cx[:, o, 0], craw[:, o], ACT.Copy).then_inc(c_hi, 1)
                    act.activation(cxT[:, o, 0, :, 0:C], ctraw[:, o], ACT.Copy).then_inc(c_hi, 1)
                if mid:
                    act.wait_ge(nmr2_done, s + 1)
                    for j in range(TB):
                        act.activation(xq[:, j], x3[:, j], ACT.Identity, bias=nmr[:, 1, j:j + 1],
                                       scale=rs[:, 1, j:j + 1]).then_inc(x4_done, 1)
                if front:
                    act.wait_ge(nmr1_done, s + 2)
                    for j in range(TB):
                        act.activation(xn[:, j], x1[:, 1 - par, j], ACT.Identity, bias=nmr[:, 0, j:j + 1],
                                       scale=rs[:, 0, j:j + 1]).then_inc(xn_done, 1)
                if mid:
                    act.wait_ge(sc_done, s + 1)
                    for j in range(TB):
                        act.activation(xq[:, j], xq[:, j], ACT.Copy, bias=MAGIC, scale=sc[:, j:j + 1]).then_inc(q_done, 1)

            whole(act, run)

        @block.vector
        def _(dve):
            def stats(which, src, mv_sem, base):
                for j in range(TB):
                    dve.bn_stats(st[:, which, j], src[:, j]).then_inc(st_done, 1)
                for j in range(TB):
                    hold(dve, st_done, base + j + 1, n.passed_dve)
                    dve.bn_aggr(mv[:, which, j], st[:, which, j]).then_inc(mv_sem, 1)

            def combine(s, o, tiles, first):
                b = s + 1
                k = b * 3 * TB + (0 if first else 3 * len(tiles))
                for j in tiles:
                    dve.scalar_tensor_tensor(out=y1[:, o, j], in0=y1[:, o, j], scalar=gcol[:, o, 0, j:j + 1],
                                             in1=sh0[:, o, j], op0=ALU.mult, op1=ALU.add).then_inc(comb, 1)
                for i, j in enumerate(tiles):
                    dve.wait_ge(comb, k + i + 1)
                    dve.scalar_tensor_tensor(out=y2[:, o, j], in0=y2[:, o, j], scalar=gcol[:, o, 1, j:j + 1],
                                             in1=y1[:, o, j], op0=ALU.mult, op1=ALU.add).then_inc(comb, 1)
                for i, j in enumerate(tiles):
                    dve.wait_ge(comb, k + len(tiles) + i + 1)
                    dve.scalar_tensor_tensor(out=x1[:, o, j], in0=y2[:, o, j], scalar=tg[:, 2:3],
                                             in1=x1[:, o, j], op0=ALU.mult, op1=ALU.add).then_inc(comb, 1)

            def run(s, mid, front, par=None):
                par = s % 2 if par is None else par
                o = 1 - par
                if mid:
                    for j in range(TB):
                        dve.wait_ge(t_hi, s * TB + j + 1)
                        dve.tensor_tensor(xT[:, 1, j], t_ps[:, j % 2], xT[:, 0, j].bitcast(F32), ALU.subtract).then_inc(t_lo, 1)
                if front:
                    dve.tensor_copy(gcol[:, o], gate[:, :, ds((s + 1) * TB, TB)]).then_inc(gcol_done, 1)
                    dve.wait_ge(gcol_done, s + 2)
                    dve.wait_ge(y_in[o], half_of(s, par) * 32 * TB + 32 * TB)
                    dve.wait_ge(sh_done, (s + 2) * TB)
                    combine(s, o, range(0, TB // 2), True)
                if mid:
                    dve.wait_ge(s_full, s + 1)
                    dve.tensor_reduce(nm[:], s_ps[:, :, 0:C], AX.X, ALU.max, negate=True).then_inc(nm_done, 1)
                if front:
                    combine(s, o, range(TB // 2, TB), False)
                if mid:
                    dve.wait_ge(e_done, s * TB + TB)
                    dve.reciprocal(ri[:], su[:]).then_inc(ri_done, 1)
                    dve.wait_ge(ri_done, s + 1)
                    dve.tensor_scalar(rt[:], ri[:], tg[:, 1:2], None, ALU.mult).then_inc(rt_done, 1)
                    dve.wait_ge(p_hi, s + 1)
                    dve.tensor_tensor(prT[:, 1], p_ps[0:C], prT[:, 0].bitcast(F32), ALU.subtract).then_inc(p_lo, 1)
                if front:
                    dve.wait_ge(c_hi, s * 2 + 3)
                    dve.tensor_tensor(cx[:, o, 1], craw[:, o], cx[:, o, 0].bitcast(F32), ALU.subtract).then_inc(c_lo, 1)
                    dve.wait_ge(c_hi, s * 2 + 4)
                    dve.tensor_tensor(cxT[:, o, 1, :, 0:C], ctraw[:, o], cxT[:, o, 0, :, 0:C].bitcast(F32),
                                      ALU.subtract).then_inc(c_lo, 1)
                if mid:
                    dve.wait_ge(rt_done, s + 1)
                    if not (isinstance(s, int) and s == 0):
                        dve.wait_ge(x3_out, s * 16)
                    for j in range(TB):
                        dve.wait_ge(o_full, s * TB + j + 1)
                        dve.scalar_tensor_tensor(out=x3[:, j], in0=o_ps[:, j % 2], scalar=rt[:, j:j + 1], in1=x1[:, par, j],
                                                 op0=ALU.mult, op1=ALU.add).then_inc(x3_done, 1)
                    dve.wait_ge(x3_done, s * TB + TB)
                    stats(1, x3, mv2_done, s * 2 * TB + TB)
                if front:
                    dve.wait_ge(comb, (s + 2) * 3 * TB)
                    stats(0, x1[:, o], mv1_done, (s + 1) * 2 * TB)
                if mid:
                    dve.wait_ge(rs2_done, s + 1)
                    dve.scalar_tensor_tensor(out=nmr[:, 1], in0=mv[:, 1, :, 0], scalar=-1.0, in1=rs[:, 1], op0=ALU.mult,
                                             op1=ALU.mult).then_inc(nmr2_done, 1)
                if front:
                    dve.wait_ge(rs1_done, s + 2)
                    dve.scalar_tensor_tensor(out=nmr[:, 0], in0=mv[:, 0, :, 0], scalar=-1.0, in1=rs[:, 0], op0=ALU.mult,
                                             op1=ALU.mult).then_inc(nmr1_done, 1)
                if mid:
                    for j in range(TB):
                        dve.wait_ge(x4_done, s * TB + j + 1)
                        dve.tensor_reduce(am[:, j:j + 1], xq[:, j], AX.X, ALU.max, apply_absolute_value=True).then_inc(am_done, 1)
                    dve.wait_ge(am_done, s * TB + TB)
                    dve.tensor_scalar(am[:], am[:], EPS_Q, None, ALU.max).then_inc(amc_done, 1)
                    dve.wait_ge(amc_done, s + 1)
                    dve.reciprocal(ami[:], am[:]).then_inc(ami_done, 1)
                    dve.tensor_scalar(dq[:], am[:], 1.0 / 127.0, None, ALU.mult)
                    dve.wait_ge(ami_done, s + 1)
                    dve.tensor_scalar(sc[:], ami[:], 127.0, None, ALU.mult).then_inc(sc_done, 1)
                    if not (isinstance(s, int) and s == 0):
                        dve.wait_ge(xd_out, s * 16)
                    for j in range(TB):
                        dve.wait_ge(q_done, s * TB + j + 1)
                        dve.tensor_scalar(xd[:, j], xq[:, j], MAGIC, dq[:, j:j + 1], ALU.subtract, ALU.mult).then_inc(xd_done, 1)

            whole(dve, run)

        @block.tensor
        def _(pe):
            def run(s, mid, front, par=None):
                par = s % 2 if par is None else par
                if not mid:
                    return
                for j in range(TB):
                    pe.wait_ge(xn_done, s * TB + j + 1)
                    if not (isinstance(s, int) and s * TB + j < 2):
                        pe.wait_ge(t_lo, s * TB + j - 1)
                    for k in range(KD):
                        mm = pe.transpose(t_ps[:, j % 2, k], xn[:, j, k * P:(k + 1) * P], ident[:])
                    mm.then_inc(t_full, 1)
                pe.wait_ge(t_lo, s * TB + TB)
                pe.wait_ge(c_lo, s * 2 + 2)
                for j in range(TB):
                    for k in range(KD):
                        for pa, pb in PASSES:
                            mm = pe.matmul(s_ps[:, j, 0:CP], xT[:, pa, j, k], cxT[:, par, pb, k],
                                           start=(k == 0 and (pa, pb) == PASSES[0]),
                                           stop=(k == KD - 1 and (pa, pb) == PASSES[-1]))
                mm.then_inc(s_full, 1)
                pe.wait_ge(e_done, s * TB + TB)
                for j in range(TB):
                    mm = pe.transpose(p_ps[0:C, j], pr[:, j], ident[:])
                mm.then_inc(p_full, 1)
                pe.wait_ge(p_lo, s + 1)
                for j in range(TB):
                    if not (isinstance(s, int) and s * TB + j < 2):
                        pe.wait_ge(x3_done, s * TB + j - 1)
                    for pa, pb in PASSES:
                        mm = pe.matmul(o_ps[:, j % 2], prT[:, pa, j], cx[:, par, pb], start=((pa, pb) == PASSES[0]),
                                       stop=((pa, pb) == PASSES[-1]))
                    mm.then_inc(o_full, 1)

            whole(pe, run)


def ffn(nc, n):
    B, S, D, KD, NT, TB, DH, KF = n.B, n.S, n.D, n.KD, n.NT, n.TB, n.DH, n.KF
    ident, tg = n.ident, n.tg
    CH = 4
    WC = KD * DH // CH
    RING = 4

    with ExitStack() as ctx:
        def sb(name, shape, dt=F32, c=ctx):
            return c.enter_context(nc.sbuf_tensor("b_" + name, shape, dt))

        def sem(name, c=ctx):
            return c.enter_context(nc.semaphore("b_" + name))

        w1q = sb("w1q", [P, KD, DH], FR)
        w2q = sb("w2q", [P, KF, D], BF16)
        cw = sb("cw", [P, KF, 3])
        cb = sb("cb", [P, KF])
        g2 = sb("g2", [P, 1])
        ones = sb("ones", [P, P])

        with ExitStack() as c1:
            wr = sb("wr", [P, 2, CH, WC], F32, c1)
            cwr = sb("cwr", [P, KF, 3], F32, c1)
            asum = sb("asum", [P, 2, CH], F32, c1)
            total = sb("total", [P, 2], F32, c1)
            mean = sb("mean", [P, 2], F32, c1)
            inv = sb("inv", [P, 2], F32, c1)
            a_ps = c1.enter_context(nc.psum_tensor("b_a_ps", [P, 2, 512], F32))
            w_in = [[sem(f"w_in{i}{c}", c1) for c in range(CH)] for i in range(2)]
            small_in = sem("small_in", c1)
            set_done = sem("set_done", c1)
            asum_done = sem("asum_done", c1)
            total_full = sem("total_full", c1)
            mean_steps = sem("mean_steps", c1)
            biased = sem("biased", c1)
            clipped = sem("clipped", c1)
            block = c1.enter_context(nc.Block())

            @block.sync
            def _(sp):
                for i in range(2):
                    src = (n.w1T.rearrange("p k f -> p (k f)"), n.w2T.rearrange("p k f -> p (k f)"))[i]
                    for c in range(CH):
                        sp.dma_start(wr[:, i, c], src[:, c * WC:(c + 1) * WC]).then_inc(w_in[i][c], 16)
                    if i == 0:
                        sp.dma_start(cwr[:], n.conv_w).then_inc(small_in, 16)
                        sp.dma_start(cb[:], n.conv_b).then_inc(small_in, 16)

            @block.gpsimd
            def _(pool):
                pool.memset(ones[:], 1.0).then_inc(set_done, 1)

            @block.scalar
            def _(act):
                for i in range(2):
                    act.wait_ge(mean_steps, i * 3 + 3)
                    for c in range(CH):
                        act.activation(wr[:, i, c], wr[:, i, c], ACT.Copy, bias=MAGIC,
                                       scale=inv[:, i:i + 1]).then_inc(biased, 1)

            @block.tensor
            def _(pe):
                pe.wait_ge(set_done, 1)
                for i in range(2):
                    pe.wait_ge(asum_done, CH * (i + 1))
                    pe.matmul(a_ps[:, i, 0:CH], ones[:], asum[:, i], start=True, stop=True).then_inc(total_full, 1)

            @block.vector
            def _(dve):
                outs = (w1q[:].rearrange("p k f -> p (k f)"), w2q[:].rearrange("p k f -> p (k f)"))
                for i in range(2):
                    for c in range(CH):
                        dve.wait_ge(w_in[i][c], 16)
                        dve.tensor_reduce(asum[:, i, c:c + 1], wr[:, i, c], AX.X, ALU.add,
                                          apply_absolute_value=True).then_inc(asum_done, 1)
                    dve.wait_ge(total_full, i + 1)
                    dve.tensor_reduce(total[:, i:i + 1], a_ps[:, i, 0:CH], AX.X, ALU.add).then_inc(mean_steps, 1)
                    dve.wait_ge(mean_steps, i * 3 + 1)
                    dve.tensor_scalar(mean[:, i:i + 1], total[:, i:i + 1], 1.0 / (D * DH), EPS_Q, ALU.mult,
                                      ALU.max).then_inc(mean_steps, 1)
                    dve.wait_ge(mean_steps, i * 3 + 2)
                    dve.reciprocal(inv[:, i:i + 1], mean[:, i:i + 1]).then_inc(mean_steps, 1)
                    if i == 0:
                        dve.wait_ge(small_in, 32)
                        dve.tensor_scalar(cw[:], cwr[:], mean[:, 0:1], None, ALU.mult)
                    else:
                        dve.tensor_scalar(g2[:], mean[:, 1:2], tg[:, 3:4], 1.0 / 127.0, ALU.mult, ALU.mult)
                    for c in range(CH):
                        dve.wait_ge(biased, i * CH + c + 1)
                        dve.tensor_scalar(wr[:, i, c], wr[:, i, c], MAGIC - 1.0, MAGIC + 1.0, ALU.max,
                                          ALU.min).then_inc(clipped, 1)
                        dve.wait_ge(clipped, i * CH + c + 1)
                        dve.tensor_scalar(outs[i][:, c * WC:(c + 1) * WC], wr[:, i, c], MAGIC, None, ALU.subtract)

        xd = sb("xd", [P, TB, D])
        xdT = sb("xdT", [P, 2, KD, TB, P], FR)
        av = sb("av", [P, RING, S])
        h = sb("h", [P, 2, KF, S])
        hq = sb("hq", [P, KF, S], BF16)
        am = sb("am", [P, S])
        mx = sb("mx", [P, TB])
        mxc = sb("mxc", [P, TB])
        mi = sb("mi", [P, TB])
        s2 = sb("s2", [P, TB])
        d2 = sb("d2", [P, 2, TB])
        srow = sb("srow", [P, S])
        x3 = sb("x3", [P, 2, TB, D])
        f_ps = ctx.enter_context(nc.psum_tensor("b_f_ps", [P, RING, 512], F32))
        q_ps = ctx.enter_context(nc.psum_tensor("b_q_ps", [P, TB, P], F32))
        o_ps = ctx.enter_context(nc.psum_tensor("b_o_ps", [P, 2, D], F32))

        xd_in = sem("xd_in")
        x3_in = [sem("x3_in0"), sem("x3_in1")]
        t_full = sem("t_full")
        t_hi = sem("t_hi")
        t_lo = sem("t_lo")
        f_full = sem("f_full")
        mid_tap = sem("mid_tap")
        prev_tap = sem("prev_tap")
        conv_done = sem("conv_done")
        h_done = sem("h_done")
        am_done = sem("am_done")
        amt_full = sem("amt_full")
        scale_steps = sem("scale_steps")
        row_full = sem("row_full")
        row_done = sem("row_done")
        u_done = sem("u_done")
        hq_done = sem("hq_done")
        o_full = sem("o_full")
        o_done = sem("o_done")
        out_done = sem("out_done")

        def whole(run):
            def steps(eng):
                run(-1, False, False, False, True, 1)
                run(0, True, False, False, True, 0)
                run(1, True, True, False, True, 1)
                run(2, True, True, True, True, 0)
                run(3, True, True, True, B > 4, 1)
                if B > 4:
                    with eng.Fori(2, B // 2 - 1) as i:
                        run(i * 2, True, True, True, True, 0)
                        run(i * 2 + 1, True, True, True, True, 1)
                    run(B - 2, True, True, True, True, 0)
                    run(B - 1, True, True, True, False, 1)
                run(B, False, True, True, False, 0)
                run(B + 1, False, False, True, False, 1)
            return steps

        def transposed(j):
            return f_ps[:, j].rearrange("p (k t) -> p k t", t=P)

        assert B % 2 == 0 and B >= 4 and KF == 16 and TB == RING
        rounds = {6: (0,), 7: (1,), 8: (2,), 9: (3, 4), 10: (5,), 11: (6, 7), 12: (8,), 13: (9, 10), 14: (11, 12),
                  15: (13,), 16: (14, 15)}
        block = ctx.enter_context(nc.Block())

        @block.sync
        def _(sp):
            def run(s, f1, quant, f2, front, par):
                if front:
                    if not (isinstance(s, int) and s < 0):
                        sp.wait_ge(t_full, (s + 1) * TB)
                    sp.dma_start(xd[:], n.tile_rows(n.xd_d, (s + 1) * TB, TB)).then_inc(xd_in, 16)
                if quant:
                    if not (isinstance(s, int) and s < 3):
                        sp.wait_ge(out_done, (s - 2) * 16)
                    sp.dma_start(x3[:, 1 - par], n.tile_rows(n.x3_d, (s - 1) * TB, TB)).then_inc(x3_in[1 - par], 16)
                if f2:
                    sp.wait_ge(o_done, (s - 1) * TB)
                    sp.dma_start(n.tile_rows(n.out, (s - 2) * TB, TB), x3[:, par]).then_inc(out_done, 16)

            whole(run)(sp)
            sp.wait_ge(out_done, B * 16)

        @block.gpsimd
        def _(pool):
            def run(s, f1, quant, f2, front, par):
                if not quant:
                    return
                for m in range(KF):
                    if m == 0:
                        pool.wait_ge(row_done, s)
                    pool.tensor_tensor(h[:, 1 - par, m], h[:, 1 - par, m], srow[:], ALU.mult).then_inc(u_done, 1)

            whole(run)(pool)

        @block.scalar
        def _(act):
            def run(s, f1, quant, f2, front, par):
                def silu(m):
                    act.wait_ge(conv_done, s * KF + m + 1)
                    if not (isinstance(s, int) and s < 2):
                        act.wait_ge(hq_done, (s - 2) * KF + m + 1)
                    act.activation(h[:, par, m], av[:, m % RING], ACT.Silu).then_inc(h_done, 1)

                for m in range(KF):
                    if f1:
                        act.wait_ge(f_full, s * KF + m + 1)
                        if m >= RING or not (isinstance(s, int) and s == 0):
                            act.wait_ge(h_done, s * KF + m + 1 - RING)
                        act.activation(av[:, m % RING], f_ps[:, m % RING], ACT.Identity, bias=cb[:, m:m + 1],
                                       scale=cw[:, m, 1:2]).then_inc(mid_tap, 1)
                        if m >= 1:
                            silu(m - 1)
                    if quant and m == 5:
                        act.wait_ge(row_full, s)
                        if not (isinstance(s, int) and s == 1):
                            act.wait_ge(u_done, (s - 1) * KF)
                        act.activation(srow[:], q_ps[:], ACT.Copy).then_inc(row_done, 1)
                if f1:
                    silu(KF - 1)
                if front:
                    for j in range(TB):
                        act.wait_ge(t_full, (s + 1) * TB + j + 1)
                        act.activation(xdT[:, 0, :, j], transposed(j), ACT.Copy).then_inc(t_hi, 1)

            whole(run)(act)

        @block.vector
        def _(dve):
            def run(s, f1, quant, f2, front, par):
                def outputs(j):
                    dve.wait_ge(o_full, (s - 2) * TB + j + 1)
                    dve.wait_ge(x3_in[par], s // 2 * 16)
                    dve.scalar_tensor_tensor(out=x3[:, par, j], in0=o_ps[:, j % 2], scalar=d2[:, par, j:j + 1],
                                             in1=x3[:, par, j], op0=ALU.mult, op1=ALU.add).then_inc(o_done, 1)

                def round_tile(m):
                    dve.wait_ge(u_done, (s - 1) * KF + m + 1)
                    if m == 0 and not (isinstance(s, int) and s == 1):
                        dve.wait_ge(o_full, (s - 1) * TB)
                    dve.tensor_scalar(hq[:, m], h[:, 1 - par, m], MAGIC, MAGIC, ALU.add, ALU.subtract).then_inc(hq_done, 1)

                if quant:
                    dve.wait_ge(h_done, s * KF)
                    dve.tensor_reduce(am[:], h[:, 1 - par].rearrange("p m t -> p t m"), AX.X, ALU.max,
                                      apply_absolute_value=True).then_inc(am_done, 1)
                if f2:
                    outputs(0)
                    outputs(1)
                for m in range(KF + 1):
                    if f1 and m < KF:
                        u = s * KF + m + 1
                        dve.wait_ge(mid_tap, u)
                        a, f = av[:, m % RING], f_ps[:, m % RING]
                        dve.scalar_tensor_tensor(out=a[:, 1:S], in0=f[:, 0:S - 1], scalar=cw[:, m, 0:1], in1=a[:, 1:S],
                                                 op0=ALU.mult, op1=ALU.add).then_inc(prev_tap, 1)
                        dve.wait_ge(prev_tap, u)
                        dve.scalar_tensor_tensor(out=a[:, 0:S - 1], in0=f[:, 1:S], scalar=cw[:, m, 2:3], in1=a[:, 0:S - 1],
                                                 op0=ALU.mult, op1=ALU.add).then_inc(conv_done, 1)
                    if f2 and m in (1, 3):
                        outputs(2 + m // 2)
                    if quant and m == 2:
                        dve.wait_ge(amt_full, s)
                        dve.tensor_reduce(mx[:], q_ps[:], AX.X, ALU.max).then_inc(scale_steps, 1)
                        dve.wait_ge(scale_steps, s * 4 - 3)
                        dve.tensor_scalar(mxc[:], mx[:], EPS_Q, None, ALU.max).then_inc(scale_steps, 1)
                        dve.wait_ge(scale_steps, s * 4 - 2)
                        dve.reciprocal(mi[:], mxc[:]).then_inc(scale_steps, 1)
                        dve.tensor_scalar(d2[:, 1 - par], mxc[:], g2[:], None, ALU.mult)
                        dve.wait_ge(scale_steps, s * 4 - 1)
                        dve.tensor_scalar(s2[:], mi[:], 127.0, None, ALU.mult).then_inc(scale_steps, 1)
                    if m == KF and front:
                        transposed_low(s + 1)
                    if quant:
                        for r in rounds.get(m, ()):
                            round_tile(r)

            def transposed_low(b):
                for j in range(TB):
                    dve.wait_ge(t_hi, b * TB + j + 1)
                    dve.tensor_tensor(xdT[:, 1, :, j], transposed(j), xdT[:, 0, :, j].bitcast(F32),
                                      ALU.subtract).then_inc(t_lo, 1)

            whole(run)(dve)

        @block.tensor
        def _(pe):
            def run(s, f1, quant, f2, front, par):
                def down(j):
                    u = (s - 2) * TB + j
                    if j == 0:
                        pe.wait_ge(hq_done, (s - 1) * KF)
                    if not (isinstance(s, int) and s == 2 and j < 2):
                        pe.wait_ge(o_done, u - 1)
                    for k in range(KF):
                        mm = pe.matmul(o_ps[:, j % 2], hq[:, k, j * P:(j + 1) * P], w2q[:, k, :], start=(k == 0),
                                       stop=(k == KF - 1))
                    mm.then_inc(o_full, 1)

                if f2:
                    down(0)
                    down(1)
                for m in range(KF):
                    if f1:
                        if m == 0:
                            pe.wait_ge(t_lo, (s + 1) * TB)
                        if m >= RING:
                            pe.wait_ge(conv_done, s * KF + m + 1 - RING)
                        for k in range(KD):
                            for part in range(2):
                                mm = pe.matmul(f_ps[:, m % RING], w1q[:, k, m * P:(m + 1) * P], xdT[:, part, k],
                                               start=(k == 0 and part == 0), stop=(k == KD - 1 and part == 1))
                        mm.then_inc(f_full, 1)
                    if f2 and m in (1, 3):
                        down(2 + m // 2)
                    if quant and m == 2:
                        pe.wait_ge(am_done, s)
                        if not (isinstance(s, int) and s == 1):
                            pe.wait_ge(row_done, s - 1)
                        for j in range(TB):
                            mm = pe.transpose(q_ps[:, j], am[:, j * P:(j + 1) * P], ident[:])
                        mm.then_inc(amt_full, 1)
                    if quant and m == 4:
                        pe.wait_ge(scale_steps, s * 4)
                        for j in range(TB):
                            mm = pe.matmul(q_ps[:, j], s2[:, j:j + 1].to_broadcast([P, P]), ident[:], start=True, stop=True)
                        mm.then_inc(row_full, 1)
                if front:
                    pe.wait_ge(xd_in, (s + 2) * 16)
                    for j in range(TB):
                        if f1:
                            pe.wait_ge(conv_done, (s + 1) * KF - RING + j + 1)
                        for k in range(KD):
                            mm = pe.transpose(f_ps[:, j, k * P:(k + 1) * P], xd[:, j, k * P:(k + 1) * P], ident[:])
                        mm.then_inc(t_full, 1)

            whole(run)(pe)


def kernel(x, ctx_1024, g_xattn, g_ffn, L0_xattn_Wq, L0_xattn_bq, L0_xattn_Wk, L0_xattn_bk, L0_xattn_Wv,
           L0_xattn_bv, L0_xattn_Wo, L0_xattn_bo, L0_ffn_router_w, L0_ffn_router_b, L0_ffn_routed_w1,
           L0_ffn_routed_w3, L0_ffn_routed_w2, L0_ffn_shared_w1, L0_ffn_shared_w3, L0_ffn_shared_w2,
           L1_ffn_w1, L1_ffn_conv_w, L1_ffn_conv_b, L1_ffn_w2):
    import numpy as np
    import concourse.bacc as bacc
    from concourse.bass_utils import run_bass_kernel_spmd

    def rows(w):
        w = np.asarray(w)
        return np.swapaxes(w.reshape(*w.shape[:-2], w.shape[-2] // P, P, w.shape[-1]), -3, -2)

    def columns(v):
        return np.asarray(v).reshape(-1, P).T

    x, c = np.asarray(x), np.asarray(ctx_1024)
    B, S, D = x.shape
    w13 = np.concatenate([np.concatenate([L0_ffn_shared_w1, L0_ffn_shared_w3], -1),
                          np.concatenate([L0_ffn_routed_w1, L0_ffn_routed_w3], -1)])
    w2 = np.concatenate([L0_ffn_shared_w2, L0_ffn_routed_w2])
    w1 = np.asarray(L1_ffn_w1)
    ins = {
        "x": x.reshape(B * S, D),
        "ctx": c,
        "ctxT": rows(c.reshape(-1, D).T),
        "gates": np.concatenate([g_xattn, g_ffn]),
        "wqT": rows(np.asarray(L0_xattn_Wq).T),
        "wkT": rows(np.asarray(L0_xattn_Wk).T),
        "wvT": rows(np.asarray(L0_xattn_Wv).T),
        "woT": rows(np.asarray(L0_xattn_Wo).T),
        "bq": columns(L0_xattn_bq),
        "bk": columns(L0_xattn_bk),
        "bv": np.asarray(L0_xattn_bv),
        "bo": np.asarray(L0_xattn_bo),
        "router_w": rows(L0_ffn_router_w),
        "router_b": np.asarray(L0_ffn_router_b),
        "w13": rows(w13),
        "w2e": rows(w2),
        "w1T": rows(w1.T),
        "conv_w": np.asarray(L1_ffn_conv_w).reshape(-1, P, 3).swapaxes(0, 1),
        "conv_b": columns(L1_ffn_conv_b),
        "w2T": rows(np.asarray(L1_ffn_w2).T),
    }
    nc = bacc.Bacc("TRN2", target_bir_lowering=False, num_devices=1)
    arrays, aps = {}, {}
    for name, a in ins.items():
        a = np.ascontiguousarray(a)
        arrays[f"in_{name}"] = a
        aps[name] = nc.dram_tensor(f"in_{name}", a.shape, mybir.dt.from_np(a.dtype), kind="ExternalInput").ap()
    out = nc.dram_tensor("out", (B * S, D), F32, kind="ExternalOutput").ap()
    flamingo(nc, **aps, out=out)
    r = run_bass_kernel_spmd(nc, [arrays], core_ids=[0])
    return r.results[0]["out"].reshape(B, S, D)
```

```python
from contextlib import ExitStack

import concourse.bass as bass
from concourse import mybir

F32 = mybir.dt.float32
FR = mybir.dt.float32r
BF16 = mybir.dt.bfloat16
I32 = mybir.dt.int32
U32 = mybir.dt.uint32
ALU = mybir.AluOpType
ACT = mybir.ActivationFunctionType
AX = mybir.AxisListType
ds = bass.ds

P = 128
MAGIC = 12582912.0
PASSES = ((0, 0), (0, 1), (1, 0))
EPS_LN = 1e-5
EPS_Q = 1e-5


class Program:
    pass


def flamingo(nc, x, ctx, ctxT, gates, wqT, wkT, wvT, woT, bq, bk, bv, bo, router_w, router_b,
             w13, w2e, w1T, conv_w, conv_b, w2T, out):
    B, C, D = ctx.shape
    T = x.shape[0]
    S = T // B
    KD = D // P
    NT = T // P
    TB = S // P
    HD = 32
    H = D // HD
    HG = P // HD
    NG = H // HG
    CP = C + C % 2
    E = router_w.shape[2]
    NE = w13.shape[0]
    NSH = NE - E
    HID = w13.shape[3] // 2
    KH = HID // P
    MIN_TILES = 3
    MAXT = 2 * NT + MIN_TILES * E
    DH = w1T.shape[2]
    KF = DH // P
    SCALE = float(HD) ** -0.5

    x1_d = nc.dram_tensor("x1_scratch", [T, D], F32)
    xn2_d = nc.dram_tensor("xn2_scratch", [T, D], F32)
    xs_d = nc.dram_tensor("slots_in_scratch", [MAXT * P, D], F32)
    ys_d = nc.dram_tensor("experts_out_scratch", [MAXT * P, D], F32)
    x2_d = nc.dram_tensor("x2_scratch", [T, D], F32)
    w1q_d = nc.dram_tensor("w1q_scratch", [P, KD * DH], FR)
    w2q_d = nc.dram_tensor("w2q_scratch", [P, KF * D], BF16)
    x3_d = nc.dram_tensor("x3_scratch", [T, D], F32)
    xd_d = nc.dram_tensor("xd_scratch", [T, D], F32)

    def tile_rows(t, first, n=1):
        if n == 1:
            return t[ds(first * P, P), :]
        return t[ds(first * P, n * P), :].rearrange("(n p) d -> p n d", p=P)

    with ExitStack() as top:
        def keep(name, shape, dt):
            return top.enter_context(nc.sbuf_tensor(name, shape, dt))

        ident = keep("ident", [P, P], F32)
        tg = keep("tanh_gates", [P, 4], F32)
        logits = keep("logits", [P, NT, E], F32)
        gate = keep("gate", [P, 2, NT], F32)
        slot = keep("slot", [P, 2, NT], U32)
        mean = keep("mean", [P, 2], F32)

        passed_dve = top.enter_context(nc.semaphore("passed_dve"))
        passed_pool = top.enter_context(nc.semaphore("passed_pool"))

        n = Program()
        n.B = B
        n.C = C
        n.CP = CP
        n.D = D
        n.DH = DH
        n.E = E
        n.H = H
        n.HD = HD
        n.HG = HG
        n.HID = HID
        n.KD = KD
        n.KF = KF
        n.KH = KH
        n.MAXT = MAXT
        n.MIN_TILES = MIN_TILES
        n.NE = NE
        n.NG = NG
        n.NSH = NSH
        n.NT = NT
        n.S = S
        n.SCALE = SCALE
        n.T = T
        n.TB = TB
        n.bk = bk
        n.bo = bo
        n.bq = bq
        n.bv = bv
        n.conv_b = conv_b
        n.conv_w = conv_w
        n.ctx = ctx
        n.ctxT = ctxT
        n.gate = gate
        n.gates = gates
        n.ident = ident
        n.logits = logits
        n.out = out
        n.passed_dve = passed_dve
        n.passed_pool = passed_pool
        n.router_b = router_b
        n.router_w = router_w
        n.slot = slot
        n.mean = mean
        n.x2_d = x2_d
        n.w1q_d = w1q_d
        n.w2q_d = w2q_d
        n.tg = tg
        n.tile_rows = tile_rows
        n.w13 = w13
        n.w1T = w1T
        n.w2T = w2T
        n.w2e = w2e
        n.wkT = wkT
        n.woT = woT
        n.wqT = wqT
        n.wvT = wvT
        n.x = x
        n.x1_d = x1_d
        n.x3_d = x3_d
        n.xd_d = xd_d
        n.xn2_d = xn2_d
        n.xs_d = xs_d
        n.ys_d = ys_d

        attention(nc, n)
        experts(nc, n)

        n.w1q = keep("w1q", [P, KD, DH], FR)
        n.w2q = keep("w2q", [P, KF, D], BF16)
        n.cw = keep("cw", [P, KF, 3], F32)
        n.cb = keep("cb", [P, KF], F32)
        n.g2 = keep("g2", [P, 1], F32)
        fuse(nc, n)
        ffn(nc, n)


def hold(eng, sem, value, passed):
    eng.wait_ge(sem, value)
    eng.sem_inc(passed, 1)


def attention(nc, n):
    B, C, D, S, KD, NT, TB, HD, H, HG, NG, E = n.B, n.C, n.D, n.S, n.KD, n.NT, n.TB, n.HD, n.H, n.HG, n.NG, n.E
    ident, tg, logits = n.ident, n.tg, n.logits
    W2 = 2 * P
    NSTEP = n.T // W2
    GC = HG * C

    with ExitStack() as ctx:
        def sb(name, shape, dt, c=ctx):
            return c.enter_context(nc.sbuf_tensor(name, shape, dt))

        def sem(name, c=ctx):
            return c.enter_context(nc.semaphore(name))

        wq = sb("wq", [P, 2, KD, D], FR)
        wo = sb("wo", [P, 2, KD, D], FR)
        kc = sb("k_all", [P, B, NG, C], F32)
        vc = sb("v_all", [C, B, D], F32)
        kbd = sb("k_blocks", [P, 2, NG, GC], FR)
        vbd = sb("v_blocks", [C, 2, H, P], FR)
        bq_s = sb("bq_s", [P, NG], F32)
        bo_t = sb("bo_t", [P, D], F32)
        rw = sb("rw", [P, KD, E], F32)
        rb = sb("rb", [P, E], F32)
        half = sb("minus_half", [P, 2], F32)
        eps = sb("eps", [P, 2], F32)

        with ExitStack() as c1:
            wraw = sb("wraw", [P, 4, KD, D], F32, c1)
            wkv = sb("wkv", [P, 2, 2, KD, D], FR, c1)
            craw = sb("craw", [P, KD, B * C], F32, c1)
            cts = sb("cts", [P, 2, KD, B * C], FR, c1)
            bk_s = sb("bk_s", [P, NG], F32, c1)
            bv_s = sb("bv_s", [C, D], F32, c1)
            bo_s = sb("bo_s", [P, D], F32, c1)
            graw = sb("graw", [P, 4], F32, c1)
            kv_ps = [c1.enter_context(nc.psum_tensor(f"kv_ps{i}", [P, 512], F32)) for i in range(4)]
            ctx_in = sem("ctx_in", c1)
            small_in = sem("small_in", c1)
            w_in = [sem(f"w_in{i}", c1) for i in range(4)]
            hi_done = sem("hi_done", c1)
            lo_done = sem("lo_done", c1)
            cleared = sem("cleared", c1)
            id_done = sem("id_done", c1)
            tanh_done = sem("tanh_done", c1)
            kv_full = sem("kv_full", c1)
            kv_free = sem("kv_free", c1)
            block = c1.enter_context(nc.Block())
            srcs = [craw[:], wraw[:, 0], wraw[:, 1], wraw[:, 2], wraw[:, 3]]
            his = [cts[:, 0], wkv[:, 0, 0], wkv[:, 1, 0], wq[:, 0], wo[:, 0]]
            los = [cts[:, 1], wkv[:, 0, 1], wkv[:, 1, 1], wq[:, 1], wo[:, 1]]
            loaded = [(ctx_in, 16), (w_in[0], 16), (w_in[1], 16), (w_in[2], 16), (w_in[3], 16)]

            @block.sync
            def _(sp):
                sp.dma_start(craw[:], n.ctxT).then_inc(ctx_in, 16)
                for i, w in enumerate((n.wkT, n.wvT, n.wqT, n.woT)):
                    sp.dma_start(wraw[:, i], w).then_inc(w_in[i], 16)
                sp.dma_start(bq_s[:], n.bq).then_inc(small_in, 16)
                sp.dma_start(bk_s[:], n.bk).then_inc(small_in, 16)
                sp.dma_start(bv_s[:], n.bv.partition_broadcast(C)).then_inc(small_in, 16)
                sp.dma_start(bo_s[:], n.bo.partition_broadcast(P)).then_inc(small_in, 16)
                sp.dma_start(rb[:], n.router_b.partition_broadcast(P)).then_inc(small_in, 16)
                sp.dma_start(graw[:], n.gates.partition_broadcast(P)).then_inc(small_in, 16)
                sp.dma_start(rw[:], n.router_w).then_inc(small_in, 16)

            @block.gpsimd
            def _(pool):
                pool.memset(half[:], -0.5)
                pool.memset(eps[:], EPS_LN)
                pool.memset(kbd[:].bitcast(F32), 0.0)
                pool.memset(vbd[:].bitcast(F32), 0.0)
                pool.memset(ident[:], 0.0).then_inc(cleared, 1)
                pool.wait_ge(cleared, 1)
                pool.affine_select(out=ident[:], in_=ident[:], compare_op=ALU.not_equal, fill=1.0, base=0,
                                   pattern=[[-1, P]], channel_multiplier=1).then_inc(id_done, 1)

            @block.scalar
            def _(act):
                for s, h, (q, v) in zip(srcs, his, loaded):
                    act.wait_ge(q, v)
                    act.activation(h, s, ACT.Copy).then_inc(hi_done, 1)
                act.wait_ge(small_in, 112)
                act.activation(tg[:], graw[:], ACT.Tanh).then_inc(tanh_done, 1)

            @block.vector
            def _(dve):
                def lo(i):
                    dve.wait_ge(hi_done, i + 1)
                    dve.wait_ge(loaded[i][0], loaded[i][1])
                    dve.tensor_tensor(los[i], srcs[i], his[i].bitcast(F32), ALU.subtract).then_inc(lo_done, 1)

                for i in range(3):
                    lo(i)
                dve.wait_ge(small_in, 112)
                use = 0
                for half_b in range(2):
                    for m in range(NG):
                        dve.wait_ge(kv_full, use + 1)
                        bs = slice(half_b * B // 2, (half_b + 1) * B // 2)
                        dve.tensor_scalar(kc[:, bs, m, :],
                                          kv_ps[use % 4][:, 0:B // 2 * C].rearrange("p (b c) -> p b c", c=C),
                                          bk_s[:, m:m + 1], None, ALU.add).then_inc(kv_free, 1)
                        use += 1
                for b in range(B):
                    dve.wait_ge(kv_full, use + 1)
                    dve.tensor_tensor(vc[:, b], kv_ps[use % 4][0:C, :], bv_s[:], ALU.add).then_inc(kv_free, 1)
                    use += 1
                for i in range(3, 5):
                    lo(i)
                dve.wait_ge(tanh_done, 1)
                dve.tensor_scalar(bo_t[:], bo_s[:], tg[:, 0:1], None, ALU.mult)

            @block.tensor
            def _(pe):
                use = 0
                pe.wait_ge(lo_done, 2)
                N = B // 2 * C
                for half_b in range(2):
                    for m in range(NG):
                        if use >= 4:
                            pe.wait_ge(kv_free, use - 3)
                        for k in range(KD):
                            for pa, pb in PASSES:
                                mm = pe.matmul(kv_ps[use % 4][:, 0:N], wkv[:, 0, pa, k, m * P:(m + 1) * P],
                                               cts[:, pb, k, half_b * N:(half_b + 1) * N],
                                               start=(k == 0 and (pa, pb) == PASSES[0]),
                                               stop=(k == KD - 1 and (pa, pb) == PASSES[-1]))
                        mm.then_inc(kv_full, 1)
                        use += 1
                pe.wait_ge(lo_done, 3)
                for bb in range(B):
                    pe.wait_ge(kv_free, use - 3)
                    for k in range(KD):
                        for pa, pb in PASSES:
                            mm = pe.matmul(kv_ps[use % 4][0:C, :], cts[:, pa, k, bb * C:(bb + 1) * C],
                                           wkv[:, 1, pb, k, :],
                                           start=(k == 0 and (pa, pb) == PASSES[0]),
                                           stop=(k == KD - 1 and (pa, pb) == PASSES[-1]))
                    mm.then_inc(kv_full, 1)
                    use += 1

        xin = sb("xin", [P, 2, D], F32)
        xn = sb("xn", [P, 2, D], F32)
        xT = sb("xT", [P, 2, KD, W2], FR)
        qT = sb("qT", [P, 2, 2, NG, W2], FR)
        prob = sb("prob", [P, 2, H, C], F32)
        pT = sb("pT", [C, 2, H, W2], FR)
        oT = sb("oT", [P, 2, NG, W2], FR)
        xres = sb("xres", [P, 2, D], F32)
        x1 = sb("x1", [P, 2, D], F32)
        xn2 = sb("xn2", [P, 2, D], F32)
        x2T = sb("x2T", [P, KD, W2], F32)
        st1 = sb("st1", [P, 2, 6], F32)
        mv1 = sb("mv1", [P, 2, 2], F32)
        ve1 = sb("ve1", [P, 2], F32)
        rs1 = sb("rs1", [P, 2], F32)
        st2 = sb("st2", [P, 2, 6], F32)
        mv2 = sb("mv2", [P, 2, 2], F32)
        ve2 = sb("ve2", [P, 2], F32)
        rs2 = sb("rs2", [P, 2], F32)
        mx = sb("mx", [P, 2, H], F32)
        sm = sb("sm", [P, 2, H], F32)
        ri = sb("ri", [P, 2, H], F32)
        s_ps = ctx.enter_context(nc.psum_tensor("s_ps", [P, NG, 512], F32))
        t_ps = ctx.enter_context(nc.psum_tensor("t_ps", [P, 2, 512], F32))
        m_ps = ctx.enter_context(nc.psum_tensor("m_ps", [P, 2, 512], F32))

        x_in = sem("x_in")
        xres_in = sem("xres_in")
        mv1_done = sem("mv1_done")
        mv2_done = sem("mv2_done")
        st_done = sem("st_done")
        rs_tmp = sem("rs_tmp")
        rs1_done = sem("rs1_done")
        rs2_done = sem("rs2_done")
        xn_done = sem("xn_done")
        xb_done = sem("xb_done")
        t_full = sem("t_full")
        t_hi = sem("t_hi")
        t_free = sem("t_free")
        m_full = sem("m_full")
        m_hi = sem("m_hi")
        m_free = sem("m_free")
        s_full = sem("s_full")
        s_sub = sem("s_sub")
        mx_done = sem("mx_done")
        e_done = sem("e_done")
        sum_done = sem("sum_done")
        ri_done = sem("ri_done")
        p_done = sem("p_done")
        bd_hi = sem("bd_hi")
        k_bd = sem("k_bd")
        v_bd = sem("v_bd")
        xn2_done = sem("xn2_done")
        x1_out = sem("x1_out")
        xn2_out = sem("xn2_out")


        def whole(eng, run):
            run(-1, -1, False, False, True)
            run(0, 0, True, False, True)
            run(1, 0, True, True, True)
            if B > 2:
                with eng.Fori(1, B - 1) as b:
                    run(b * 2, b, True, True, True, 0)
                    run(b * 2 + 1, b, True, True, True, 1)
            run(NSTEP - 2, B - 1, True, True, True)
            run(NSTEP - 1, B - 1, True, True, False)
            run(NSTEP, B, False, True, False)

        def before(s, first, front, back):
            if isinstance(s, int):
                return max(0, min(s + 1, NSTEP)) * front + max(0, s) * first + max(0, s - 1) * back
            return s * (front + first + back) + (front - back)

        def t_base(s):
            return before(s, 2 * NG, 2, 2)

        def hi_base(s):
            return before(s, 2 * NG, 2, 0)

        def m_base(s):
            return before(s, 0, 2, 6)

        def plan(mid, back, front):
            t = (["x0", "x1"] if front else []) + ([("p", 0, g) for g in range(NG)] if mid else []) \
                + (["n0", "n1"] if back else []) + ([("p", 1, g) for g in range(NG)] if mid else [])
            m = (["o0", "o1", "w0", "w1"] if back else []) + (["q0", "q1"] if front else []) \
                + (["r0", "r1"] if back else [])
            return {u: i for i, u in enumerate(t)}, {u: i for i, u in enumerate(m)}

        def kc_heads(q, b):
            return kc[q, ds(b, 1), :, :].rearrange("p o g c -> p (o g) c")

        def vbd_heads(part, i):
            return vbd[:, part].rearrange("c (g i) p -> c g i p", i=HG)[:, :, i, i * HD:(i + 1) * HD]

        def vc_heads(b, i):
            return vc[:, ds(b, 1), :].rearrange("c o (g i d) -> c (o g) i d", i=HG, d=HD)[:, :, i, :]

        assert NG == 4 and B >= 2
        block = ctx.enter_context(nc.Block())

        @block.sync
        def _(sp):
            def run(s, b, mid, back, front, par=None):
                par = s % 2 if par is None else par
                if front:
                    if not (isinstance(s, int) and s < 0):
                        sp.wait_ge(xn_done, (s + 1) * 2)
                    sp.dma_start(xin[:], tile_rows2(n.x, s + 1)).then_inc(x_in, 16)
                if back:
                    sp.dma_start(xres[:], tile_rows2(n.x, s - 1)).then_inc(xres_in, 16)
                    for j in range(2):
                        sp.wait_ge(m_free, m_base(s) + plan(mid, back, front)[1][f"w{j}"] + 1)
                        sp.dma_start(n.tile_rows(n.x1_d, (s - 1) * 2 + j), x1[:, j]).then_inc(x1_out, 16)
                    for j in range(2):
                        sp.wait_ge(xn2_done, (s - 1) * 2 + j + 1)
                        sp.dma_start(n.tile_rows(n.xn2_d, (s - 1) * 2 + j), xn2[:, j]).then_inc(xn2_out, 16)

            def tile_rows2(t, s):
                return n.tile_rows(t, s * 2, 2)

            whole(sp, run)
            sp.wait_ge(x1_out, 16 * NT)
            sp.wait_ge(xn2_out, 16 * NT)

        @block.gpsimd
        def _(pool):
            def rstd(mv_sem, count, mv, ve, rs, out_sem, tmp_count):
                pool.wait_ge(mv_sem, count)
                pool.tensor_tensor(ve[:], mv[:, :, 1], eps[:], ALU.add).then_inc(rs_tmp, 1)
                pool.wait_ge(rs_tmp, tmp_count)
                pool.tensor_tensor(rs[:], ve[:], half[:], ALU.pow).then_inc(out_sem, 1)

            def run(s, b, mid, back, front, par=None):
                par = s % 2 if par is None else par
                tmp = before(s, 0, 1, 1)
                if front:
                    rstd(mv1_done, s * 2 + 4, mv1, ve1, rs1, rs1_done, tmp + 1)
                if back:
                    pool.wait_ge(xres_in, s * 16)
                    for j in range(2):
                        pool.tensor_tensor(xres[:, j], xres[:, j], bo_t[:], ALU.add).then_inc(xb_done, 1)
                if mid:
                    normalise(s, 0)
                if back:
                    rstd(mv2_done, s * 2, mv2, ve2, rs2, rs2_done, tmp + (2 if front else 1))
                if mid:
                    normalise(s, 1)

            def normalise(s, j):
                pool.wait_ge(ri_done, s * 2 + j + 1)
                pool.tensor_tensor(prob[:, j], prob[:, j], ri[:, j].unsqueeze(2).to_broadcast([P, H, C]),
                                   ALU.mult).then_inc(p_done, 1)

            whole(pool, run)

        @block.scalar
        def _(act):
            def hi(full, count, done, dst, src):
                act.wait_ge(full, count)
                act.activation(dst, src, ACT.Copy).then_inc(done, 1)

            def run(s, b, mid, back, front, par=None):
                par = s % 2 if par is None else par
                tb, mb = t_base(s), m_base(s)
                t, m = plan(mid, back, front)

                def keys(b):
                    for i in range(HG):
                        q = slice(i * HD, (i + 1) * HD)
                        act.activation(kbd[q, 0, :, i * C:(i + 1) * C], kc_heads(q, b),
                                       ACT.Copy).then_inc(bd_hi, 1)

                def tcopy(u, dst, parts=P):
                    i = t[u]
                    act.wait_ge(t_full, tb + i + 1)
                    act.activation(dst, t_ps[0:parts, i % 2].rearrange("p (a b) -> p a b", b=P), ACT.Copy).then_inc(t_hi, 1)

                def exps(j):
                    for pair in range(2):
                        act.wait_ge(s_sub, s * 4 + 2 * j + pair + 1)
                        g = slice(pair * H // 2, (pair + 1) * H // 2)
                        act.activation(prob[:, j, g], prob[:, j, g], ACT.Exp, scale=n.SCALE).then_inc(e_done, 1)

                if mid:
                    exps(0)
                if back:
                    for i, u in enumerate(("o0", "o1")):
                        act.wait_ge(m_full, mb + m[u] + 1)
                        act.activation(oT[:, 0, 2 * i:2 * i + 2], m_ps[:, m[u] % 2].rearrange("p (a b) -> p a b", b=W2),
                                       ACT.Copy).then_inc(m_hi, 1)
                if mid and par == 0:
                    for i in range(HG):
                        act.activation(vbd_heads(0, i), vc_heads(b, i), ACT.Copy).then_inc(bd_hi, 1)
                if front:
                    for j in range(2):
                        tcopy(f"x{j}", xT[:, 0, :, j * P:(j + 1) * P])
                if mid:
                    exps(1)
                    for g in range(NG):
                        tcopy(("p", 0, g), pT[:, 0, g * HG:(g + 1) * HG, 0:P], C)
                if par == 1 and front:
                    keys(b + 1)
                if front:
                    for i in range(2):
                        u = f"q{i}"
                        act.wait_ge(m_full, mb + m[u] + 1)
                        for g in range(2):
                            act.activation(qT[:, 1 - par, 0, 2 * i + g], m_ps[:, m[u] % 2, g * W2:(g + 1) * W2],
                                           ACT.Identity, bias=bq_s[:, 2 * i + g:2 * i + g + 1]).then_inc(m_hi, 1)
                if mid:
                    for g in range(NG):
                        tcopy(("p", 1, g), pT[:, 0, g * HG:(g + 1) * HG, P:W2], C)

            whole(act, run)

        @block.vector
        def _(dve):
            def run(s, b, mid, back, front, par=None):
                par = s % 2 if par is None else par
                tb, mb = t_base(s), m_base(s)
                t, m = plan(mid, back, front)
                hb = before(s, 0, 4, 2)
                sb0 = before(s, 0, 2, 2)

                def keys(b):
                    for i in range(HG):
                        q = slice(i * HD, (i + 1) * HD)
                        dve.wait_ge(bd_hi, b * 2 * HG + i + 1)
                        hi = kbd[q, 0, :, i * C:(i + 1) * C].bitcast(F32)
                        dve.tensor_tensor(kbd[q, 1, :, i * C:(i + 1) * C],
                                          kc_heads(q, b), hi,
                                          ALU.subtract).then_inc(k_bd, 1)

                def tlow(u, dst, hi_ap, parts=P):
                    i = t[u]
                    after_n = 2 if back and i > t["n1"] else 0
                    dve.wait_ge(t_hi, hi_base(s) + i - after_n + 1)
                    dve.tensor_tensor(dst, t_ps[0:parts, i % 2].rearrange("p (a b) -> p a b", b=P),
                                      hi_ap.bitcast(F32), ALU.subtract).then_inc(t_free, 1)

                def softmax_in(j):
                    for pair in range(2):
                        dve.wait_ge(s_full, s * 4 + 2 * j + pair + 1)
                        hs = slice(pair * H // 2, (pair + 1) * H // 2)
                        sc = s_ps[:, 2 * pair:2 * pair + 2, 0:GC].rearrange("p g (i c) -> p g i c", c=C)
                        mxp = mx[:, j, hs].rearrange("p (g i) -> p g i", i=HG)
                        dve.tensor_reduce(mxp, sc, AX.X, ALU.max).then_inc(mx_done, 1)
                        dve.wait_ge(mx_done, s * 4 + 2 * j + pair + 1)
                        dve.tensor_tensor(prob[:, j, hs].rearrange("p (g i) c -> p g i c", i=HG), sc,
                                          mxp.unsqueeze(3).to_broadcast([P, 2, HG, C]), ALU.subtract).then_inc(s_sub, 1)

                def softmax_sum(j):
                    dve.wait_ge(e_done, s * 4 + 2 * j + 2)
                    dve.tensor_reduce(sm[:, j], prob[:, j], AX.X, ALU.add).then_inc(sum_done, 1)
                    dve.wait_ge(sum_done, s * 2 + j + 1)
                    dve.reciprocal(ri[:, j], sm[:, j]).then_inc(ri_done, 1)

                def norm_stats(src_of, st, mv, done, base):
                    for j in range(2):
                        dve.bn_stats(st[:, j], src_of(j)).then_inc(st_done, 1)
                    for j in range(2):
                        hold(dve, st_done, base + j + 1, n.passed_dve)
                        dve.bn_aggr(mv[:, j], st[:, j]).then_inc(done, 1)

                if front:
                    dve.wait_ge(x_in, s * 16 + 32)
                    norm_stats(lambda j: xin[:, j], st1, mv1, mv1_done, sb0)
                if mid:
                    softmax_in(0)
                if front:
                    dve.wait_ge(rs1_done, s + 2)
                    for j in range(2):
                        dve.tensor_scalar(xn[:, j], xin[:, j], mv1[:, j, 0:1], rs1[:, j:j + 1], ALU.subtract,
                                          ALU.mult).then_inc(xn_done, 1)
                if back:
                    for i, u in enumerate(("o0", "o1")):
                        dve.wait_ge(m_hi, hb + i + 1)
                        dve.tensor_tensor(oT[:, 1, 2 * i:2 * i + 2], m_ps[:, m[u] % 2].rearrange("p (a b) -> p a b", b=W2),
                                          oT[:, 0, 2 * i:2 * i + 2].bitcast(F32), ALU.subtract).then_inc(m_free, 1)
                if mid and par == 0:
                    for i in range(HG):
                        dve.wait_ge(bd_hi, b * 2 * HG + HG + i + 1)
                        dve.tensor_tensor(vbd_heads(1, i), vc_heads(b, i), vbd_heads(0, i).bitcast(F32),
                                          ALU.subtract).then_inc(v_bd, 1)
                if mid:
                    softmax_sum(0)
                    softmax_in(1)
                if front:
                    for j in range(2):
                        tlow(f"x{j}", xT[:, 1, :, j * P:(j + 1) * P], xT[:, 0, :, j * P:(j + 1) * P])
                if back:
                    dve.wait_ge(xb_done, s * 2)
                    if not (isinstance(s, int) and s <= 1):
                        dve.wait_ge(x1_out, (s - 1) * 32)
                    for j in range(2):
                        u = f"w{j}"
                        dve.wait_ge(m_full, mb + m[u] + 1)
                        dve.scalar_tensor_tensor(out=x1[:, j], in0=m_ps[:, m[u] % 2], scalar=tg[:, 0:1], in1=xres[:, j],
                                                 op0=ALU.mult, op1=ALU.add).then_inc(m_free, 1)
                    dve.wait_ge(m_free, mb + m["w1"] + 1)
                    norm_stats(lambda j: x1[:, j], st2, mv2, mv2_done, sb0 + (2 if front else 0))
                if mid:
                    for g in range(NG):
                        hs = slice(g * HG, (g + 1) * HG)
                        tlow(("p", 0, g), pT[:, 1, hs, 0:P], pT[:, 0, hs, 0:P], C)
                        if g == 1:
                            softmax_sum(1)
                if par == 1 and front:
                    keys(b + 1)
                if back:
                    dve.wait_ge(rs2_done, s)
                    if not (isinstance(s, int) and s <= 1):
                        dve.wait_ge(xn2_out, (s - 1) * 32)
                    for j in range(2):
                        dve.tensor_scalar(xn2[:, j], x1[:, j], mv2[:, j, 0:1], rs2[:, j:j + 1], ALU.subtract,
                                          ALU.mult).then_inc(xn2_done, 1)
                for i in range(2):
                    if front:
                        u = f"q{i}"
                        for g in range(2):
                            dve.wait_ge(m_hi, hb + (2 if back else 0) + 2 * i + 2)
                            ins = dve.scalar_tensor_tensor(
                                out=qT[:, 1 - par, 1, 2 * i + g], in0=m_ps[:, m[u] % 2, g * W2:(g + 1) * W2],
                                scalar=bq_s[:, 2 * i + g:2 * i + g + 1], in1=qT[:, 1 - par, 0, 2 * i + g].bitcast(F32),
                                op0=ALU.add, op1=ALU.subtract)
                        ins.then_inc(m_free, 1)
                    if back and i == 0:
                        for j in range(2):
                            dve.wait_ge(t_full, tb + t[f"n{j}"] + 1)
                            dve.tensor_copy(x2T[:, :, j * P:(j + 1) * P],
                                            t_ps[:, t[f"n{j}"] % 2].rearrange("p (a b) -> p a b", b=P)).then_inc(t_free, 1)
                if back:
                    for j in range(2):
                        u = f"r{j}"
                        dve.wait_ge(m_full, mb + m[u] + 1)
                        dve.tensor_tensor(logits[:, ds((s - 1) * 2 + j, 1), :].rearrange("p o e -> p (o e)"),
                                          m_ps[:, m[u] % 2, 0:E], rb[:], ALU.add).then_inc(m_free, 1)
                if mid:
                    for g in range(NG):
                        hs = slice(g * HG, (g + 1) * HG)
                        tlow(("p", 1, g), pT[:, 1, hs, P:W2], pT[:, 0, hs, P:W2], C)

            whole(dve, run)

        @block.tensor
        def _(pe):
            def run(s, b, mid, back, front, par=None):
                par = s % 2 if par is None else par
                tb, mb = t_base(s), m_base(s)
                t, m = plan(mid, back, front)

                def t_room(u):
                    if not (isinstance(s, int) and tb + t[u] < 2):
                        pe.wait_ge(t_free, tb + t[u] - 1)

                def m_room(u):
                    if not (isinstance(s, int) and mb + m[u] < 2):
                        pe.wait_ge(m_free, mb + m[u] - 1)

                def scores(j):
                    for g in range(NG):
                        if g % 2 == 0 and not (isinstance(s, int) and s * 4 + 2 * j + g // 2 < 2):
                            pe.wait_ge(s_sub, s * 4 + 2 * j + g // 2 - 1)
                        for pa, pb in PASSES:
                            mm = pe.matmul(s_ps[:, g, 0:GC], qT[:, par, pa, g, j * P:(j + 1) * P], kbd[:, pb, g, :],
                                           start=((pa, pb) == PASSES[0]), stop=((pa, pb) == PASSES[-1]))
                        if g % 2:
                            mm.then_inc(s_full, 1)

                def prob_transposes(j):
                    pe.wait_ge(p_done, s * 2 + j + 1)
                    for g in range(NG):
                        t_room(("p", j, g))
                        for i in range(HG):
                            mm = pe.transpose(t_ps[0:C, t[("p", j, g)] % 2, i * P:(i + 1) * P], prob[:, j, g * HG + i, :],
                                              ident[:])
                        mm.then_inc(t_full, 1)

                if mid:
                    if par == 0:
                        pe.wait_ge(k_bd, b * HG + HG)
                    pe.wait_ge(m_free, mb)
                    scores(0)
                if back:
                    pe.wait_ge(t_free, tb)
                    pe.wait_ge(v_bd, (b - 1 if par == 0 else b) * HG + HG)
                    for i in range(2):
                        m_room(f"o{i}")
                        for g in range(2):
                            for h in range(HG):
                                hh = (2 * i + g) * HG + h
                                for pa, pb in PASSES:
                                    mm = pe.matmul(m_ps[:, m[f"o{i}"] % 2, g * W2:(g + 1) * W2], vbd[:, pa, hh, :],
                                                   pT[:, pb, hh, :], start=(h == 0 and (pa, pb) == PASSES[0]),
                                                   stop=(h == HG - 1 and (pa, pb) == PASSES[-1]))
                        mm.then_inc(m_full, 1)
                if mid:
                    scores(1)
                if front:
                    pe.wait_ge(xn_done, s * 2 + 4)
                    for j in range(2):
                        t_room(f"x{j}")
                        for k in range(KD):
                            mm = pe.transpose(t_ps[:, t[f"x{j}"] % 2, k * P:(k + 1) * P], xn[:, j, k * P:(k + 1) * P],
                                              ident[:])
                        mm.then_inc(t_full, 1)
                if back:
                    pe.wait_ge(m_free, mb + m["o1"] + 1)
                    for j in range(2):
                        m_room(f"w{j}")
                        for k in range(KD):
                            for pa, pb in PASSES:
                                mm = pe.matmul(m_ps[:, m[f"w{j}"] % 2], oT[:, pa, k, j * P:(j + 1) * P], wo[:, pb, k, :],
                                               start=(k == 0 and (pa, pb) == PASSES[0]),
                                               stop=(k == KD - 1 and (pa, pb) == PASSES[-1]))
                        mm.then_inc(m_full, 1)
                if mid:
                    prob_transposes(0)
                if front:
                    pe.wait_ge(t_free, tb + t["x1"] + 1)
                    for i in range(2):
                        m_room(f"q{i}")
                        for g in range(2):
                            mt = 2 * i + g
                            for k in range(KD):
                                for pa, pb in PASSES:
                                    mm = pe.matmul(m_ps[:, m[f"q{i}"] % 2, g * W2:(g + 1) * W2],
                                                   wq[:, pa, k, mt * P:(mt + 1) * P], xT[:, pb, k, :],
                                                   start=(k == 0 and (pa, pb) == PASSES[0]),
                                                   stop=(k == KD - 1 and (pa, pb) == PASSES[-1]))
                        mm.then_inc(m_full, 1)
                if back:
                    pe.wait_ge(xn2_done, s * 2)
                    for j in range(2):
                        t_room(f"n{j}")
                        for k in range(KD):
                            mm = pe.transpose(t_ps[:, t[f"n{j}"] % 2, k * P:(k + 1) * P], xn2[:, j, k * P:(k + 1) * P],
                                              ident[:])
                        mm.then_inc(t_full, 1)
                    pe.wait_ge(t_free, tb + t["n1"] + 1)
                    for j in range(2):
                        m_room(f"r{j}")
                        for k in range(KD):
                            mm = pe.matmul(m_ps[:, m[f"r{j}"] % 2, 0:E], x2T[:, k, j * P:(j + 1) * P], rw[:, k, :],
                                           start=(k == 0), stop=(k == KD - 1))
                        mm.then_inc(m_full, 1)
                if mid:
                    prob_transposes(1)

            whole(pe, run)


def experts(nc, n):
    NT, E, KD, D, KH, HID, NSH, NE = n.NT, n.E, n.KD, n.D, n.KH, n.HID, n.NSH, n.NE
    MT, MAXT, DH = n.MIN_TILES, n.MAXT, n.DH
    ident, logits, gate, slot, tg, mean = n.ident, n.logits, n.gate, n.slot, n.tg, n.mean
    NC = 4
    WC = KD * DH // NC
    WN = KD * 2 * HID + KH * D
    W1N = KD * 2 * HID

    with ExitStack() as ctx:
        def sb(name, shape, dt):
            return ctx.enter_context(nc.sbuf_tensor("e_" + name, shape, dt))

        def sem(name):
            return ctx.enter_context(nc.semaphore("e_" + name))

        def psum(name, shape, dt=F32):
            return ctx.enter_context(nc.psum_tensor("e_" + name, shape, dt))

        top8 = sb("top8", [P, NT, 8], F32)
        idx8 = sb("idx8", [P, NT, 8], U32)
        idx = sb("idx", [P, 2, NT], F32)
        iota_e = sb("iota_e", [P, E], F32)
        iota_t = sb("iota_t", [P, NT], F32)
        hot = sb("hot", [P, 2, NT, E], F32)
        chosen = sb("chosen", [P, NT, E], BF16)
        before = sb("before", [P, P], BF16)
        ones = sb("ones", [P, P], BF16)
        onesf = sb("onesf", [P, NT], F32)
        tot = sb("tot", [P, E, NT], F32)
        cum = sb("cum", [P, E, NT], F32)
        big = sb("big", [P, E, NT], F32)
        tiles = sb("tiles", [P, E], F32)
        tcum = sb("tcum", [P, E], F32)
        first = sb("first", [P, E + 1], F32)
        least = sb("least", [P, E + 1], F32)
        bounds = sb("bounds", [P, E + 1], I32)
        base = sb("base", [P, E, NT], F32)
        pos = sb("pos", [P, NT, E], F32)
        sel = sb("sel", [P, 2, NT, E], F32)
        posf = sb("posf", [P, 2, NT], F32)
        dif = sb("dif", [P, NT], F32)
        ex = sb("ex", [P, NT], F32)
        den = sb("den", [P, NT], F32)
        zero = sb("zero", [P, MT, D], F32)
        srow = sb("srow", [P, 2, D], F32)
        scol = sb("scol", [P, 2, 2], U32)
        wraw = sb("wraw", [P, WN], F32)
        w = sb("w", [P, 2, 2, WN], FR)
        xe = sb("xe", [P, D], F32)
        xr = sb("xr", [P, D], F32)
        x2 = sb("x2", [P, D], F32)
        xeT = sb("xeT", [P, 2, KD, P], FR)
        sg = sb("sg", [P, NSH, HID], F32)
        hh = sb("hh", [P, NSH, HID], F32)
        hT = sb("hT", [P, 2, NSH * KH, P], FR)
        ye = sb("ye", [P, D], F32)
        r_ps = psum("r_ps", [P, 2, NT * E])
        x_ps = psum("x_ps", [P, KD, P])
        u_ps = psum("u_ps", [P, NSH, 2 * HID])
        h_ps = psum("h_ps", [P, NSH * KH, P])
        y_ps = psum("y_ps", [P, D])
        s_ps = psum("s_ps", [P, 512])
        fraw = sb("fraw", [P, 2, WC], F32)
        asum = sb("asum", [P, 2, NC], F32)
        inv = sb("inv", [P, 2], F32)
        fones = sb("fones", [P, P], F32)
        f1q = sb("f1q", [P, WC], FR)
        f2q = sb("f2q", [P, WC], BF16)

        zero_set = sem("zero_set")
        consts = sem("consts")
        masks = sem("masks")
        route = sem("route")
        chosen_done = sem("chosen_done")
        counted = sem("counted")
        bounds_done = sem("bounds_done")
        dif_done = sem("dif_done")
        ex_done = sem("ex_done")
        slot_done = sem("slot_done")
        zeroed = sem("zeroed")
        srow_in = [sem("srow_in0"), sem("srow_in1")]
        scol_done = sem("scol_done")
        scattered = [sem("scattered0"), sem("scattered1")]
        w_in = sem("w_in")
        w_hi = sem("w_hi")
        w_ready = sem("w_ready")
        xe_in = sem("xe_in")
        x_full = sem("x_full")
        x_hi = sem("x_hi")
        x_lo = sem("x_lo")
        u_full = sem("u_full")
        sg_done = sem("sg_done")
        hh_done = sem("hh_done")
        h_full = sem("h_full")
        h_hi = sem("h_hi")
        h_lo = sem("h_lo")
        y_full = sem("y_full")
        y_copied = sem("y_copied")
        y_out = sem("y_out")
        xr_in = sem("xr_in")
        x2_done = sem("x2_done")
        x2_out = sem("x2_out")
        f_in = [sem("f_in0"), sem("f_in1")]
        asum_done = sem("asum_done")
        asum_full = sem("asum_full")
        mean_steps = sem("mean_steps")
        fq_in = sem("fq_in")
        fq_steps = sem("fq_steps")
        fq_out = sem("fq_out")

        def bound(eng, e):
            return eng.value_load(bounds[0:1, e:e + 1], min_val=0, max_val=MAXT - MT * E) + MT * e

        def f_chunk(c):
            src = (n.w1T, n.w2T)[c // NC].rearrange("p k f -> p (k f)")
            return src[:, c % NC * WC:(c % NC + 1) * WC]

        block = ctx.enter_context(nc.Block())

        @block.sync
        def _(sp):
            def load(src, row_tile, g):
                if not (isinstance(g, int) and g == 0):
                    sp.wait_ge(x_full, g)
                sp.dma_start(xe[:], n.tile_rows(src, row_tile)).then_inc(xe_in, 16)

            def store_x2(t):
                sp.wait_ge(x2_done, t + 1)
                sp.dma_start(n.tile_rows(n.x2_d, t), x2[:]).then_inc(x2_out, 16)

            def load_x1(t):
                sp.dma_start(xr[:], n.tile_rows(n.x1_d, t)).then_inc(xr_in, 16)

            load(n.xn2_d, 0, 0)
            load_x1(0)
            load(n.xn2_d, 1, 1)
            with sp.Fori(1, NT - 1) as t:
                load(n.xn2_d, t + 1, t + 1)
                store_x2(t - 1)
                load_x1(t)
            store_x2(NT - 2)
            load_x1(NT - 1)
            sp.wait_ge(bounds_done, 1)
            for par in range(2):
                sp.wait_ge(scattered[par], NT // 2 * 32)
            load(n.xs_d, 0, NT)
            store_x2(NT - 1)
            end = bound(sp, E)
            with sp.Fori(1, end) as r:
                load(n.xs_d, r, r + NT)
            sp.wait_ge(x2_out, NT * 16)

        @block.gpsimd
        def _(pool):
            def fetch(e):
                pool.dma_start(wraw[:, 0:W1N].rearrange("p (k f) -> p k f", k=KD), n.w13[ds(e, 1)].rearrange("o p k f -> p (o k) f")).then_inc(w_in, 16)
                pool.dma_start(wraw[:, W1N:WN].rearrange("p (k f) -> p k f", k=KH), n.w2e[ds(e, 1)].rearrange("o p k f -> p (o k) f")).then_inc(w_in, 16)

            def split(e, par):
                pool.wait_ge(w_in, e * 32 + 32)
                pool.tensor_copy(w[:, par, 0], wraw[:]).then_inc(w_hi, 1)
                pool.wait_ge(w_hi, e + 1)
                pool.tensor_tensor(w[:, par, 1], wraw[:], w[:, par, 0].bitcast(F32), ALU.subtract).then_inc(w_ready, 1)
                pool.wait_ge(w_ready, e + 1)

            def quantise(c):
                i = c // NC
                out = (f1q, f2q)[i]
                if c == 0:
                    pool.wait_ge(mean_steps, 3)
                else:
                    pool.wait_ge(fq_steps, c * 3)
                pool.dma_start(fraw[:, 0], f_chunk(c)).then_inc(fq_in, 16)
                pool.wait_ge(fq_in, c * 16 + 16)
                pool.tensor_scalar(fraw[:, 0], fraw[:, 0], inv[:, i:i + 1], MAGIC, ALU.mult, ALU.add).then_inc(fq_steps, 1)
                pool.wait_ge(fq_steps, c * 3 + 1)
                pool.tensor_scalar(fraw[:, 0], fraw[:, 0], MAGIC - 1.0, MAGIC + 1.0, ALU.max, ALU.min).then_inc(fq_steps, 1)
                pool.wait_ge(fq_steps, c * 3 + 2)
                if c:
                    pool.wait_ge(fq_out, c * 16)
                pool.tensor_scalar(out[:], fraw[:, 0], MAGIC, None, ALU.subtract).then_inc(fq_steps, 1)
                pool.wait_ge(fq_steps, c * 3 + 3)
                dst = (n.w1q_d, n.w2q_d)[i]
                pool.dma_start(dst[:, c % NC * WC:(c % NC + 1) * WC], out[:]).then_inc(fq_out, 16)

            fetch(0)
            pool.memset(zero[:], 0.0).then_inc(zero_set, 1)
            pool.memset(onesf[:], 1.0)
            pool.memset(ones[:], 1.0)
            pool.memset(fones[:], 1.0)
            pool.iota(iota_e[:], pattern=[[1, E]], base=0, channel_multiplier=0, allow_small_or_imprecise_dtypes=True)
            pool.iota(least[:], pattern=[[MT, E + 1]], base=0, channel_multiplier=0, allow_small_or_imprecise_dtypes=True)
            pool.iota(iota_t[:], pattern=[[P, NT]], base=0, channel_multiplier=0, allow_small_or_imprecise_dtypes=True)
            pool.memset(before[:], 1.0).then_inc(masks, 1)
            pool.wait_ge(masks, 1)
            pool.affine_select(out=before[:], in_=before[:], compare_op=ALU.is_gt, fill=0.0, base=0,
                               pattern=[[1, P]], channel_multiplier=-1).then_inc(consts, 1)
            split(0, 0)
            fetch(1)
            split(1, 1)
            fetch(2)
            pool.wait_ge(bounds_done, 1)
            for e in range(E):
                end = bound(pool, e + 1)
                pool.dma_start(n.xs_d[ds((end - MT) * P, MT * P), :].rearrange("(n p) d -> p n d", p=P),
                               zero[:]).then_inc(zeroed, 16)
            pool.wait_ge(slot_done, 1)
            pool.wait_ge(zeroed, 16 * E)

            def stage(t, par, used):
                if used is not None:
                    pool.wait_ge(scattered[par], used)
                pool.dma_start(srow[:, par], n.tile_rows(n.xn2_d, t)).then_inc(srow_in[par], 16)
                pool.tensor_copy(scol[:, par], slot[:, :, ds(t, 1)].rearrange("p s o -> p (s o)")).then_inc(scol_done, 1)

            def send(i, par, count):
                hold(pool, srow_in[par], i * 16 + 16, n.passed_pool)
                hold(pool, scol_done, count, n.passed_pool)
                for s in range(2):
                    pool.indirect_dma_start(out=n.xs_d[:, :], out_offset=bass.IndirectOffsetOnAxis(ap=scol[:, par, s:s + 1], axis=0),
                                            in_=srow[:, par], in_offset=None).then_inc(scattered[par], 16)

            for par in range(2):
                stage(par, par, None)
            for par in range(2):
                send(0, par, par + 1)
            with pool.Fori(1, NT // 2) as i:
                for par in range(2):
                    stage(i * 2 + par, par, i * 32)
                for par in range(2):
                    send(i, par, i * 2 + par + 1)
            for c in range(2 * NC):
                quantise(c)
            for e in range(NSH, NE):
                if e < NSH + 2:
                    pool.wait_ge(y_full, NT)
                else:
                    hold(pool, y_full, bound(pool, e - 1 - NSH) + NT, n.passed_pool)
                split(e, e % 2)
                if e + 1 < NE:
                    fetch(e + 1)
            pool.wait_ge(fq_out, 16 * 2 * NC)

        @block.scalar
        def _(act):
            act.wait_ge(dif_done, 1)
            act.activation(ex[:], dif[:], ACT.Exp).then_inc(ex_done, 1)

            def shared(t, last=False):
                for i in range(NSH):
                    act.wait_ge(u_full, t * NSH + i + 1)
                    act.activation(sg[:, i], u_ps[:, i, 0:HID], ACT.Silu).then_inc(sg_done, 1)
                if not last:
                    x_high(t + 1)
                act.wait_ge(h_full, t + 1)
                act.activation(hT[:, 0], h_ps[:], ACT.Copy).then_inc(h_hi, 1)
                if last:
                    x_high(t + 1)

            def routed(r, lead, last):
                g = r + NT
                act.wait_ge(u_full, g + NT * (NSH - 1) + 1)
                act.activation(sg[:, 0], u_ps[:, 0, 0:HID], ACT.Silu).then_inc(sg_done, 1)
                if not last:
                    x_high(g + 1)
                if lead:
                    y_copy(r - 1)
                act.wait_ge(h_full, g + 1)
                act.activation(hT[:, 0, 0:KH], h_ps[:, 0:KH], ACT.Copy).then_inc(h_hi, 1)

            def x_high(g):
                act.wait_ge(x_full, g + 1)
                act.activation(xeT[:, 0], x_ps[:], ACT.Copy).then_inc(x_hi, 1)

            def y_copy(r):
                act.wait_ge(y_full, r + NT + 1)
                if not (isinstance(r, int) and r == 0):
                    act.wait_ge(y_out, r * 16)
                act.activation(ye[:], y_ps[:], ACT.Copy).then_inc(y_copied, 1)
                act.wait_ge(y_copied, r + 1)
                act.dma_start(n.tile_rows(n.ys_d, r), ye[:]).then_inc(y_out, 16)

            def sum_chunk(c):
                act.wait_ge(f_in[c % 2], c // 2 * 16 + 16)
                act.activation(fraw[:, c % 2], fraw[:, c % 2], ACT.Abs,
                               accum_out=asum[:, c // NC, c % NC:c % NC + 1]).then_inc(asum_done, 1)
                if c + 2 < 2 * NC:
                    act.wait_ge(asum_done, c + 1)
                    act.dma_start(fraw[:, c % 2], f_chunk(c + 2)).then_inc(f_in[c % 2], 16)

            for c in range(2):
                act.dma_start(fraw[:, c], f_chunk(c)).then_inc(f_in[c], 16)
            x_high(0)
            for t in range(2 * NC):
                shared(t)
                sum_chunk(t)
            with act.Fori(2 * NC, NT - 1) as t:
                shared(t)
            shared(NT - 1, True)
            routed(0, False, False)
            act.wait_ge(bounds_done, 1)
            end = bound(act, E)
            with act.Fori(1, end - 1) as r:
                routed(r, True, False)
            routed(end - 1, True, True)
            y_copy(end - 1)
            act.wait_ge(zero_set, 1)
            with act.Fori(end, MAXT) as r:
                act.dma_start(n.tile_rows(n.ys_d, r), zero[:, 0]).then_inc(y_out, 16)
            act.wait_ge(y_out, MAXT * 16)

        @block.vector
        def _(dve):
            steps = [0]

            def then(ins):
                steps[0] += 1
                ins.then_inc(route, 1)
                dve.wait_ge(route, steps[0])

            for t in range(NT):
                ins = dve.max(top8[:, t], logits[:, t])
            then(ins)
            for t in range(NT):
                ins = dve.max_index(idx8[:, t], top8[:, t], logits[:, t])
            then(ins)
            dve.tensor_tensor(dif[:], top8[:, :, 1], top8[:, :, 0], ALU.subtract).then_inc(dif_done, 1)
            then(dve.tensor_copy(idx[:], idx8[:, :, 0:2].rearrange("p t s -> p s t")))
            dve.wait_ge(consts, 1)
            for s in range(2):
                ins = dve.tensor_tensor(hot[:, s], idx[:, s].unsqueeze(2).to_broadcast([P, NT, E]),
                                        iota_e[:].unsqueeze(1).to_broadcast([P, NT, E]), ALU.is_equal)
            then(ins)
            dve.tensor_tensor(chosen[:], hot[:, 0], hot[:, 1], ALU.add).then_inc(chosen_done, 1)
            dve.wait_ge(counted, 1)
            then(dve.tensor_copy(tot[:], r_ps[:, 1].rearrange("p (t e) -> p e t", e=E)))
            for e in range(E):
                ins = dve.tensor_tensor_scan(cum[:, e], onesf[:], tot[:, e], 0.0, ALU.mult, ALU.add)
            then(ins)
            then(dve.tensor_tensor(big[:], cum[:, :, NT - 1:NT].to_broadcast([P, E, NT]),
                                   iota_t[:].unsqueeze(1).to_broadcast([P, E, NT]), ALU.is_gt))
            then(dve.tensor_reduce(tiles[:], big[:], AX.X, ALU.add))
            then(dve.tensor_scalar(tiles[:], tiles[:], float(MT), None, ALU.max))
            then(dve.tensor_tensor_scan(tcum[:], onesf[:, 0:E], tiles[:], 0.0, ALU.mult, ALU.add))
            dve.tensor_tensor(first[:, 0:E], tcum[:], tiles[:], ALU.subtract)
            then(dve.tensor_copy(first[:, E:E + 1], tcum[:, E - 1:E]))
            dve.tensor_tensor(bounds[:], first[:], least[:], ALU.subtract).then_inc(bounds_done, 1)
            then(dve.tensor_tensor(base[:], cum[:], tot[:], ALU.subtract))
            then(dve.scalar_tensor_tensor(out=base[:], in0=first[:, 0:E].unsqueeze(2).to_broadcast([P, E, NT]),
                                          scalar=float(P), in1=base[:], op0=ALU.mult, op1=ALU.add))
            then(dve.tensor_tensor(pos[:], r_ps[:, 0].rearrange("p (t e) -> p t e", e=E),
                                   base[:].rearrange("p e t -> p t e"), ALU.add))
            for s in range(2):
                ins = dve.tensor_tensor(sel[:, s], hot[:, s], pos[:], ALU.mult)
            then(ins)
            then(dve.tensor_reduce(posf[:], sel[:], AX.X, ALU.add))
            dve.tensor_copy(slot[:], posf[:]).then_inc(slot_done, 1)
            dve.wait_ge(ex_done, 1)
            then(dve.tensor_scalar(den[:], ex[:], 1.0, None, ALU.add))
            then(dve.reciprocal(den[:], den[:]))
            then(dve.tensor_scalar(gate[:, 0], den[:], tg[:, 2:3], None, ALU.mult))
            then(dve.tensor_tensor(gate[:, 1], gate[:, 0], ex[:], ALU.mult))

            def x_low(g):
                dve.wait_ge(x_hi, g + 1)
                dve.tensor_tensor(xeT[:, 1], x_ps[:], xeT[:, 0].bitcast(F32), ALU.subtract).then_inc(x_lo, 1)

            def shared(t, lead=True, last=False):
                for i in range(NSH):
                    dve.wait_ge(sg_done, t * NSH + i + 1)
                    dve.tensor_tensor(hh[:, i], u_ps[:, i, HID:2 * HID], sg[:, i], ALU.mult).then_inc(hh_done, 1)
                if not last:
                    x_low(t + 1)
                if lead:
                    add_shared(t - 1)
                dve.wait_ge(h_hi, t + 1)
                dve.tensor_tensor(hT[:, 1], h_ps[:], hT[:, 0].bitcast(F32), ALU.subtract).then_inc(h_lo, 1)
                if last:
                    add_shared(t)
                    x_low(t + 1)

            def add_shared(t):
                dve.wait_ge(y_full, t + 1)
                dve.wait_ge(xr_in, t * 16 + 16)
                if not (isinstance(t, int) and t == 0):
                    dve.wait_ge(x2_out, t * 16)
                dve.scalar_tensor_tensor(out=x2[:], in0=y_ps[:], scalar=tg[:, 2:3], in1=xr[:], op0=ALU.mult,
                                         op1=ALU.add).then_inc(x2_done, 1)

            def routed(r, last):
                g = r + NT
                dve.wait_ge(sg_done, g + NT * (NSH - 1) + 1)
                dve.tensor_tensor(hh[:, 0], u_ps[:, 0, HID:2 * HID], sg[:, 0], ALU.mult).then_inc(hh_done, 1)
                if not last:
                    x_low(g + 1)
                dve.wait_ge(h_hi, g + 1)
                dve.tensor_tensor(hT[:, 1, 0:KH], h_ps[:, 0:KH], hT[:, 0, 0:KH].bitcast(F32),
                                  ALU.subtract).then_inc(h_lo, 1)

            x_low(0)
            for t in range(2 * NC + 2):
                shared(t, t > 0)
            dve.wait_ge(asum_full, 1)
            dve.tensor_reduce(inv[:], s_ps[:, 0:2 * NC].rearrange("p (i c) -> p i c", c=NC), AX.X, ALU.add).then_inc(mean_steps, 1)
            dve.wait_ge(mean_steps, 1)
            dve.tensor_scalar(mean[:], inv[:], 1.0 / (D * DH), EPS_Q, ALU.mult, ALU.max).then_inc(mean_steps, 1)
            dve.wait_ge(mean_steps, 2)
            dve.reciprocal(inv[:], mean[:]).then_inc(mean_steps, 1)
            with dve.Fori(2 * NC + 2, NT - 1) as t:
                shared(t)
            shared(NT - 1, True, True)
            routed(0, False)
            dve.wait_ge(bounds_done, 1)
            end = bound(dve, E)
            with dve.Fori(1, end - 1) as r:
                routed(r, False)
            routed(end - 1, True)

        @block.tensor
        def _(pe):
            pe.wait_ge(consts, 1)
            pe.wait_ge(chosen_done, 1)
            for i, m in enumerate((before, ones)):
                mm = pe.matmul(r_ps[:, i], m[:], chosen[:].rearrange("p t e -> p (t e)"), start=True, stop=True)
            mm.then_inc(counted, 1)

            def x_transposes(g):
                pe.wait_ge(xe_in, g * 16 + 16)
                for k in range(KD):
                    mm = pe.transpose(x_ps[:, k], xe[:, k * P:(k + 1) * P], ident[:])
                mm.then_inc(x_full, 1)

            def up(g, i, par):
                pe.wait_ge(x_lo, g + 1)
                for k in range(KD):
                    for pa, pb in PASSES:
                        mm = pe.matmul(u_ps[:, i], xeT[:, pa, k], w[:, par, pb, k * 2 * HID:(k + 1) * 2 * HID],
                                       start=(k == 0 and (pa, pb) == PASSES[0]),
                                       stop=(k == KD - 1 and (pa, pb) == PASSES[-1]))
                mm.then_inc(u_full, 1)

            def down(g, pars):
                pe.wait_ge(h_lo, g + 1)
                for i, par in enumerate(pars):
                    for k in range(KH):
                        for pa, pb in PASSES:
                            mm = pe.matmul(y_ps[:], hT[:, pa, i * KH + k], w[:, par, pb, W1N + k * D:W1N + (k + 1) * D],
                                           start=(i == 0 and k == 0 and (pa, pb) == PASSES[0]),
                                           stop=(i == len(pars) - 1 and k == KH - 1 and (pa, pb) == PASSES[-1]))
                mm.then_inc(y_full, 1)

            def h_transposes(count, parts):
                pe.wait_ge(hh_done, count)
                for i in range(parts):
                    for k in range(KH):
                        mm = pe.transpose(h_ps[:, i * KH + k], hh[:, i, k * P:(k + 1) * P], ident[:])
                mm.then_inc(h_full, 1)

            def shared(t, lead=True):
                for i in range(NSH):
                    up(t, i, i)
                x_transposes(t + 1)
                if lead:
                    if not (isinstance(t, int) and t <= 1):
                        pe.wait_ge(x2_done, t - 1)
                    down(t - 1, range(NSH))
                h_transposes((t + 1) * NSH, NSH)

            def routed(r, par, before_par=None, last=False):
                up(r + NT, 0, par)
                if not last:
                    x_transposes(r + NT + 1)
                if before_par is not None:
                    if not (isinstance(r, int) and r == 1):
                        pe.wait_ge(y_copied, r - 1)
                    down(r + NT - 1, (before_par,))
                h_transposes(r + NT * NSH + 1, 1)

            x_transposes(0)
            pe.wait_ge(w_ready, NSH)
            for t in range(2 * NC + 1):
                shared(t, t > 0)
            pe.wait_ge(asum_done, 2 * NC)
            pe.matmul(s_ps[:, 0:2 * NC], fones[:], asum[:].rearrange("p i c -> p (i c)"), start=True,
                      stop=True).then_inc(asum_full, 1)
            with pe.Fori(2 * NC + 1, NT - 1) as t:
                shared(t)
            for i in range(NSH):
                up(NT - 1, i, i)
            pe.wait_ge(x2_done, NT - 2)
            down(NT - 2, range(NSH))
            h_transposes(NT * NSH, NSH)
            pe.wait_ge(x2_done, NT - 1)
            down(NT - 1, range(NSH))
            x_transposes(NT)
            pe.wait_ge(x2_done, NT)
            for q in range(E):
                e = q + NSH
                par = e % 2
                pe.wait_ge(w_ready, e + 1)
                if q == 0:
                    routed(0, par)
                    routed(1, par, par)
                    pe.wait_ge(bounds_done, 1)
                    first_tile = 2
                else:
                    first_tile = bound(pe, q)
                    routed(first_tile, par, 1 - par)
                    first_tile = first_tile + 1
                end = bound(pe, q + 1)
                final = q == E - 1
                with pe.Fori(first_tile, end - 1 if final else end) as r:
                    routed(r, par, par)
                if final:
                    routed(end - 1, par, par, True)
                    pe.wait_ge(y_copied, end - 1)
                    down(end + (NT - 1), (par,))


def fuse(nc, n):
    B, C, CP, D, KD, NT, TB = n.B, n.C, n.CP, n.D, n.KD, n.NT, n.TB
    ident, tg, gate, slot = n.ident, n.tg, n.gate, n.slot

    with ExitStack() as ctx:
        def sb(name, shape, dt=F32):
            return ctx.enter_context(nc.sbuf_tensor(name, shape, dt))

        def sem(name):
            return ctx.enter_context(nc.semaphore(name))

        def psum(name, shape):
            return ctx.enter_context(nc.psum_tensor(name, shape, F32))

        x1 = sb("f_x1", [P, 2, TB, D])
        y1 = sb("y1", [P, 2, TB, D])
        y2 = sb("y2", [P, 2, TB, D])
        ycol = sb("ycol", [P, 2, 2, TB], U32)
        gcol = sb("gcol", [P, 2, 2, TB])
        cwr = sb("cwr", [P, n.KF, 3])
        craw = sb("f_craw", [C, 2, D])
        ctraw = sb("f_ctraw", [P, 2, KD, C])
        cx = sb("cx", [C, 2, 2, D], FR)
        cxT = sb("cxT", [P, 2, 2, KD, CP], FR)
        xn = sb("f_xn", [P, TB, D])
        xT = sb("f_xT", [P, 2, TB, KD, P], FR)
        pr = sb("pr", [P, TB, C])
        prT = sb("prT", [C, 2, TB, P], FR)
        x3 = sb("x3", [P, TB, D])
        xq = sb("xq", [P, TB, D])
        xd = sb("xd", [P, TB, D])
        st = sb("f_st", [P, 2, TB, 6])
        mv = sb("f_mv", [P, 2, TB, 2])
        ve = sb("f_ve", [P, 2, TB])
        rs = sb("f_rs", [P, 2, TB])
        nmr = sb("nmr", [P, 2, TB])
        nm = sb("nm", [P, TB])
        su = sb("su", [P, TB])
        ri = sb("f_ri", [P, TB])
        rt = sb("rt", [P, TB])
        am = sb("am", [P, TB])
        ami = sb("ami", [P, TB])
        sc = sb("sc", [P, TB])
        dq = sb("dq", [P, TB])
        half = sb("f_half", [P, TB])
        eps = sb("f_eps", [P, TB])
        t_ps = psum("f_t_ps", [P, 2, KD, P])
        s_ps = psum("f_s_ps", [P, TB, P])
        p_ps = psum("f_p_ps", [P, TB, P])
        o_ps = psum("f_o_ps", [P, 2, D])

        ld_in = [sem("ld_in0"), sem("ld_in1")]
        y_in = [sem("y_in0"), sem("y_in1")]
        consts = sem("f_consts")
        ycol_done = sem("ycol_done")
        gcol_done = sem("gcol_done")
        fw_in = sem("fw_in")
        cwr_in = sem("cwr_in")
        comb = sem("comb")
        st_done = sem("f_st_done")
        mv1_done = sem("f_mv1_done")
        mv2_done = sem("f_mv2_done")
        ve_done = sem("f_ve_done")
        rs1_done = sem("f_rs1_done")
        rs2_done = sem("f_rs2_done")
        nmr1_done = sem("nmr1_done")
        nmr2_done = sem("nmr2_done")
        xn_done = sem("f_xn_done")
        c_hi = sem("c_hi")
        c_lo = sem("c_lo")
        padded = sem("padded")
        t_full = sem("f_t_full")
        t_hi = sem("f_t_hi")
        t_lo = sem("f_t_lo")
        s_full = sem("f_s_full")
        nm_done = sem("nm_done")
        e_done = sem("f_e_done")
        p_full = sem("p_full")
        p_hi = sem("p_hi")
        p_lo = sem("p_lo")
        ri_done = sem("f_ri_done")
        rt_done = sem("rt_done")
        o_full = sem("o_full")
        x3_done = sem("x3_done")
        x4_done = sem("x4_done")
        am_done = sem("am_done")
        amc_done = sem("amc_done")
        ami_done = sem("ami_done")
        sc_done = sem("sc_done")
        q_done = sem("q_done")
        xd_done = sem("xd_done")
        x3_out = sem("x3_out")
        xd_out = sem("xd_out")

        def whole(eng, run):
            run(-1, False, True)
            run(0, True, True)
            with eng.Fori(1, B // 2) as i:
                run(i * 2 - 1, True, True, 1)
                run(i * 2, True, True, 0)
            run(B - 1, True, False)

        def half_of(s, par):
            return (s + 1) // 2

        assert B % 2 == 0 and B >= 4
        block = ctx.enter_context(nc.Block())

        @block.sync
        def _(sp):
            def load_x(b, par):
                sp.dma_start(x1[:, par], n.tile_rows(n.x2_d, b * TB, TB)).then_inc(ld_in[par], 16)

            def load(b, par):
                sp.dma_start(craw[:, par], n.ctx[ds(b, 1)].rearrange("o c d -> c (o d)")).then_inc(ld_in[par], 16)
                sp.dma_start(ctraw[:, par], n.ctxT[:, :, ds(b * C, C)]).then_inc(ld_in[par], 16)

            def run(s, mid, front, par=None):
                par = s % 2 if par is None else par
                if isinstance(s, int) and s < 0:
                    for b in range(2):
                        load(b, b)
                        load_x(b, b)
                    sp.dma_start(cwr[:], n.conv_w).then_inc(cwr_in, 16)
                    sp.dma_start(n.cb[:], n.conv_b).then_inc(cwr_in, 16)
                    return
                if not (isinstance(s, int) and s >= B - 2):
                    sp.wait_ge(c_lo, (s + 1) * 2)
                    load(s + 2, par)
                if mid:
                    sp.wait_ge(x3_done, (s + 1) * TB)
                    sp.dma_start(n.tile_rows(n.x3_d, s * TB, TB), x3[:]).then_inc(x3_out, 16)
                    if not (isinstance(s, int) and s >= B - 2):
                        load_x(s + 2, par)
                    sp.wait_ge(xd_done, (s + 1) * TB)
                    sp.dma_start(n.tile_rows(n.xd_d, s * TB, TB), xd[:]).then_inc(xd_out, 16)

            def whole_sp():
                run(-1, False, True)
                run(0, True, True)
                if B > 4:
                    with sp.Fori(1, B // 2 - 1) as i:
                        run(i * 2 - 1, True, True, 1)
                        run(i * 2, True, True, 0)
                for s in range(B - 3, B):
                    run(s, True, True)

            whole_sp()
            sp.wait_ge(x3_out, B * 16)
            sp.wait_ge(xd_out, B * 16)

        @block.gpsimd
        def _(pool):
            def gather(b, par):
                pool.tensor_copy(ycol[:, par], slot[:, :, ds(b * TB, TB)]).then_inc(ycol_done, 1)
                hold(pool, ycol_done, b + 1, n.passed_pool)
                for i, y in enumerate((y1, y2)):
                    for j in range(TB):
                        pool.indirect_dma_start(out=y[:, par, j], out_offset=None, in_=n.ys_d[:, :],
                                                in_offset=bass.IndirectOffsetOnAxis(ap=ycol[:, par, i, j:j + 1], axis=0)
                                                ).then_inc(y_in[par], 16)

            def rstd(which, mv_sem, count, out_sem, ve_count):
                pool.wait_ge(mv_sem, count)
                pool.tensor_tensor(ve[:, which], mv[:, which, :, 1], eps[:], ALU.add).then_inc(ve_done, 1)
                pool.wait_ge(ve_done, ve_count)
                pool.tensor_tensor(rs[:, which], ve[:, which], half[:], ALU.pow).then_inc(out_sem, 1)

            def run(s, mid, front, par=None):
                par = s % 2 if par is None else par
                if mid and gathers(s):
                    hold(pool, comb, (s + 1) * 2 * TB, n.passed_pool)
                    gather(s + 2, par)
                if mid:
                    rstd(1, mv2_done, (s + 1) * TB, rs2_done, s * 2 + 2)
                if front:
                    rstd(0, mv1_done, (s + 2) * TB, rs1_done, s * 2 + 3)

            def gathers(s):
                return not isinstance(s, int) or s < B - 2

            pool.memset(half[:], -0.5)
            pool.memset(eps[:], EPS_LN)
            pool.memset(cxT[:].bitcast(F32), 0.0).then_inc(padded, 1)
            gather(0, 0)
            gather(1, 1)
            pool.dma_start(n.w1q[:].rearrange("p k f -> p (k f)"), n.w1q_d[:, :]).then_inc(fw_in, 16)
            pool.dma_start(n.w2q[:].rearrange("p k f -> p (k f)"), n.w2q_d[:, :]).then_inc(fw_in, 16)
            pool.wait_ge(cwr_in, 32)
            pool.tensor_scalar(n.cw[:], cwr[:], n.mean[:, 0:1], None, ALU.mult)
            pool.tensor_scalar(n.g2[:], n.mean[:, 1:2], tg[:, 3:4], 1.0 / 127.0, ALU.mult, ALU.mult)
            run(-1, False, True)
            run(0, True, True)
            if B > 4:
                with pool.Fori(1, B // 2 - 1) as i:
                    run(i * 2 - 1, True, True, 1)
                    run(i * 2, True, True, 0)
            for s in range(B - 3, B):
                run(s, True, s < B - 1)
            pool.wait_ge(fw_in, 32)

        @block.scalar
        def _(act):
            def run(s, mid, front, par=None):
                par = s % 2 if par is None else par
                if mid:
                    for j in range(TB):
                        act.wait_ge(t_full, s * TB + j + 1)
                        act.activation(xT[:, 0, j], t_ps[:, j % 2], ACT.Copy).then_inc(t_hi, 1)
                    act.wait_ge(nm_done, s + 1)
                    for j in range(TB):
                        act.activation(pr[:, j], s_ps[:, j, 0:C], ACT.Exp, bias=nm[:, j:j + 1],
                                       accum_out=su[:, j:j + 1]).then_inc(e_done, 1)
                    act.wait_ge(p_full, s + 1)
                    act.activation(prT[:, 0], p_ps[0:C], ACT.Copy).then_inc(p_hi, 1)
                if front:
                    o = 1 - par
                    act.wait_ge(ld_in[o], half_of(s, par) * 48 + 48)
                    act.wait_ge(padded, 1)
                    act.activation(cx[:, o, 0], craw[:, o], ACT.Copy).then_inc(c_hi, 1)
                    act.activation(cxT[:, o, 0, :, 0:C], ctraw[:, o], ACT.Copy).then_inc(c_hi, 1)
                if mid:
                    act.wait_ge(nmr2_done, s + 1)
                    for j in range(TB):
                        act.activation(xq[:, j], x3[:, j], ACT.Identity, bias=nmr[:, 1, j:j + 1],
                                       scale=rs[:, 1, j:j + 1]).then_inc(x4_done, 1)
                if front:
                    act.wait_ge(nmr1_done, s + 2)
                    for j in range(TB):
                        act.activation(xn[:, j], x1[:, 1 - par, j], ACT.Identity, bias=nmr[:, 0, j:j + 1],
                                       scale=rs[:, 0, j:j + 1]).then_inc(xn_done, 1)
                if mid:
                    act.wait_ge(sc_done, s + 1)
                    for j in range(TB):
                        act.activation(xq[:, j], xq[:, j], ACT.Copy, bias=MAGIC, scale=sc[:, j:j + 1]).then_inc(q_done, 1)

            whole(act, run)

        @block.vector
        def _(dve):
            def stats(which, src, mv_sem, base):
                for j in range(TB):
                    dve.bn_stats(st[:, which, j], src[:, j]).then_inc(st_done, 1)
                for j in range(TB):
                    hold(dve, st_done, base + j + 1, n.passed_dve)
                    dve.bn_aggr(mv[:, which, j], st[:, which, j]).then_inc(mv_sem, 1)

            def combine(s, o, tiles, first):
                b = s + 1
                k = b * 2 * TB + (0 if first else 2 * len(tiles))
                for j in tiles:
                    dve.scalar_tensor_tensor(out=y1[:, o, j], in0=y1[:, o, j], scalar=gcol[:, o, 0, j:j + 1],
                                             in1=x1[:, o, j], op0=ALU.mult, op1=ALU.add).then_inc(comb, 1)
                for i, j in enumerate(tiles):
                    dve.wait_ge(comb, k + i + 1)
                    dve.scalar_tensor_tensor(out=x1[:, o, j], in0=y2[:, o, j], scalar=gcol[:, o, 1, j:j + 1],
                                             in1=y1[:, o, j], op0=ALU.mult, op1=ALU.add).then_inc(comb, 1)

            def run(s, mid, front, par=None):
                par = s % 2 if par is None else par
                o = 1 - par
                if mid:
                    for j in range(TB):
                        dve.wait_ge(t_hi, s * TB + j + 1)
                        dve.tensor_tensor(xT[:, 1, j], t_ps[:, j % 2], xT[:, 0, j].bitcast(F32), ALU.subtract).then_inc(t_lo, 1)
                if front:
                    dve.tensor_copy(gcol[:, o], gate[:, :, ds((s + 1) * TB, TB)]).then_inc(gcol_done, 1)
                    dve.wait_ge(gcol_done, s + 2)
                    dve.wait_ge(y_in[o], half_of(s, par) * 32 * TB + 32 * TB)
                    dve.wait_ge(ld_in[o], half_of(s, par) * 48 + 48)
                    combine(s, o, range(0, TB // 2), True)
                if mid:
                    dve.wait_ge(s_full, s + 1)
                    dve.tensor_reduce(nm[:], s_ps[:, :, 0:C], AX.X, ALU.max, negate=True).then_inc(nm_done, 1)
                if front:
                    combine(s, o, range(TB // 2, TB), False)
                if mid:
                    dve.wait_ge(e_done, s * TB + TB)
                    dve.reciprocal(ri[:], su[:]).then_inc(ri_done, 1)
                    dve.wait_ge(ri_done, s + 1)
                    dve.tensor_scalar(rt[:], ri[:], tg[:, 1:2], None, ALU.mult).then_inc(rt_done, 1)
                    dve.wait_ge(p_hi, s + 1)
                    dve.tensor_tensor(prT[:, 1], p_ps[0:C], prT[:, 0].bitcast(F32), ALU.subtract).then_inc(p_lo, 1)
                if front:
                    dve.wait_ge(c_hi, s * 2 + 3)
                    dve.tensor_tensor(cx[:, o, 1], craw[:, o], cx[:, o, 0].bitcast(F32), ALU.subtract).then_inc(c_lo, 1)
                    dve.wait_ge(c_hi, s * 2 + 4)
                    dve.tensor_tensor(cxT[:, o, 1, :, 0:C], ctraw[:, o], cxT[:, o, 0, :, 0:C].bitcast(F32),
                                      ALU.subtract).then_inc(c_lo, 1)
                if mid:
                    dve.wait_ge(rt_done, s + 1)
                    if not (isinstance(s, int) and s == 0):
                        dve.wait_ge(x3_out, s * 16)
                    for j in range(TB):
                        dve.wait_ge(o_full, s * TB + j + 1)
                        dve.scalar_tensor_tensor(out=x3[:, j], in0=o_ps[:, j % 2], scalar=rt[:, j:j + 1], in1=x1[:, par, j],
                                                 op0=ALU.mult, op1=ALU.add).then_inc(x3_done, 1)
                    dve.wait_ge(x3_done, s * TB + TB)
                    stats(1, x3, mv2_done, s * 2 * TB + TB)
                if front:
                    dve.wait_ge(comb, (s + 2) * 2 * TB)
                    stats(0, x1[:, o], mv1_done, (s + 1) * 2 * TB)
                if mid:
                    dve.wait_ge(rs2_done, s + 1)
                    dve.scalar_tensor_tensor(out=nmr[:, 1], in0=mv[:, 1, :, 0], scalar=-1.0, in1=rs[:, 1], op0=ALU.mult,
                                             op1=ALU.mult).then_inc(nmr2_done, 1)
                if front:
                    dve.wait_ge(rs1_done, s + 2)
                    dve.scalar_tensor_tensor(out=nmr[:, 0], in0=mv[:, 0, :, 0], scalar=-1.0, in1=rs[:, 0], op0=ALU.mult,
                                             op1=ALU.mult).then_inc(nmr1_done, 1)
                if mid:
                    for j in range(TB):
                        dve.wait_ge(x4_done, s * TB + j + 1)
                        dve.tensor_reduce(am[:, j:j + 1], xq[:, j], AX.X, ALU.max, apply_absolute_value=True).then_inc(am_done, 1)
                    dve.wait_ge(am_done, s * TB + TB)
                    dve.tensor_scalar(am[:], am[:], EPS_Q, None, ALU.max).then_inc(amc_done, 1)
                    dve.wait_ge(amc_done, s + 1)
                    dve.reciprocal(ami[:], am[:]).then_inc(ami_done, 1)
                    dve.tensor_scalar(dq[:], am[:], 1.0 / 127.0, None, ALU.mult)
                    dve.wait_ge(ami_done, s + 1)
                    dve.tensor_scalar(sc[:], ami[:], 127.0, None, ALU.mult).then_inc(sc_done, 1)
                    if not (isinstance(s, int) and s == 0):
                        dve.wait_ge(xd_out, s * 16)
                    for j in range(TB):
                        dve.wait_ge(q_done, s * TB + j + 1)
                        dve.tensor_scalar(xd[:, j], xq[:, j], MAGIC, dq[:, j:j + 1], ALU.subtract, ALU.mult).then_inc(xd_done, 1)

            whole(dve, run)

        @block.tensor
        def _(pe):
            def run(s, mid, front, par=None):
                par = s % 2 if par is None else par
                if not mid:
                    return
                for j in range(TB):
                    pe.wait_ge(xn_done, s * TB + j + 1)
                    if not (isinstance(s, int) and s * TB + j < 2):
                        pe.wait_ge(t_lo, s * TB + j - 1)
                    for k in range(KD):
                        mm = pe.transpose(t_ps[:, j % 2, k], xn[:, j, k * P:(k + 1) * P], ident[:])
                    mm.then_inc(t_full, 1)
                pe.wait_ge(t_lo, s * TB + TB)
                pe.wait_ge(c_lo, s * 2 + 2)
                for j in range(TB):
                    for k in range(KD):
                        for pa, pb in PASSES:
                            mm = pe.matmul(s_ps[:, j, 0:CP], xT[:, pa, j, k], cxT[:, par, pb, k],
                                           start=(k == 0 and (pa, pb) == PASSES[0]),
                                           stop=(k == KD - 1 and (pa, pb) == PASSES[-1]))
                mm.then_inc(s_full, 1)
                pe.wait_ge(e_done, s * TB + TB)
                for j in range(TB):
                    mm = pe.transpose(p_ps[0:C, j], pr[:, j], ident[:])
                mm.then_inc(p_full, 1)
                pe.wait_ge(p_lo, s + 1)
                for j in range(TB):
                    if not (isinstance(s, int) and s * TB + j < 2):
                        pe.wait_ge(x3_done, s * TB + j - 1)
                    for pa, pb in PASSES:
                        mm = pe.matmul(o_ps[:, j % 2], prT[:, pa, j], cx[:, par, pb], start=((pa, pb) == PASSES[0]),
                                       stop=((pa, pb) == PASSES[-1]))
                    mm.then_inc(o_full, 1)

            whole(pe, run)


def ffn(nc, n):
    B, S, D, KD, NT, TB, DH, KF = n.B, n.S, n.D, n.KD, n.NT, n.TB, n.DH, n.KF
    ident, w1q, w2q, cw, cb, g2 = n.ident, n.w1q, n.w2q, n.cw, n.cb, n.g2
    RING = 4

    with ExitStack() as ctx:
        def sb(name, shape, dt=F32, c=ctx):
            return c.enter_context(nc.sbuf_tensor("b_" + name, shape, dt))

        def sem(name, c=ctx):
            return c.enter_context(nc.semaphore("b_" + name))

        xd = sb("xd", [P, TB, D])
        xdT = sb("xdT", [P, 2, KD, TB, P], FR)
        av = sb("av", [P, RING, S])
        h = sb("h", [P, 2, KF, S])
        hq = sb("hq", [P, KF, S], BF16)
        am = sb("am", [P, S])
        mx = sb("mx", [P, TB])
        mxc = sb("mxc", [P, TB])
        mi = sb("mi", [P, TB])
        s2 = sb("s2", [P, TB])
        d2 = sb("d2", [P, 2, TB])
        srow = sb("srow", [P, S])
        x3 = sb("x3", [P, 2, TB, D])
        f_ps = ctx.enter_context(nc.psum_tensor("b_f_ps", [P, RING, 512], F32))
        q_ps = ctx.enter_context(nc.psum_tensor("b_q_ps", [P, TB, P], F32))
        o_ps = ctx.enter_context(nc.psum_tensor("b_o_ps", [P, 2, D], F32))

        xd_in = sem("xd_in")
        x3_in = [sem("x3_in0"), sem("x3_in1")]
        t_full = sem("t_full")
        t_hi = sem("t_hi")
        t_lo = sem("t_lo")
        f_full = sem("f_full")
        mid_tap = sem("mid_tap")
        prev_tap = sem("prev_tap")
        conv_done = sem("conv_done")
        h_done = sem("h_done")
        am_done = sem("am_done")
        amt_full = sem("amt_full")
        scale_steps = sem("scale_steps")
        row_full = sem("row_full")
        row_done = sem("row_done")
        u_done = sem("u_done")
        hq_done = sem("hq_done")
        o_full = sem("o_full")
        o_done = sem("o_done")
        out_done = sem("out_done")

        def whole(run):
            def steps(eng):
                run(-1, False, False, False, True, 1)
                run(0, True, False, False, True, 0)
                run(1, True, True, False, True, 1)
                run(2, True, True, True, True, 0)
                run(3, True, True, True, B > 4, 1)
                if B > 4:
                    with eng.Fori(2, B // 2 - 1) as i:
                        run(i * 2, True, True, True, True, 0)
                        run(i * 2 + 1, True, True, True, True, 1)
                    run(B - 2, True, True, True, True, 0)
                    run(B - 1, True, True, True, False, 1)
                run(B, False, True, True, False, 0)
                run(B + 1, False, False, True, False, 1)
            return steps

        def transposed(j):
            return f_ps[:, j].rearrange("p (k t) -> p k t", t=P)

        assert B % 2 == 0 and B >= 4 and KF == 16 and TB == RING
        rounds = {6: (0,), 7: (1,), 8: (2,), 9: (3, 4), 10: (5,), 11: (6, 7), 12: (8,), 13: (9, 10), 14: (11, 12),
                  15: (13,), 16: (14, 15)}
        block = ctx.enter_context(nc.Block())

        @block.sync
        def _(sp):
            def run(s, f1, quant, f2, front, par):
                if front:
                    if not (isinstance(s, int) and s < 0):
                        sp.wait_ge(t_full, (s + 1) * TB)
                    sp.dma_start(xd[:], n.tile_rows(n.xd_d, (s + 1) * TB, TB)).then_inc(xd_in, 16)
                if quant:
                    if not (isinstance(s, int) and s < 3):
                        sp.wait_ge(out_done, (s - 2) * 16)
                    sp.dma_start(x3[:, 1 - par], n.tile_rows(n.x3_d, (s - 1) * TB, TB)).then_inc(x3_in[1 - par], 16)
                if f2:
                    sp.wait_ge(o_done, (s - 1) * TB)
                    sp.dma_start(n.tile_rows(n.out, (s - 2) * TB, TB), x3[:, par]).then_inc(out_done, 16)

            whole(run)(sp)
            sp.wait_ge(out_done, B * 16)

        @block.gpsimd
        def _(pool):
            def run(s, f1, quant, f2, front, par):
                if not quant:
                    return
                for m in range(KF):
                    if m == 0:
                        pool.wait_ge(row_done, s)
                    pool.tensor_tensor(h[:, 1 - par, m], h[:, 1 - par, m], srow[:], ALU.mult).then_inc(u_done, 1)

            whole(run)(pool)

        @block.scalar
        def _(act):
            def run(s, f1, quant, f2, front, par):
                def silu(m):
                    act.wait_ge(conv_done, s * KF + m + 1)
                    if not (isinstance(s, int) and s < 2):
                        act.wait_ge(hq_done, (s - 2) * KF + m + 1)
                    act.activation(h[:, par, m], av[:, m % RING], ACT.Silu).then_inc(h_done, 1)

                for m in range(KF):
                    if f1:
                        act.wait_ge(f_full, s * KF + m + 1)
                        if m >= RING or not (isinstance(s, int) and s == 0):
                            act.wait_ge(h_done, s * KF + m + 1 - RING)
                        act.activation(av[:, m % RING], f_ps[:, m % RING], ACT.Identity, bias=cb[:, m:m + 1],
                                       scale=cw[:, m, 1:2]).then_inc(mid_tap, 1)
                        if m >= 1:
                            silu(m - 1)
                    if quant and m == 5:
                        act.wait_ge(row_full, s)
                        if not (isinstance(s, int) and s == 1):
                            act.wait_ge(u_done, (s - 1) * KF)
                        act.activation(srow[:], q_ps[:], ACT.Copy).then_inc(row_done, 1)
                if f1:
                    silu(KF - 1)
                if front:
                    for j in range(TB):
                        act.wait_ge(t_full, (s + 1) * TB + j + 1)
                        act.activation(xdT[:, 0, :, j], transposed(j), ACT.Copy).then_inc(t_hi, 1)

            whole(run)(act)

        @block.vector
        def _(dve):
            def run(s, f1, quant, f2, front, par):
                def outputs(j):
                    dve.wait_ge(o_full, (s - 2) * TB + j + 1)
                    dve.wait_ge(x3_in[par], s // 2 * 16)
                    dve.scalar_tensor_tensor(out=x3[:, par, j], in0=o_ps[:, j % 2], scalar=d2[:, par, j:j + 1],
                                             in1=x3[:, par, j], op0=ALU.mult, op1=ALU.add).then_inc(o_done, 1)

                def round_tile(m):
                    dve.wait_ge(u_done, (s - 1) * KF + m + 1)
                    if m == 0 and not (isinstance(s, int) and s == 1):
                        dve.wait_ge(o_full, (s - 1) * TB)
                    dve.tensor_scalar(hq[:, m], h[:, 1 - par, m], MAGIC, MAGIC, ALU.add, ALU.subtract).then_inc(hq_done, 1)

                if quant:
                    dve.wait_ge(h_done, s * KF)
                    dve.tensor_reduce(am[:], h[:, 1 - par].rearrange("p m t -> p t m"), AX.X, ALU.max,
                                      apply_absolute_value=True).then_inc(am_done, 1)
                if f2:
                    outputs(0)
                    outputs(1)
                for m in range(KF + 1):
                    if f1 and m < KF:
                        u = s * KF + m + 1
                        dve.wait_ge(mid_tap, u)
                        a, f = av[:, m % RING], f_ps[:, m % RING]
                        dve.scalar_tensor_tensor(out=a[:, 1:S], in0=f[:, 0:S - 1], scalar=cw[:, m, 0:1], in1=a[:, 1:S],
                                                 op0=ALU.mult, op1=ALU.add).then_inc(prev_tap, 1)
                        dve.wait_ge(prev_tap, u)
                        dve.scalar_tensor_tensor(out=a[:, 0:S - 1], in0=f[:, 1:S], scalar=cw[:, m, 2:3], in1=a[:, 0:S - 1],
                                                 op0=ALU.mult, op1=ALU.add).then_inc(conv_done, 1)
                    if f2 and m in (1, 3):
                        outputs(2 + m // 2)
                    if quant and m == 2:
                        dve.wait_ge(amt_full, s)
                        dve.tensor_reduce(mx[:], q_ps[:], AX.X, ALU.max).then_inc(scale_steps, 1)
                        dve.wait_ge(scale_steps, s * 4 - 3)
                        dve.tensor_scalar(mxc[:], mx[:], EPS_Q, None, ALU.max).then_inc(scale_steps, 1)
                        dve.wait_ge(scale_steps, s * 4 - 2)
                        dve.reciprocal(mi[:], mxc[:]).then_inc(scale_steps, 1)
                        dve.tensor_scalar(d2[:, 1 - par], mxc[:], g2[:], None, ALU.mult)
                        dve.wait_ge(scale_steps, s * 4 - 1)
                        dve.tensor_scalar(s2[:], mi[:], 127.0, None, ALU.mult).then_inc(scale_steps, 1)
                    if m == KF and front:
                        transposed_low(s + 1)
                    if quant:
                        for r in rounds.get(m, ()):
                            round_tile(r)

            def transposed_low(b):
                for j in range(TB):
                    dve.wait_ge(t_hi, b * TB + j + 1)
                    dve.tensor_tensor(xdT[:, 1, :, j], transposed(j), xdT[:, 0, :, j].bitcast(F32),
                                      ALU.subtract).then_inc(t_lo, 1)

            whole(run)(dve)

        @block.tensor
        def _(pe):
            def run(s, f1, quant, f2, front, par):
                def down(j):
                    u = (s - 2) * TB + j
                    if j == 0:
                        pe.wait_ge(hq_done, (s - 1) * KF)
                    if not (isinstance(s, int) and s == 2 and j < 2):
                        pe.wait_ge(o_done, u - 1)
                    for k in range(KF):
                        mm = pe.matmul(o_ps[:, j % 2], hq[:, k, j * P:(j + 1) * P], w2q[:, k, :], start=(k == 0),
                                       stop=(k == KF - 1))
                    mm.then_inc(o_full, 1)

                if f2:
                    down(0)
                    down(1)
                for m in range(KF):
                    if f1:
                        if m == 0:
                            pe.wait_ge(t_lo, (s + 1) * TB)
                        if m >= RING:
                            pe.wait_ge(conv_done, s * KF + m + 1 - RING)
                        for k in range(KD):
                            for part in range(2):
                                mm = pe.matmul(f_ps[:, m % RING], w1q[:, k, m * P:(m + 1) * P], xdT[:, part, k],
                                               start=(k == 0 and part == 0), stop=(k == KD - 1 and part == 1))
                        mm.then_inc(f_full, 1)
                    if f2 and m in (1, 3):
                        down(2 + m // 2)
                    if quant and m == 2:
                        pe.wait_ge(am_done, s)
                        if not (isinstance(s, int) and s == 1):
                            pe.wait_ge(row_done, s - 1)
                        for j in range(TB):
                            mm = pe.transpose(q_ps[:, j], am[:, j * P:(j + 1) * P], ident[:])
                        mm.then_inc(amt_full, 1)
                    if quant and m == 4:
                        pe.wait_ge(scale_steps, s * 4)
                        for j in range(TB):
                            mm = pe.matmul(q_ps[:, j], s2[:, j:j + 1].to_broadcast([P, P]), ident[:], start=True, stop=True)
                        mm.then_inc(row_full, 1)
                if front:
                    pe.wait_ge(xd_in, (s + 2) * 16)
                    for j in range(TB):
                        if f1:
                            pe.wait_ge(conv_done, (s + 1) * KF - RING + j + 1)
                        for k in range(KD):
                            mm = pe.transpose(f_ps[:, j, k * P:(k + 1) * P], xd[:, j, k * P:(k + 1) * P], ident[:])
                        mm.then_inc(t_full, 1)

            whole(run)(pe)


def kernel(x, ctx_1024, g_xattn, g_ffn, L0_xattn_Wq, L0_xattn_bq, L0_xattn_Wk, L0_xattn_bk, L0_xattn_Wv,
           L0_xattn_bv, L0_xattn_Wo, L0_xattn_bo, L0_ffn_router_w, L0_ffn_router_b, L0_ffn_routed_w1,
           L0_ffn_routed_w3, L0_ffn_routed_w2, L0_ffn_shared_w1, L0_ffn_shared_w3, L0_ffn_shared_w2,
           L1_ffn_w1, L1_ffn_conv_w, L1_ffn_conv_b, L1_ffn_w2):
    import numpy as np
    import concourse.bacc as bacc
    from concourse.bass_utils import run_bass_kernel_spmd

    def rows(w):
        w = np.asarray(w)
        return np.swapaxes(w.reshape(*w.shape[:-2], w.shape[-2] // P, P, w.shape[-1]), -3, -2)

    def columns(v):
        return np.asarray(v).reshape(-1, P).T

    x, c = np.asarray(x), np.asarray(ctx_1024)
    B, S, D = x.shape
    w13 = np.concatenate([np.concatenate([L0_ffn_shared_w1, L0_ffn_shared_w3], -1),
                          np.concatenate([L0_ffn_routed_w1, L0_ffn_routed_w3], -1)])
    w2 = np.concatenate([L0_ffn_shared_w2, L0_ffn_routed_w2])
    w1 = np.asarray(L1_ffn_w1)
    ins = {
        "x": x.reshape(B * S, D),
        "ctx": c,
        "ctxT": rows(c.reshape(-1, D).T),
        "gates": np.concatenate([g_xattn, g_ffn]),
        "wqT": rows(np.asarray(L0_xattn_Wq).T),
        "wkT": rows(np.asarray(L0_xattn_Wk).T),
        "wvT": rows(np.asarray(L0_xattn_Wv).T),
        "woT": rows(np.asarray(L0_xattn_Wo).T),
        "bq": columns(L0_xattn_bq),
        "bk": columns(L0_xattn_bk),
        "bv": np.asarray(L0_xattn_bv),
        "bo": np.asarray(L0_xattn_bo),
        "router_w": rows(L0_ffn_router_w),
        "router_b": np.asarray(L0_ffn_router_b),
        "w13": rows(w13),
        "w2e": rows(w2),
        "w1T": rows(w1.T),
        "conv_w": np.asarray(L1_ffn_conv_w).reshape(-1, P, 3).swapaxes(0, 1),
        "conv_b": columns(L1_ffn_conv_b),
        "w2T": rows(np.asarray(L1_ffn_w2).T),
    }
    nc = bacc.Bacc("TRN2", target_bir_lowering=False, num_devices=1)
    arrays, aps = {}, {}
    for name, a in ins.items():
        a = np.ascontiguousarray(a)
        arrays[f"in_{name}"] = a
        aps[name] = nc.dram_tensor(f"in_{name}", a.shape, mybir.dt.from_np(a.dtype), kind="ExternalInput").ap()
    out = nc.dram_tensor("out", (B * S, D), F32, kind="ExternalOutput").ap()
    flamingo(nc, **aps, out=out)
    r = run_bass_kernel_spmd(nc, [arrays], core_ids=[0])
    return r.results[0]["out"].reshape(B, S, D)
```

```python
from contextlib import ExitStack

import concourse.bass as bass
from concourse import mybir

F32 = mybir.dt.float32
FR = mybir.dt.float32r
BF16 = mybir.dt.bfloat16
I32 = mybir.dt.int32
U32 = mybir.dt.uint32
ALU = mybir.AluOpType
ACT = mybir.ActivationFunctionType
AX = mybir.AxisListType
ds = bass.ds

P = 128
MAGIC = 12582912.0
PASSES = ((0, 0), (0, 1), (1, 0))
EPS_LN = 1e-5
EPS_Q = 1e-5


class Program:
    pass


def flamingo(nc, x, ctx, ctxT, gates, wqT, wkT, wvT, woT, bq, bk, bv, bo, router_w, router_b,
             w13, w2e, w1T, conv_w, conv_b, w2T, out):
    B, C, D = ctx.shape
    T = x.shape[0]
    S = T // B
    KD = D // P
    NT = T // P
    TB = S // P
    HD = 32
    H = D // HD
    HG = P // HD
    NG = H // HG
    E = router_w.shape[2]
    NE = w13.shape[0]
    NSH = NE - E
    HID = w13.shape[3] // 2
    KH = HID // P
    MIN_TILES = 3
    MAXT = 2 * NT + MIN_TILES * E
    DH = w1T.shape[2]
    KF = DH // P
    SCALE = float(HD) ** -0.5

    x1_d = nc.dram_tensor("x1_scratch", [T, D], F32)
    xn2_d = nc.dram_tensor("xn2_scratch", [T, D], F32)
    xs_d = nc.dram_tensor("slots_in_scratch", [MAXT * P, D], F32)
    ys_d = nc.dram_tensor("experts_out_scratch", [MAXT * P, D], F32)
    x2_d = nc.dram_tensor("x2_scratch", [T, D], F32)
    w1q_d = nc.dram_tensor("w1q_scratch", [P, KD * DH], BF16)
    w2q_d = nc.dram_tensor("w2q_scratch", [P, KF * D], BF16)
    x3_d = nc.dram_tensor("x3_scratch", [T, D], F32)
    xd_d = nc.dram_tensor("xd_scratch", [T, D], F32)

    def tile_rows(t, first, n=1):
        if n == 1:
            return t[ds(first * P, P), :]
        return t[ds(first * P, n * P), :].rearrange("(n p) d -> p n d", p=P)

    with ExitStack() as top:
        def keep(name, shape, dt):
            return top.enter_context(nc.sbuf_tensor(name, shape, dt))

        ident = keep("ident", [P, P], F32)
        tg = keep("tanh_gates", [P, 4], F32)
        logits = keep("logits", [P, NT, E], F32)
        gate = keep("gate", [P, 2, NT], F32)
        slot = keep("slot", [P, 2, NT], U32)
        mean = keep("mean", [P, 2], F32)

        passed_dve = top.enter_context(nc.semaphore("passed_dve"))
        passed_pool = top.enter_context(nc.semaphore("passed_pool"))

        n = Program()
        n.B = B
        n.C = C
        n.D = D
        n.DH = DH
        n.E = E
        n.H = H
        n.HD = HD
        n.HG = HG
        n.HID = HID
        n.KD = KD
        n.KF = KF
        n.KH = KH
        n.MAXT = MAXT
        n.MIN_TILES = MIN_TILES
        n.NE = NE
        n.NG = NG
        n.NSH = NSH
        n.NT = NT
        n.S = S
        n.SCALE = SCALE
        n.T = T
        n.TB = TB
        n.bk = bk
        n.bo = bo
        n.bq = bq
        n.bv = bv
        n.conv_b = conv_b
        n.conv_w = conv_w
        n.ctx = ctx
        n.ctxT = ctxT
        n.gate = gate
        n.gates = gates
        n.ident = ident
        n.logits = logits
        n.out = out
        n.passed_dve = passed_dve
        n.passed_pool = passed_pool
        n.router_b = router_b
        n.router_w = router_w
        n.slot = slot
        n.mean = mean
        n.x2_d = x2_d
        n.w1q_d = w1q_d
        n.w2q_d = w2q_d
        n.tg = tg
        n.tile_rows = tile_rows
        n.w13 = w13
        n.w1T = w1T
        n.w2T = w2T
        n.w2e = w2e
        n.wkT = wkT
        n.woT = woT
        n.wqT = wqT
        n.wvT = wvT
        n.x = x
        n.x1_d = x1_d
        n.x3_d = x3_d
        n.xd_d = xd_d
        n.xn2_d = xn2_d
        n.xs_d = xs_d
        n.ys_d = ys_d

        attention(nc, n)
        experts(nc, n)

        n.w1q = keep("w1q", [P, KD, DH], FR)
        n.w2q = keep("w2q", [P, KF, D], BF16)
        n.cw = keep("cw", [P, KF, 3], F32)
        n.cb = keep("cb", [P, KF], F32)
        n.g2 = keep("g2", [P, 1], F32)
        fuse(nc, n)
        ffn(nc, n)


def hold(eng, sem, value, passed):
    eng.wait_ge(sem, value)
    eng.sem_inc(passed, 1)


def attention(nc, n):
    B, C, D, S, KD, NT, TB, HD, H, HG, NG, E = n.B, n.C, n.D, n.S, n.KD, n.NT, n.TB, n.HD, n.H, n.HG, n.NG, n.E
    ident, tg, logits = n.ident, n.tg, n.logits
    W2 = 2 * P
    NSTEP = n.T // W2
    GC = HG * C

    with ExitStack() as ctx:
        def sb(name, shape, dt, c=ctx):
            return c.enter_context(nc.sbuf_tensor(name, shape, dt))

        def sem(name, c=ctx):
            return c.enter_context(nc.semaphore(name))

        wq = sb("wq", [P, 2, KD, D], FR)
        wo = sb("wo", [P, 2, KD, D], FR)
        kc = sb("k_all", [P, B, NG, C], F32)
        vc = sb("v_all", [C, B, D], F32)
        kbd = sb("k_blocks", [P, 2, NG, GC], FR)
        vbd = sb("v_blocks", [C, 2, H, P], FR)
        bq_s = sb("bq_s", [P, NG], F32)
        bo_t = sb("bo_t", [P, D], F32)
        rw = sb("rw", [P, KD, E], F32)
        rb = sb("rb", [P, E], F32)
        half = sb("minus_half", [P, 2], F32)
        eps = sb("eps", [P, 2], F32)

        with ExitStack() as c1:
            wraw = sb("wraw", [P, 4, KD, D], F32, c1)
            wkv = sb("wkv", [P, 2, 2, KD, D], FR, c1)
            craw = sb("craw", [P, KD, B * C], F32, c1)
            cts = sb("cts", [P, 2, KD, B * C], FR, c1)
            bk_s = sb("bk_s", [P, NG], F32, c1)
            bv_s = sb("bv_s", [C, D], F32, c1)
            bo_s = sb("bo_s", [P, D], F32, c1)
            graw = sb("graw", [P, 4], F32, c1)
            kv_ps = [c1.enter_context(nc.psum_tensor(f"kv_ps{i}", [P, 512], F32)) for i in range(4)]
            ctx_in = sem("ctx_in", c1)
            small_in = sem("small_in", c1)
            w_in = [sem(f"w_in{i}", c1) for i in range(4)]
            hi_done = sem("hi_done", c1)
            lo_done = sem("lo_done", c1)
            cleared = sem("cleared", c1)
            tanh_done = sem("tanh_done", c1)
            kv_full = sem("kv_full", c1)
            kv_free = sem("kv_free", c1)
            block = c1.enter_context(nc.Block())
            srcs = [craw[:], wraw[:, 0], wraw[:, 1], wraw[:, 2], wraw[:, 3]]
            his = [cts[:, 0], wkv[:, 0, 0], wkv[:, 1, 0], wq[:, 0], wo[:, 0]]
            los = [cts[:, 1], wkv[:, 0, 1], wkv[:, 1, 1], wq[:, 1], wo[:, 1]]
            loaded = [(ctx_in, 16), (w_in[0], 16), (w_in[1], 16), (w_in[2], 16), (w_in[3], 16)]

            @block.sync
            def _(sp):
                sp.dma_start(craw[:], n.ctxT).then_inc(ctx_in, 16)
                for i, w in enumerate((n.wkT, n.wvT, n.wqT, n.woT)):
                    sp.dma_start(wraw[:, i], w).then_inc(w_in[i], 16)
                sp.dma_start(bq_s[:], n.bq).then_inc(small_in, 16)
                sp.dma_start(bk_s[:], n.bk).then_inc(small_in, 16)
                sp.dma_start(bv_s[:], n.bv.partition_broadcast(C)).then_inc(small_in, 16)
                sp.dma_start(bo_s[:], n.bo.partition_broadcast(P)).then_inc(small_in, 16)
                sp.dma_start(rb[:], n.router_b.partition_broadcast(P)).then_inc(small_in, 16)
                sp.dma_start(graw[:], n.gates.partition_broadcast(P)).then_inc(small_in, 16)
                sp.dma_start(rw[:], n.router_w).then_inc(small_in, 16)

            @block.gpsimd
            def _(pool):
                pool.memset(half[:], -0.5)
                pool.memset(eps[:], EPS_LN)
                pool.memset(kbd[:].bitcast(F32), 0.0)
                pool.memset(vbd[:].bitcast(F32), 0.0)
                pool.memset(ident[:], 0.0).then_inc(cleared, 1)
                pool.wait_ge(cleared, 1)
                pool.affine_select(out=ident[:], in_=ident[:], compare_op=ALU.not_equal, fill=1.0, base=0,
                                   pattern=[[-1, P]], channel_multiplier=1)

            @block.scalar
            def _(act):
                for s, h, (q, v) in zip(srcs, his, loaded):
                    act.wait_ge(q, v)
                    act.activation(h, s, ACT.Copy).then_inc(hi_done, 1)
                act.wait_ge(small_in, 112)
                act.activation(tg[:], graw[:], ACT.Tanh).then_inc(tanh_done, 1)

            @block.vector
            def _(dve):
                def lo(i):
                    dve.wait_ge(hi_done, i + 1)
                    dve.wait_ge(loaded[i][0], loaded[i][1])
                    dve.tensor_tensor(los[i], srcs[i], his[i].bitcast(F32), ALU.subtract).then_inc(lo_done, 1)

                for i in range(3):
                    lo(i)
                dve.wait_ge(small_in, 112)
                use = 0
                for half_b in range(2):
                    for m in range(NG):
                        dve.wait_ge(kv_full, use + 1)
                        bs = slice(half_b * B // 2, (half_b + 1) * B // 2)
                        dve.tensor_scalar(kc[:, bs, m, :],
                                          kv_ps[use % 4][:, 0:B // 2 * C].rearrange("p (b c) -> p b c", c=C),
                                          bk_s[:, m:m + 1], None, ALU.add).then_inc(kv_free, 1)
                        use += 1
                for b in range(B):
                    dve.wait_ge(kv_full, use + 1)
                    dve.tensor_tensor(vc[:, b], kv_ps[use % 4][0:C, :], bv_s[:], ALU.add).then_inc(kv_free, 1)
                    use += 1
                for i in range(3, 5):
                    lo(i)
                dve.wait_ge(tanh_done, 1)
                dve.tensor_scalar(bo_t[:], bo_s[:], tg[:, 0:1], None, ALU.mult)

            @block.tensor
            def _(pe):
                use = 0
                pe.wait_ge(lo_done, 2)
                N = B // 2 * C
                for half_b in range(2):
                    for m in range(NG):
                        if use >= 4:
                            pe.wait_ge(kv_free, use - 3)
                        for k in range(KD):
                            for pa, pb in PASSES:
                                mm = pe.matmul(kv_ps[use % 4][:, 0:N], wkv[:, 0, pa, k, m * P:(m + 1) * P],
                                               cts[:, pb, k, half_b * N:(half_b + 1) * N],
                                               start=(k == 0 and (pa, pb) == PASSES[0]),
                                               stop=(k == KD - 1 and (pa, pb) == PASSES[-1]))
                        mm.then_inc(kv_full, 1)
                        use += 1
                pe.wait_ge(lo_done, 3)
                for bb in range(B):
                    pe.wait_ge(kv_free, use - 3)
                    for k in range(KD):
                        for pa, pb in PASSES:
                            mm = pe.matmul(kv_ps[use % 4][0:C, :], cts[:, pa, k, bb * C:(bb + 1) * C],
                                           wkv[:, 1, pb, k, :],
                                           start=(k == 0 and (pa, pb) == PASSES[0]),
                                           stop=(k == KD - 1 and (pa, pb) == PASSES[-1]))
                    mm.then_inc(kv_full, 1)
                    use += 1

        xin = sb("xin", [P, 2, D], F32)
        xn = sb("xn", [P, 2, D], F32)
        xT = sb("xT", [P, 2, KD, W2], FR)
        qT = sb("qT", [P, 2, 2, NG, W2], FR)
        prob = sb("prob", [P, 2, H, C], F32)
        pT = sb("pT", [C, 2, H, W2], FR)
        oT = sb("oT", [P, 2, NG, W2], FR)
        xres = sb("xres", [P, 2, D], F32)
        x1 = sb("x1", [P, 2, D], F32)
        xn2 = sb("xn2", [P, 2, D], F32)
        x2T = sb("x2T", [P, KD, W2], F32)
        st1 = sb("st1", [P, 2, 6], F32)
        mv1 = sb("mv1", [P, 2, 2], F32)
        ve1 = sb("ve1", [P, 2], F32)
        rs1 = sb("rs1", [P, 2], F32)
        st2 = sb("st2", [P, 2, 6], F32)
        mv2 = sb("mv2", [P, 2, 2], F32)
        ve2 = sb("ve2", [P, 2], F32)
        rs2 = sb("rs2", [P, 2], F32)
        mx = sb("mx", [P, 2, H], F32)
        sm = sb("sm", [P, 2, H], F32)
        ri = sb("ri", [P, 2, H], F32)
        s_ps = ctx.enter_context(nc.psum_tensor("s_ps", [P, NG, 512], F32))
        t_ps = ctx.enter_context(nc.psum_tensor("t_ps", [P, 2, 512], F32))
        m_ps = ctx.enter_context(nc.psum_tensor("m_ps", [P, 2, 512], F32))

        x_in = sem("x_in")
        xres_in = sem("xres_in")
        mv1_done = sem("mv1_done")
        mv2_done = sem("mv2_done")
        st_done = sem("st_done")
        rs_tmp = sem("rs_tmp")
        rs1_done = sem("rs1_done")
        rs2_done = sem("rs2_done")
        xn_done = sem("xn_done")
        xb_done = sem("xb_done")
        t_full = sem("t_full")
        t_hi = sem("t_hi")
        t_free = sem("t_free")
        m_full = sem("m_full")
        m_hi = sem("m_hi")
        m_free = sem("m_free")
        s_full = sem("s_full")
        s_sub = sem("s_sub")
        mx_done = sem("mx_done")
        e_done = sem("e_done")
        sum_done = sem("sum_done")
        ri_done = sem("ri_done")
        p_done = sem("p_done")
        bd_hi = sem("bd_hi")
        k_bd = sem("k_bd")
        v_bd = sem("v_bd")
        xn2_done = sem("xn2_done")
        x1_out = sem("x1_out")
        xn2_out = sem("xn2_out")


        def whole(eng, run):
            run(-1, -1, False, False, True)
            run(0, 0, True, False, True)
            run(1, 0, True, True, True)
            if B > 2:
                with eng.Fori(1, B - 1) as b:
                    run(b * 2, b, True, True, True, 0)
                    run(b * 2 + 1, b, True, True, True, 1)
            run(NSTEP - 2, B - 1, True, True, True)
            run(NSTEP - 1, B - 1, True, True, False)
            run(NSTEP, B, False, True, False)

        def before(s, first, front, back):
            if isinstance(s, int):
                return max(0, min(s + 1, NSTEP)) * front + max(0, s) * first + max(0, s - 1) * back
            return s * (front + first + back) + (front - back)

        def t_base(s):
            return before(s, 2 * NG, 2, 2)

        def hi_base(s):
            return before(s, 2 * NG, 2, 0)

        def m_base(s):
            return before(s, 0, 2, 6)

        def plan(mid, back, front):
            t = (["x0", "x1"] if front else []) + ([("p", 0, g) for g in range(NG)] if mid else []) \
                + (["n0", "n1"] if back else []) + ([("p", 1, g) for g in range(NG)] if mid else [])
            m = (["o0", "o1", "w0", "w1"] if back else []) + (["q0", "q1"] if front else []) \
                + (["r0", "r1"] if back else [])
            return {u: i for i, u in enumerate(t)}, {u: i for i, u in enumerate(m)}

        def kc_heads(q, b):
            return kc[q, ds(b, 1), :, :].rearrange("p o g c -> p (o g) c")

        def vbd_heads(part, i):
            return vbd[:, part].rearrange("c (g i) p -> c g i p", i=HG)[:, :, i, i * HD:(i + 1) * HD]

        def vc_heads(b, i):
            return vc[:, ds(b, 1), :].rearrange("c o (g i d) -> c (o g) i d", i=HG, d=HD)[:, :, i, :]

        assert NG == 4 and B >= 2
        block = ctx.enter_context(nc.Block())

        @block.sync
        def _(sp):
            def run(s, b, mid, back, front, par=None):
                par = s % 2 if par is None else par
                if front:
                    if not (isinstance(s, int) and s < 0):
                        sp.wait_ge(xn_done, (s + 1) * 2)
                    sp.dma_start(xin[:], tile_rows2(n.x, s + 1)).then_inc(x_in, 16)
                if back:
                    sp.dma_start(xres[:], tile_rows2(n.x, s - 1)).then_inc(xres_in, 16)
                    for j in range(2):
                        sp.wait_ge(m_free, m_base(s) + plan(mid, back, front)[1][f"w{j}"] + 1)
                        sp.dma_start(n.tile_rows(n.x1_d, (s - 1) * 2 + j), x1[:, j]).then_inc(x1_out, 16)
                    for j in range(2):
                        sp.wait_ge(xn2_done, (s - 1) * 2 + j + 1)
                        sp.dma_start(n.tile_rows(n.xn2_d, (s - 1) * 2 + j), xn2[:, j]).then_inc(xn2_out, 16)

            def tile_rows2(t, s):
                return n.tile_rows(t, s * 2, 2)

            whole(sp, run)
            sp.wait_ge(x1_out, 16 * NT)
            sp.wait_ge(xn2_out, 16 * NT)

        @block.gpsimd
        def _(pool):
            def rstd(mv_sem, count, mv, ve, rs, out_sem, tmp_count):
                pool.wait_ge(mv_sem, count)
                pool.tensor_tensor(ve[:], mv[:, :, 1], eps[:], ALU.add).then_inc(rs_tmp, 1)
                pool.wait_ge(rs_tmp, tmp_count)
                pool.tensor_tensor(rs[:], ve[:], half[:], ALU.pow).then_inc(out_sem, 1)

            def run(s, b, mid, back, front, par=None):
                par = s % 2 if par is None else par
                tmp = before(s, 0, 1, 1)
                if front:
                    rstd(mv1_done, s * 2 + 4, mv1, ve1, rs1, rs1_done, tmp + 1)
                if back:
                    pool.wait_ge(xres_in, s * 16)
                    for j in range(2):
                        pool.tensor_tensor(xres[:, j], xres[:, j], bo_t[:], ALU.add).then_inc(xb_done, 1)
                if mid:
                    normalise(s, 0)
                if back:
                    rstd(mv2_done, s * 2, mv2, ve2, rs2, rs2_done, tmp + (2 if front else 1))
                if mid:
                    normalise(s, 1)

            def normalise(s, j):
                pool.wait_ge(ri_done, s * 2 + j + 1)
                pool.tensor_tensor(prob[:, j], prob[:, j], ri[:, j].unsqueeze(2).to_broadcast([P, H, C]),
                                   ALU.mult).then_inc(p_done, 1)

            whole(pool, run)

        @block.scalar
        def _(act):
            def hi(full, count, done, dst, src):
                act.wait_ge(full, count)
                act.activation(dst, src, ACT.Copy).then_inc(done, 1)

            def run(s, b, mid, back, front, par=None):
                par = s % 2 if par is None else par
                tb, mb = t_base(s), m_base(s)
                t, m = plan(mid, back, front)

                def keys(b):
                    for i in range(HG):
                        q = slice(i * HD, (i + 1) * HD)
                        act.activation(kbd[q, 0, :, i * C:(i + 1) * C], kc_heads(q, b),
                                       ACT.Copy).then_inc(bd_hi, 1)

                def tcopy(u, dst, parts=P):
                    i = t[u]
                    act.wait_ge(t_full, tb + i + 1)
                    act.activation(dst, t_ps[0:parts, i % 2].rearrange("p (a b) -> p a b", b=P), ACT.Copy).then_inc(t_hi, 1)

                def exps(j):
                    for pair in range(2):
                        act.wait_ge(s_sub, s * 4 + 2 * j + pair + 1)
                        g = slice(pair * H // 2, (pair + 1) * H // 2)
                        act.activation(prob[:, j, g], prob[:, j, g], ACT.Exp, scale=n.SCALE).then_inc(e_done, 1)

                if mid:
                    exps(0)
                if back:
                    for i, u in enumerate(("o0", "o1")):
                        act.wait_ge(m_full, mb + m[u] + 1)
                        act.activation(oT[:, 0, 2 * i:2 * i + 2], m_ps[:, m[u] % 2].rearrange("p (a b) -> p a b", b=W2),
                                       ACT.Copy).then_inc(m_hi, 1)
                if mid and par == 0:
                    for i in range(HG):
                        act.activation(vbd_heads(0, i), vc_heads(b, i), ACT.Copy).then_inc(bd_hi, 1)
                if front:
                    for j in range(2):
                        tcopy(f"x{j}", xT[:, 0, :, j * P:(j + 1) * P])
                if mid:
                    exps(1)
                    for g in range(NG):
                        tcopy(("p", 0, g), pT[:, 0, g * HG:(g + 1) * HG, 0:P], C)
                if par == 1 and front:
                    keys(b + 1)
                if front:
                    for i in range(2):
                        u = f"q{i}"
                        act.wait_ge(m_full, mb + m[u] + 1)
                        for g in range(2):
                            act.activation(qT[:, 1 - par, 0, 2 * i + g], m_ps[:, m[u] % 2, g * W2:(g + 1) * W2],
                                           ACT.Identity, bias=bq_s[:, 2 * i + g:2 * i + g + 1]).then_inc(m_hi, 1)
                if mid:
                    for g in range(NG):
                        tcopy(("p", 1, g), pT[:, 0, g * HG:(g + 1) * HG, P:W2], C)

            whole(act, run)

        @block.vector
        def _(dve):
            def run(s, b, mid, back, front, par=None):
                par = s % 2 if par is None else par
                tb, mb = t_base(s), m_base(s)
                t, m = plan(mid, back, front)
                hb = before(s, 0, 4, 2)
                sb0 = before(s, 0, 2, 2)

                def keys(b):
                    for i in range(HG):
                        q = slice(i * HD, (i + 1) * HD)
                        dve.wait_ge(bd_hi, b * 2 * HG + i + 1)
                        hi = kbd[q, 0, :, i * C:(i + 1) * C].bitcast(F32)
                        dve.tensor_tensor(kbd[q, 1, :, i * C:(i + 1) * C],
                                          kc_heads(q, b), hi,
                                          ALU.subtract).then_inc(k_bd, 1)

                def tlow(u, dst, hi_ap, parts=P):
                    i = t[u]
                    after_n = 2 if back and i > t["n1"] else 0
                    dve.wait_ge(t_hi, hi_base(s) + i - after_n + 1)
                    dve.tensor_tensor(dst, t_ps[0:parts, i % 2].rearrange("p (a b) -> p a b", b=P),
                                      hi_ap.bitcast(F32), ALU.subtract).then_inc(t_free, 1)

                def softmax_in(j):
                    for pair in range(2):
                        dve.wait_ge(s_full, s * 4 + 2 * j + pair + 1)
                        hs = slice(pair * H // 2, (pair + 1) * H // 2)
                        sc = s_ps[:, 2 * pair:2 * pair + 2, 0:GC].rearrange("p g (i c) -> p g i c", c=C)
                        mxp = mx[:, j, hs].rearrange("p (g i) -> p g i", i=HG)
                        dve.tensor_reduce(mxp, sc, AX.X, ALU.max).then_inc(mx_done, 1)
                        dve.wait_ge(mx_done, s * 4 + 2 * j + pair + 1)
                        dve.tensor_tensor(prob[:, j, hs].rearrange("p (g i) c -> p g i c", i=HG), sc,
                                          mxp.unsqueeze(3).to_broadcast([P, 2, HG, C]), ALU.subtract).then_inc(s_sub, 1)

                def softmax_sum(j):
                    dve.wait_ge(e_done, s * 4 + 2 * j + 2)
                    dve.tensor_reduce(sm[:, j], prob[:, j], AX.X, ALU.add).then_inc(sum_done, 1)
                    dve.wait_ge(sum_done, s * 2 + j + 1)
                    dve.reciprocal(ri[:, j], sm[:, j]).then_inc(ri_done, 1)

                def x1_stats():
                    dve.wait_ge(m_free, mb + m["w1"] + 1)
                    norm_stats(lambda j: x1[:, j], st2, mv2, mv2_done, sb0 + (2 if front else 0))

                def norm_stats(src_of, st, mv, done, base):
                    for j in range(2):
                        dve.bn_stats(st[:, j], src_of(j)).then_inc(st_done, 1)
                    for j in range(2):
                        hold(dve, st_done, base + j + 1, n.passed_dve)
                        dve.bn_aggr(mv[:, j], st[:, j]).then_inc(done, 1)

                if front:
                    dve.wait_ge(x_in, s * 16 + 32)
                    norm_stats(lambda j: xin[:, j], st1, mv1, mv1_done, sb0)
                if mid:
                    softmax_in(0)
                if front:
                    dve.wait_ge(rs1_done, s + 2)
                    for j in range(2):
                        dve.tensor_scalar(xn[:, j], xin[:, j], mv1[:, j, 0:1], rs1[:, j:j + 1], ALU.subtract,
                                          ALU.mult).then_inc(xn_done, 1)
                if back:
                    for i, u in enumerate(("o0", "o1")):
                        dve.wait_ge(m_hi, hb + i + 1)
                        dve.tensor_tensor(oT[:, 1, 2 * i:2 * i + 2], m_ps[:, m[u] % 2].rearrange("p (a b) -> p a b", b=W2),
                                          oT[:, 0, 2 * i:2 * i + 2].bitcast(F32), ALU.subtract).then_inc(m_free, 1)
                if mid and par == 0:
                    for i in range(HG):
                        dve.wait_ge(bd_hi, b * 2 * HG + HG + i + 1)
                        dve.tensor_tensor(vbd_heads(1, i), vc_heads(b, i), vbd_heads(0, i).bitcast(F32),
                                          ALU.subtract).then_inc(v_bd, 1)
                if mid:
                    softmax_sum(0)
                    softmax_in(1)
                if front:
                    for j in range(2):
                        tlow(f"x{j}", xT[:, 1, :, j * P:(j + 1) * P], xT[:, 0, :, j * P:(j + 1) * P])
                if back:
                    dve.wait_ge(xb_done, s * 2)
                    if not (isinstance(s, int) and s <= 1):
                        dve.wait_ge(x1_out, (s - 1) * 32)
                    for j in range(2):
                        u = f"w{j}"
                        dve.wait_ge(m_full, mb + m[u] + 1)
                        dve.scalar_tensor_tensor(out=x1[:, j], in0=m_ps[:, m[u] % 2], scalar=tg[:, 0:1], in1=xres[:, j],
                                                 op0=ALU.mult, op1=ALU.add).then_inc(m_free, 1)
                    if not mid:
                        x1_stats()
                if mid:
                    for g in range(NG):
                        hs = slice(g * HG, (g + 1) * HG)
                        tlow(("p", 0, g), pT[:, 1, hs, 0:P], pT[:, 0, hs, 0:P], C)
                        if g == 1 and back:
                            x1_stats()
                        if g == 1:
                            softmax_sum(1)
                if par == 1 and front:
                    keys(b + 1)
                if back:
                    dve.wait_ge(rs2_done, s)
                    if not (isinstance(s, int) and s <= 1):
                        dve.wait_ge(xn2_out, (s - 1) * 32)
                    for j in range(2):
                        dve.tensor_scalar(xn2[:, j], x1[:, j], mv2[:, j, 0:1], rs2[:, j:j + 1], ALU.subtract,
                                          ALU.mult).then_inc(xn2_done, 1)
                for i in range(2):
                    if front:
                        u = f"q{i}"
                        for g in range(2):
                            dve.wait_ge(m_hi, hb + (2 if back else 0) + 2 * i + 2)
                            ins = dve.scalar_tensor_tensor(
                                out=qT[:, 1 - par, 1, 2 * i + g], in0=m_ps[:, m[u] % 2, g * W2:(g + 1) * W2],
                                scalar=bq_s[:, 2 * i + g:2 * i + g + 1], in1=qT[:, 1 - par, 0, 2 * i + g].bitcast(F32),
                                op0=ALU.add, op1=ALU.subtract)
                        ins.then_inc(m_free, 1)
                    if back and i == 0:
                        for j in range(2):
                            dve.wait_ge(t_full, tb + t[f"n{j}"] + 1)
                            dve.tensor_copy(x2T[:, :, j * P:(j + 1) * P],
                                            t_ps[:, t[f"n{j}"] % 2].rearrange("p (a b) -> p a b", b=P)).then_inc(t_free, 1)
                if back:
                    for j in range(2):
                        u = f"r{j}"
                        dve.wait_ge(m_full, mb + m[u] + 1)
                        dve.tensor_tensor(logits[:, ds((s - 1) * 2 + j, 1), :].rearrange("p o e -> p (o e)"),
                                          m_ps[:, m[u] % 2, 0:E], rb[:], ALU.add).then_inc(m_free, 1)
                if mid:
                    for g in range(NG):
                        hs = slice(g * HG, (g + 1) * HG)
                        tlow(("p", 1, g), pT[:, 1, hs, P:W2], pT[:, 0, hs, P:W2], C)

            whole(dve, run)

        @block.tensor
        def _(pe):
            def run(s, b, mid, back, front, par=None):
                par = s % 2 if par is None else par
                tb, mb = t_base(s), m_base(s)
                t, m = plan(mid, back, front)

                def t_room(u):
                    if not (isinstance(s, int) and tb + t[u] < 2):
                        pe.wait_ge(t_free, tb + t[u] - 1)

                def m_room(u):
                    if not (isinstance(s, int) and mb + m[u] < 2):
                        pe.wait_ge(m_free, mb + m[u] - 1)

                def scores(j):
                    for g in range(NG):
                        if g % 2 == 0 and not (isinstance(s, int) and s * 4 + 2 * j + g // 2 < 2):
                            pe.wait_ge(s_sub, s * 4 + 2 * j + g // 2 - 1)
                        for pa, pb in PASSES:
                            mm = pe.matmul(s_ps[:, g, 0:GC], qT[:, par, pa, g, j * P:(j + 1) * P], kbd[:, pb, g, :],
                                           start=((pa, pb) == PASSES[0]), stop=((pa, pb) == PASSES[-1]))
                        if g % 2:
                            mm.then_inc(s_full, 1)

                def prob_transposes(j):
                    pe.wait_ge(p_done, s * 2 + j + 1)
                    for g in range(NG):
                        t_room(("p", j, g))
                        for i in range(HG):
                            mm = pe.transpose(t_ps[0:C, t[("p", j, g)] % 2, i * P:(i + 1) * P], prob[:, j, g * HG + i, :],
                                              ident[:])
                        mm.then_inc(t_full, 1)

                if mid:
                    if par == 0:
                        pe.wait_ge(k_bd, b * HG + HG)
                    pe.wait_ge(m_free, mb)
                    scores(0)
                if back:
                    pe.wait_ge(t_free, tb)
                    pe.wait_ge(v_bd, (b - 1 if par == 0 else b) * HG + HG)
                    for i in range(2):
                        m_room(f"o{i}")
                        for g in range(2):
                            for h in range(HG):
                                hh = (2 * i + g) * HG + h
                                for pa, pb in PASSES:
                                    mm = pe.matmul(m_ps[:, m[f"o{i}"] % 2, g * W2:(g + 1) * W2], vbd[:, pa, hh, :],
                                                   pT[:, pb, hh, :], start=(h == 0 and (pa, pb) == PASSES[0]),
                                                   stop=(h == HG - 1 and (pa, pb) == PASSES[-1]))
                        mm.then_inc(m_full, 1)
                if mid:
                    scores(1)
                if front:
                    pe.wait_ge(xn_done, s * 2 + 4)
                    for j in range(2):
                        t_room(f"x{j}")
                        for k in range(KD):
                            mm = pe.transpose(t_ps[:, t[f"x{j}"] % 2, k * P:(k + 1) * P], xn[:, j, k * P:(k + 1) * P],
                                              ident[:])
                        mm.then_inc(t_full, 1)
                if back:
                    pe.wait_ge(m_free, mb + m["o1"] + 1)
                    for j in range(2):
                        m_room(f"w{j}")
                        for k in range(KD):
                            for pa, pb in PASSES:
                                mm = pe.matmul(m_ps[:, m[f"w{j}"] % 2], oT[:, pa, k, j * P:(j + 1) * P], wo[:, pb, k, :],
                                               start=(k == 0 and (pa, pb) == PASSES[0]),
                                               stop=(k == KD - 1 and (pa, pb) == PASSES[-1]))
                        mm.then_inc(m_full, 1)
                if mid:
                    prob_transposes(0)
                if front:
                    pe.wait_ge(t_free, tb + t["x1"] + 1)
                    for i in range(2):
                        m_room(f"q{i}")
                        for g in range(2):
                            mt = 2 * i + g
                            for k in range(KD):
                                for pa, pb in PASSES:
                                    mm = pe.matmul(m_ps[:, m[f"q{i}"] % 2, g * W2:(g + 1) * W2],
                                                   wq[:, pa, k, mt * P:(mt + 1) * P], xT[:, pb, k, :],
                                                   start=(k == 0 and (pa, pb) == PASSES[0]),
                                                   stop=(k == KD - 1 and (pa, pb) == PASSES[-1]))
                        mm.then_inc(m_full, 1)
                if back:
                    pe.wait_ge(xn2_done, s * 2)
                    for j in range(2):
                        t_room(f"n{j}")
                        for k in range(KD):
                            mm = pe.transpose(t_ps[:, t[f"n{j}"] % 2, k * P:(k + 1) * P], xn2[:, j, k * P:(k + 1) * P],
                                              ident[:])
                        mm.then_inc(t_full, 1)
                    pe.wait_ge(t_free, tb + t["n1"] + 1)
                    for j in range(2):
                        m_room(f"r{j}")
                        for k in range(KD):
                            mm = pe.matmul(m_ps[:, m[f"r{j}"] % 2, 0:E], x2T[:, k, j * P:(j + 1) * P], rw[:, k, :],
                                           start=(k == 0), stop=(k == KD - 1))
                        mm.then_inc(m_full, 1)
                if mid:
                    prob_transposes(1)

            whole(pe, run)


def experts(nc, n):
    NT, E, KD, D, KH, HID, NSH, NE = n.NT, n.E, n.KD, n.D, n.KH, n.HID, n.NSH, n.NE
    MT, MAXT, DH = n.MIN_TILES, n.MAXT, n.DH
    ident, logits, gate, slot, tg, mean = n.ident, n.logits, n.gate, n.slot, n.tg, n.mean
    NC = 4
    WC = KD * DH // NC
    WN = KD * 2 * HID + KH * D
    W1N = KD * 2 * HID
    WB = 4
    T_QUANT = 2 * NC + 2
    T_END = T_QUANT + 4 * NC
    assert T_END < NT - 1 and NE > WB and (MAXT - 2 * NT) % MT == 0 and (MAXT - 2 * NT) // MT <= 2 * NC

    with ExitStack() as ctx:
        def sb(name, shape, dt):
            return ctx.enter_context(nc.sbuf_tensor("e_" + name, shape, dt))

        def sem(name):
            return ctx.enter_context(nc.semaphore("e_" + name))

        def psum(name, shape, dt=F32):
            return ctx.enter_context(nc.psum_tensor("e_" + name, shape, dt))

        top8 = sb("top8", [P, NT, 8], F32)
        idx8 = sb("idx8", [P, NT, 8], U32)
        idx = sb("idx", [P, 2, NT], F32)
        iota_e = sb("iota_e", [P, E], F32)
        iota_t = sb("iota_t", [P, NT], F32)
        hot = sb("hot", [P, 2, NT, E], F32)
        chosen = sb("chosen", [P, NT, E], BF16)
        before = sb("before", [P, P], BF16)
        ones = sb("ones", [P, P], BF16)
        onesf = sb("onesf", [P, NT], F32)
        tot = sb("tot", [P, E, NT], F32)
        cum = sb("cum", [P, E, NT], F32)
        big = sb("big", [P, E, NT], F32)
        tiles = sb("tiles", [P, E], F32)
        tcum = sb("tcum", [P, E], F32)
        first = sb("first", [P, E + 1], F32)
        least = sb("least", [P, E + 1], F32)
        bounds = sb("bounds", [P, E + 1], I32)
        base = sb("base", [P, E, NT], F32)
        pos = sb("pos", [P, NT, E], F32)
        sel = sb("sel", [P, 2, NT, E], F32)
        posf = sb("posf", [P, 2, NT], F32)
        dif = sb("dif", [P, NT], F32)
        ex = sb("ex", [P, NT], F32)
        den = sb("den", [P, NT], F32)
        zero = sb("zero", [P, MT, D], F32)
        srow = sb("srow", [P, 2, D], F32)
        scol = sb("scol", [P, 2, 2], U32)
        wraw = sb("wraw", [P, 2, WN], F32)
        w = sb("w", [P, WB, 2, WN], FR)
        xe = sb("xe", [P, D], F32)
        xr = sb("xr", [P, D], F32)
        x2 = sb("x2", [P, D], F32)
        xeT = sb("xeT", [P, 2, KD, P], FR)
        sg = sb("sg", [P, NSH, HID], F32)
        hh = sb("hh", [P, NSH, HID], F32)
        hT = sb("hT", [P, 2, NSH * KH, P], FR)
        ye = sb("ye", [P, D], F32)
        r_ps = psum("r_ps", [P, 2, NT * E])
        x_ps = psum("x_ps", [P, KD, P])
        u_ps = psum("u_ps", [P, NSH, 2 * HID])
        h_ps = psum("h_ps", [P, NSH * KH, P])
        y_ps = psum("y_ps", [P, D])
        s_ps = psum("s_ps", [P, 512])
        fraw = sb("fraw", [P, 2, WC], F32)
        asum = sb("asum", [P, 2, NC], F32)
        inv = sb("inv", [P, 2], F32)
        fones = sb("fones", [P, P], F32)
        fq = sb("fq", [P, 2, WC], BF16)

        passed_act = sem("passed_act")
        zero_set = sem("zero_set")
        tail_out = sem("tail_out")
        consts = sem("consts")
        masks = sem("masks")
        route = sem("route")
        chosen_done = sem("chosen_done")
        counted = sem("counted")
        bounds_done = sem("bounds_done")
        dif_done = sem("dif_done")
        ex_done = sem("ex_done")
        slot_done = sem("slot_done")
        zeroed = sem("zeroed")
        srow_in = [sem("srow_in0"), sem("srow_in1")]
        scol_done = sem("scol_done")
        scattered = [sem("scattered0"), sem("scattered1")]
        w_in = [sem("w_in0"), sem("w_in1")]
        ws_in = [sem("ws_in0"), sem("ws_in1")]
        ws_hi = sem("ws_hi")
        ws_ready = sem("ws_ready")
        w_hi = sem("w_hi")
        w_ready = sem("w_ready")
        xe_in = sem("xe_in")
        x_full = sem("x_full")
        x_hi = sem("x_hi")
        x_lo = sem("x_lo")
        u_full = sem("u_full")
        sg_done = sem("sg_done")
        hh_done = sem("hh_done")
        h_full = sem("h_full")
        h_hi = sem("h_hi")
        h_lo = sem("h_lo")
        y_full = sem("y_full")
        y_copied = sem("y_copied")
        y_out = sem("y_out")
        xr_in = sem("xr_in")
        x2_done = sem("x2_done")
        x2_out = sem("x2_out")
        f_in = [sem("f_in0"), sem("f_in1")]
        asum_done = sem("asum_done")
        asum_full = sem("asum_full")
        mean_steps = sem("mean_steps")
        fq_steps = sem("fq_steps")
        fq_out = [sem("fq_out0"), sem("fq_out1")]

        def bound(eng, e):
            return eng.value_load(bounds[0:1, e:e + 1], min_val=0, max_val=MAXT - MT * E) + MT * e

        def first_weights(e):
            return wraw[:, e % 2, 0:W1N].rearrange("p (k f) -> p k f", k=KD), n.w13[ds(e, 1)].rearrange("o p k f -> p (o k) f")

        def second_weights(e):
            return wraw[:, e % 2, W1N:WN].rearrange("p (k f) -> p k f", k=KH), n.w2e[ds(e, 1)].rearrange("o p k f -> p (o k) f")

        def f_chunk(c):
            src = (n.w1T, n.w2T)[c // NC].rearrange("p k f -> p (k f)")
            return src[:, c % NC * WC:(c % NC + 1) * WC]

        block = ctx.enter_context(nc.Block())

        @block.sync
        def _(sp):
            def load(src, row_tile, g):
                if not (isinstance(g, int) and g == 0):
                    sp.wait_ge(x_full, g)
                sp.dma_start(xe[:], n.tile_rows(src, row_tile)).then_inc(xe_in, 16)

            for e in range(NSH):
                sp.dma_start(*first_weights(e)).then_inc(ws_in[e], 16)
                sp.dma_start(*second_weights(e)).then_inc(ws_in[e], 16)
            load(n.xn2_d, 0, 0)
            with sp.Fori(1, NT) as t:
                load(n.xn2_d, t, t)
            sp.wait_ge(bounds_done, 1)
            for par in range(2):
                sp.wait_ge(scattered[par], NT // 2 * 32)
            load(n.xs_d, 0, NT)
            end = bound(sp, E)
            with sp.Fori(1, end) as r:
                load(n.xs_d, r, r + NT)

        @block.gpsimd
        def _(pool):
            def fetch(e):
                q = w_in[e % 2]
                pool.dma_start(*first_weights(e)).then_inc(q, 16)
                pool.dma_start(*second_weights(e)).then_inc(q, 16)

            def split(e):
                par, ring, i = e % 2, e % WB, e - NSH
                pool.wait_ge(w_in[par], i // 2 * 32 + 32)
                pool.tensor_copy(w[:, ring, 0], wraw[:, par]).then_inc(w_hi, 1)
                pool.wait_ge(w_hi, i + 1)
                pool.tensor_tensor(w[:, ring, 1], wraw[:, par], w[:, ring, 0].bitcast(F32), ALU.subtract).then_inc(w_ready, 1)
                if e + 2 < NE:
                    pool.wait_ge(w_ready, i + 1)
                    fetch(e + 2)

            pool.memset(zero[:], 0.0).then_inc(zero_set, 1)
            pool.memset(onesf[:], 1.0)
            pool.memset(ones[:], 1.0)
            pool.memset(fones[:], 1.0)
            pool.iota(iota_e[:], pattern=[[1, E]], base=0, channel_multiplier=0, allow_small_or_imprecise_dtypes=True)
            pool.iota(least[:], pattern=[[MT, E + 1]], base=0, channel_multiplier=0, allow_small_or_imprecise_dtypes=True)
            pool.iota(iota_t[:], pattern=[[P, NT]], base=0, channel_multiplier=0, allow_small_or_imprecise_dtypes=True)
            pool.memset(before[:], 1.0).then_inc(masks, 1)
            pool.wait_ge(masks, 1)
            pool.affine_select(out=before[:], in_=before[:], compare_op=ALU.is_gt, fill=0.0, base=0,
                               pattern=[[1, P]], channel_multiplier=-1).then_inc(consts, 1)
            pool.wait_ge(bounds_done, 1)
            for e in range(E):
                end = bound(pool, e + 1)
                pool.dma_start(n.xs_d[ds((end - MT) * P, MT * P), :].rearrange("(n p) d -> p n d", p=P),
                               zero[:]).then_inc(zeroed, 16)
            pool.wait_ge(slot_done, 1)
            pool.wait_ge(zeroed, 16 * E)

            def stage(t, par, used):
                if used is not None:
                    pool.wait_ge(scattered[par], used)
                pool.dma_start(srow[:, par], n.tile_rows(n.xn2_d, t)).then_inc(srow_in[par], 16)
                pool.tensor_copy(scol[:, par], slot[:, :, ds(t, 1)].rearrange("p s o -> p (s o)")).then_inc(scol_done, 1)

            def send(i, par, count):
                hold(pool, srow_in[par], i * 16 + 16, n.passed_pool)
                hold(pool, scol_done, count, n.passed_pool)
                for s in range(2):
                    pool.indirect_dma_start(out=n.xs_d[:, :], out_offset=bass.IndirectOffsetOnAxis(ap=scol[:, par, s:s + 1], axis=0),
                                            in_=srow[:, par], in_offset=None).then_inc(scattered[par], 16)

            for par in range(2):
                stage(par, par, None)
            for par in range(2):
                send(0, par, par + 1)
            with pool.Fori(1, NT // 2) as i:
                for par in range(2):
                    stage(i * 2 + par, par, i * 32)
                for par in range(2):
                    send(i, par, i * 2 + par + 1)
            for e in range(NSH):
                pool.wait_ge(ws_ready, e + 1)
                fetch(NSH + e)
            for e in range(NSH, NE):
                if e >= WB + NSH:
                    hold(pool, y_full, bound(pool, e - WB + 1 - NSH) + NT, n.passed_pool)
                elif e >= WB:
                    pool.wait_ge(y_full, NT)
                split(e)

        @block.scalar
        def _(act):
            act.wait_ge(dif_done, 1)
            act.activation(ex[:], dif[:], ACT.Exp).then_inc(ex_done, 1)

            def shared(t, last=False):
                for i in range(NSH):
                    act.wait_ge(u_full, t * NSH + i + 1)
                    act.activation(sg[:, i], u_ps[:, i, 0:HID], ACT.Silu).then_inc(sg_done, 1)
                if not last:
                    x_high(t + 1)
                act.wait_ge(h_full, t + 1)
                act.activation(hT[:, 0], h_ps[:], ACT.Copy).then_inc(h_hi, 1)
                if not (isinstance(t, int) and t == 0):
                    store_x2(t - 1)
                load_x1(t)
                if last:
                    x_high(t + 1)
                    store_x2(t)

            def store_x2(t):
                act.wait_ge(x2_done, t + 1)
                act.dma_start(n.tile_rows(n.x2_d, t), x2[:]).then_inc(x2_out, 16)

            def load_x1(t):
                act.dma_start(xr[:], n.tile_rows(n.x1_d, t)).then_inc(xr_in, 16)

            def routed(r, lead, last):
                g = r + NT
                act.wait_ge(u_full, g + NT * (NSH - 1) + 1)
                act.activation(sg[:, 0], u_ps[:, 0, 0:HID], ACT.Silu).then_inc(sg_done, 1)
                if not last:
                    x_high(g + 1)
                if lead:
                    y_copy(r - 1)
                act.wait_ge(h_full, g + 1)
                act.activation(hT[:, 0, 0:KH], h_ps[:, 0:KH], ACT.Copy).then_inc(h_hi, 1)

            def x_high(g):
                act.wait_ge(x_full, g + 1)
                act.activation(xeT[:, 0], x_ps[:], ACT.Copy).then_inc(x_hi, 1)

            def y_copy(r):
                act.wait_ge(y_full, r + NT + 1)
                if not (isinstance(r, int) and r == 0):
                    act.wait_ge(y_out, r * 16)
                act.activation(ye[:], y_ps[:], ACT.Copy).then_inc(y_copied, 1)
                act.wait_ge(y_copied, r + 1)
                act.dma_start(n.tile_rows(n.ys_d, r), ye[:]).then_inc(y_out, 16)

            def sum_chunk(c):
                act.wait_ge(f_in[c % 2], c // 2 * 16 + 16)
                act.activation(fraw[:, c % 2], fraw[:, c % 2], ACT.Abs,
                               accum_out=asum[:, c // NC, c % NC:c % NC + 1]).then_inc(asum_done, 1)
                act.wait_ge(asum_done, c + 1)
                if c + 2 < 2 * NC:
                    reload(c + 2)

            def reload(c):
                act.dma_start(fraw[:, c % 2], f_chunk(c)).then_inc(f_in[c % 2], 16)

            def store_chunk(c):
                act.wait_ge(fq_steps, c * 3 + 3)
                dst = (n.w1q_d, n.w2q_d)[c // NC]
                act.dma_start(dst[:, c % NC * WC:(c % NC + 1) * WC], fq[:, c % 2]).then_inc(fq_out[c % 2], 16)
                if c + 2 < 2 * NC:
                    reload(c + 2)

            def clear_tail(i):
                if i == 0:
                    act.wait_ge(zero_set, 1)
                if i < (MAXT - 2 * NT) // MT:
                    act.dma_start(n.tile_rows(n.ys_d, 2 * NT + i * MT, MT), zero[:]).then_inc(tail_out, 16)

            for c in range(2):
                reload(c)
            for e in range(NSH):
                act.wait_ge(ws_in[e], 32)
                act.activation(w[:, e, 0], wraw[:, e], ACT.Copy).then_inc(ws_hi, 1)
                if e == 0:
                    x_high(0)
            for t in range(2 * NC):
                shared(t)
                sum_chunk(t)
            for c in range(2):
                reload(c)
            for t in range(2 * NC, T_END):
                shared(t)
                if t >= T_QUANT and (t - T_QUANT) % 2 == 0:
                    clear_tail((t - T_QUANT) // 2)
                if t >= T_QUANT and (t - T_QUANT) % 2 == 1:
                    store_chunk((t - T_QUANT) // 2)
            with act.Fori(T_END, NT - 1) as t:
                shared(t)
            for q in fq_out:
                act.wait_ge(q, NC * 16)
            shared(NT - 1, True)
            routed(0, False, False)
            act.wait_ge(tail_out, (MAXT - 2 * NT) // MT * 16)
            act.wait_ge(bounds_done, 1)
            end = bound(act, E)
            with act.Fori(1, end - 1) as r:
                routed(r, True, False)
            routed(end - 1, True, True)
            y_copy(end - 1)
            act.wait_ge(x2_out, NT * 16)
            hold(act, y_out, end * 16, passed_act)

        @block.vector
        def _(dve):
            steps = [0]

            def then(ins):
                steps[0] += 1
                ins.then_inc(route, 1)
                dve.wait_ge(route, steps[0])

            for t in range(NT):
                ins = dve.max(top8[:, t], logits[:, t])
            then(ins)
            for t in range(NT):
                ins = dve.max_index(idx8[:, t], top8[:, t], logits[:, t])
            then(ins)
            dve.tensor_tensor(dif[:], top8[:, :, 1], top8[:, :, 0], ALU.subtract).then_inc(dif_done, 1)
            then(dve.tensor_copy(idx[:], idx8[:, :, 0:2].rearrange("p t s -> p s t")))
            dve.wait_ge(consts, 1)
            for s in range(2):
                ins = dve.tensor_tensor(hot[:, s], idx[:, s].unsqueeze(2).to_broadcast([P, NT, E]),
                                        iota_e[:].unsqueeze(1).to_broadcast([P, NT, E]), ALU.is_equal)
            then(ins)
            dve.tensor_tensor(chosen[:], hot[:, 0], hot[:, 1], ALU.add).then_inc(chosen_done, 1)
            dve.wait_ge(counted, 1)
            then(dve.tensor_copy(tot[:], r_ps[:, 1].rearrange("p (t e) -> p e t", e=E)))
            for e in range(E):
                ins = dve.tensor_tensor_scan(cum[:, e], onesf[:], tot[:, e], 0.0, ALU.mult, ALU.add)
            then(ins)
            then(dve.tensor_tensor(big[:], cum[:, :, NT - 1:NT].to_broadcast([P, E, NT]),
                                   iota_t[:].unsqueeze(1).to_broadcast([P, E, NT]), ALU.is_gt))
            then(dve.tensor_reduce(tiles[:], big[:], AX.X, ALU.add))
            then(dve.tensor_scalar(tiles[:], tiles[:], float(MT), None, ALU.max))
            then(dve.tensor_tensor_scan(tcum[:], onesf[:, 0:E], tiles[:], 0.0, ALU.mult, ALU.add))
            dve.tensor_tensor(first[:, 0:E], tcum[:], tiles[:], ALU.subtract)
            then(dve.tensor_copy(first[:, E:E + 1], tcum[:, E - 1:E]))
            dve.tensor_tensor(bounds[:], first[:], least[:], ALU.subtract).then_inc(bounds_done, 1)
            then(dve.tensor_tensor(base[:], cum[:], tot[:], ALU.subtract))
            then(dve.scalar_tensor_tensor(out=base[:], in0=first[:, 0:E].unsqueeze(2).to_broadcast([P, E, NT]),
                                          scalar=float(P), in1=base[:], op0=ALU.mult, op1=ALU.add))
            then(dve.tensor_tensor(pos[:], r_ps[:, 0].rearrange("p (t e) -> p t e", e=E),
                                   base[:].rearrange("p e t -> p t e"), ALU.add))
            for s in range(2):
                ins = dve.tensor_tensor(sel[:, s], hot[:, s], pos[:], ALU.mult)
            then(ins)
            then(dve.tensor_reduce(posf[:], sel[:], AX.X, ALU.add))
            dve.tensor_copy(slot[:], posf[:]).then_inc(slot_done, 1)
            dve.wait_ge(ex_done, 1)
            then(dve.tensor_scalar(den[:], ex[:], 1.0, None, ALU.add))
            then(dve.reciprocal(den[:], den[:]))
            then(dve.tensor_scalar(gate[:, 0], den[:], tg[:, 2:3], None, ALU.mult))
            then(dve.tensor_tensor(gate[:, 1], gate[:, 0], ex[:], ALU.mult))

            def x_low(g):
                dve.wait_ge(x_hi, g + 1)
                dve.tensor_tensor(xeT[:, 1], x_ps[:], xeT[:, 0].bitcast(F32), ALU.subtract).then_inc(x_lo, 1)

            def shared(t, lead=True, last=False):
                for i in range(NSH):
                    dve.wait_ge(sg_done, t * NSH + i + 1)
                    dve.tensor_tensor(hh[:, i], u_ps[:, i, HID:2 * HID], sg[:, i], ALU.mult).then_inc(hh_done, 1)
                if not last:
                    x_low(t + 1)
                if lead:
                    add_shared(t - 1)
                dve.wait_ge(h_hi, t + 1)
                dve.tensor_tensor(hT[:, 1], h_ps[:], hT[:, 0].bitcast(F32), ALU.subtract).then_inc(h_lo, 1)
                if last:
                    add_shared(t)
                    x_low(t + 1)

            def add_shared(t):
                dve.wait_ge(y_full, t + 1)
                dve.wait_ge(xr_in, t * 16 + 16)
                if not (isinstance(t, int) and t == 0):
                    dve.wait_ge(x2_out, t * 16)
                dve.scalar_tensor_tensor(out=x2[:], in0=y_ps[:], scalar=tg[:, 2:3], in1=xr[:], op0=ALU.mult,
                                         op1=ALU.add).then_inc(x2_done, 1)

            def routed(r, last):
                g = r + NT
                dve.wait_ge(sg_done, g + NT * (NSH - 1) + 1)
                dve.tensor_tensor(hh[:, 0], u_ps[:, 0, HID:2 * HID], sg[:, 0], ALU.mult).then_inc(hh_done, 1)
                if not last:
                    x_low(g + 1)
                dve.wait_ge(h_hi, g + 1)
                dve.tensor_tensor(hT[:, 1, 0:KH], h_ps[:, 0:KH], hT[:, 0, 0:KH].bitcast(F32),
                                  ALU.subtract).then_inc(h_lo, 1)

            def quantise(c):
                i = c // NC
                raw = fraw[:, c % 2]
                dve.wait_ge(f_in[c % 2], (NC + c // 2 + 1) * 16)
                dve.tensor_scalar(raw, raw, inv[:, i:i + 1], MAGIC, ALU.mult, ALU.add).then_inc(fq_steps, 1)
                dve.wait_ge(fq_steps, c * 3 + 1)
                dve.tensor_scalar(raw, raw, MAGIC - 1.0, MAGIC + 1.0, ALU.max, ALU.min).then_inc(fq_steps, 1)
                dve.wait_ge(fq_steps, c * 3 + 2)
                if c >= 2:
                    dve.wait_ge(fq_out[c % 2], c // 2 * 16)
                dve.tensor_scalar(fq[:, c % 2], raw, MAGIC, None, ALU.subtract).then_inc(fq_steps, 1)

            for e in range(NSH):
                dve.wait_ge(ws_hi, e + 1)
                dve.tensor_tensor(w[:, e, 1], wraw[:, e], w[:, e, 0].bitcast(F32), ALU.subtract).then_inc(ws_ready, 1)
                if e == 0:
                    x_low(0)
            for t in range(2 * NC + 2):
                shared(t, t > 0)
            dve.wait_ge(asum_full, 1)
            dve.tensor_reduce(inv[:], s_ps[:, 0:2 * NC].rearrange("p (i c) -> p i c", c=NC), AX.X, ALU.add).then_inc(mean_steps, 1)
            dve.wait_ge(mean_steps, 1)
            dve.tensor_scalar(mean[:], inv[:], 1.0 / (D * DH), EPS_Q, ALU.mult, ALU.max).then_inc(mean_steps, 1)
            dve.wait_ge(mean_steps, 2)
            dve.reciprocal(inv[:], mean[:]).then_inc(mean_steps, 1)
            dve.wait_ge(mean_steps, 3)
            for t in range(T_QUANT, T_END):
                shared(t)
                if (t - T_QUANT) % 2 == 0:
                    quantise((t - T_QUANT) // 2)
            with dve.Fori(T_END, NT - 1) as t:
                shared(t)
            shared(NT - 1, True, True)
            routed(0, False)
            dve.wait_ge(bounds_done, 1)
            end = bound(dve, E)
            with dve.Fori(1, end - 1) as r:
                routed(r, False)
            routed(end - 1, True)

        @block.tensor
        def _(pe):
            pe.wait_ge(consts, 1)
            pe.wait_ge(chosen_done, 1)
            for i, m in enumerate((before, ones)):
                mm = pe.matmul(r_ps[:, i], m[:], chosen[:].rearrange("p t e -> p (t e)"), start=True, stop=True)
            mm.then_inc(counted, 1)

            def x_transposes(g):
                pe.wait_ge(xe_in, g * 16 + 16)
                for k in range(KD):
                    mm = pe.transpose(x_ps[:, k], xe[:, k * P:(k + 1) * P], ident[:])
                mm.then_inc(x_full, 1)

            def up(g, i, par):
                pe.wait_ge(x_lo, g + 1)
                for k in range(KD):
                    for pa, pb in PASSES:
                        mm = pe.matmul(u_ps[:, i], xeT[:, pa, k], w[:, par, pb, k * 2 * HID:(k + 1) * 2 * HID],
                                       start=(k == 0 and (pa, pb) == PASSES[0]),
                                       stop=(k == KD - 1 and (pa, pb) == PASSES[-1]))
                mm.then_inc(u_full, 1)

            def down(g, pars):
                pe.wait_ge(h_lo, g + 1)
                for i, par in enumerate(pars):
                    for k in range(KH):
                        for pa, pb in PASSES:
                            mm = pe.matmul(y_ps[:], hT[:, pa, i * KH + k], w[:, par, pb, W1N + k * D:W1N + (k + 1) * D],
                                           start=(i == 0 and k == 0 and (pa, pb) == PASSES[0]),
                                           stop=(i == len(pars) - 1 and k == KH - 1 and (pa, pb) == PASSES[-1]))
                mm.then_inc(y_full, 1)

            def h_transposes(count, parts):
                pe.wait_ge(hh_done, count)
                for i in range(parts):
                    for k in range(KH):
                        mm = pe.transpose(h_ps[:, i * KH + k], hh[:, i, k * P:(k + 1) * P], ident[:])
                mm.then_inc(h_full, 1)

            def shared(t, lead=True):
                for i in range(NSH):
                    if isinstance(t, int) and t == 0:
                        pe.wait_ge(ws_ready, i + 1)
                    up(t, i, i)
                x_transposes(t + 1)
                if lead:
                    if not (isinstance(t, int) and t <= 1):
                        pe.wait_ge(x2_done, t - 1)
                    down(t - 1, range(NSH))
                h_transposes((t + 1) * NSH, NSH)

            def routed(r, par, before_par=None, last=False):
                up(r + NT, 0, par)
                if not last:
                    x_transposes(r + NT + 1)
                if before_par is not None:
                    if not (isinstance(r, int) and r == 1):
                        pe.wait_ge(y_copied, r - 1)
                    down(r + NT - 1, (before_par,))
                h_transposes(r + NT * NSH + 1, 1)

            x_transposes(0)
            for t in range(2 * NC + 1):
                shared(t, t > 0)
            pe.wait_ge(asum_done, 2 * NC)
            pe.matmul(s_ps[:, 0:2 * NC], fones[:], asum[:].rearrange("p i c -> p (i c)"), start=True,
                      stop=True).then_inc(asum_full, 1)
            with pe.Fori(2 * NC + 1, NT - 1) as t:
                shared(t)
            for i in range(NSH):
                up(NT - 1, i, i)
            pe.wait_ge(x2_done, NT - 2)
            down(NT - 2, range(NSH))
            h_transposes(NT * NSH, NSH)
            pe.wait_ge(x2_done, NT - 1)
            down(NT - 1, range(NSH))
            x_transposes(NT)
            pe.wait_ge(x2_done, NT)
            for q in range(E):
                ring = (q + NSH) % WB
                pe.wait_ge(w_ready, q + 1)
                if q == 0:
                    routed(0, ring)
                    routed(1, ring, ring)
                    pe.wait_ge(bounds_done, 1)
                    first_tile = 2
                else:
                    first_tile = bound(pe, q)
                    routed(first_tile, ring, (ring - 1) % WB)
                    first_tile = first_tile + 1
                end = bound(pe, q + 1)
                final = q == E - 1
                with pe.Fori(first_tile, end - 1 if final else end) as r:
                    routed(r, ring, ring)
                if final:
                    routed(end - 1, ring, ring, True)
                    pe.wait_ge(y_copied, end - 1)
                    down(end + (NT - 1), (ring,))


def fuse(nc, n):
    B, C, D, KD, NT, TB = n.B, n.C, n.D, n.KD, n.NT, n.TB
    ident, tg, gate, slot = n.ident, n.tg, n.gate, n.slot

    with ExitStack() as ctx:
        def sb(name, shape, dt=F32):
            return ctx.enter_context(nc.sbuf_tensor(name, shape, dt))

        def sem(name):
            return ctx.enter_context(nc.semaphore(name))

        def psum(name, shape):
            return ctx.enter_context(nc.psum_tensor(name, shape, F32))

        x1 = sb("f_x1", [P, 2, TB, D])
        x2 = sb("f_x2", [P, 2, TB, D])
        y1 = sb("y1", [P, 2, TB, D])
        y2 = sb("y2", [P, 2, TB, D])
        ycol = sb("ycol", [P, 2, 2, TB], U32)
        gcol = sb("gcol", [P, 2, 2, TB])
        cwr = sb("cwr", [P, n.KF, 3])
        craw = sb("f_craw", [C, 2, D])
        ctraw = sb("f_ctraw", [P, 2, KD, C])
        xn = sb("f_xn", [P, TB, D])
        xT = sb("f_xT", [P, TB, KD, P])
        pr = sb("pr", [P, TB, C])
        prT = sb("prT", [C, TB, P])
        x3 = sb("x3", [P, TB, D])
        xq = sb("xq", [P, TB, D])
        xd = sb("xd", [P, TB, D])
        st = sb("f_st", [P, 2, TB, 6])
        mv = sb("f_mv", [P, 2, TB, 2])
        ve = sb("f_ve", [P, 2, TB])
        rs = sb("f_rs", [P, 2, TB])
        nmr = sb("nmr", [P, 2, TB])
        nm = sb("nm", [P, TB])
        su = sb("su", [P, TB])
        ri = sb("f_ri", [P, TB])
        rt = sb("rt", [P, TB])
        am = sb("am", [P, TB])
        ami = sb("ami", [P, TB])
        sc = sb("sc", [P, TB])
        dq = sb("dq", [P, TB])
        half = sb("f_half", [P, TB])
        eps = sb("f_eps", [P, TB])
        t_ps = psum("f_t_ps", [P, 2, KD, P])
        s_ps = psum("f_s_ps", [P, TB, P])
        p_ps = psum("f_p_ps", [P, TB, P])
        o_ps = psum("f_o_ps", [P, 2, D])

        x2_in = [sem("x2_in0"), sem("x2_in1")]
        ctx_in = [sem("f_ctx_in0"), sem("f_ctx_in1")]
        y_in = [sem("y_in0"), sem("y_in1")]
        consts = sem("f_consts")
        ycol_done = sem("ycol_done")
        gcol_done = sem("gcol_done")
        fw_in = sem("fw_in")
        cwr_in = sem("cwr_in")
        comb = sem("comb")
        st_done = sem("f_st_done")
        mv1_done = sem("f_mv1_done")
        mv2_done = sem("f_mv2_done")
        ve_done = sem("f_ve_done")
        rs1_done = sem("f_rs1_done")
        rs2_done = sem("f_rs2_done")
        nmr1_done = sem("nmr1_done")
        nmr2_done = sem("nmr2_done")
        xn_done = sem("f_xn_done")
        t_full = sem("f_t_full")
        t_copied = sem("f_t_copied")
        s_full = sem("f_s_full")
        nm_done = sem("nm_done")
        e_done = sem("f_e_done")
        p_full = sem("p_full")
        p_copied = sem("p_copied")
        ri_done = sem("f_ri_done")
        rt_done = sem("rt_done")
        o_full = sem("o_full")
        x3_done = sem("x3_done")
        x4_done = sem("x4_done")
        am_done = sem("am_done")
        amc_done = sem("amc_done")
        ami_done = sem("ami_done")
        sc_done = sem("sc_done")
        q_done = sem("q_done")
        xd_done = sem("xd_done")
        x3_out = sem("x3_out")
        xd_out = sem("xd_out")

        def steps(eng, run, straight=3):
            run(-1, False, False, True, 1)
            run(0, False, True, True, 0)
            last = B // 2 - straight // 2
            if last > 1:
                with eng.Fori(1, last) as i:
                    run(i * 2 - 1, True, True, True, 1)
                    run(i * 2, True, True, True, 0)
            for s in range(last * 2 - 1, B + 1):
                run(s, True, s < B, s < B - 1, s % 2)

        def whole(eng, run):
            steps(eng, run, 1)

        def loads(s):
            return not isinstance(s, int) or 0 <= s < B - 2

        def half_of(s):
            return (s + 1) // 2 if not isinstance(s, int) or s >= 0 else 0

        assert B % 2 == 0 and B >= 4
        block = ctx.enter_context(nc.Block())

        @block.sync
        def _(sp):
            def load(b, par):
                sp.dma_start(x2[:, par], n.tile_rows(n.x2_d, b * TB, TB)).then_inc(x2_in[par], 16)

            def load_ctx(b, par):
                sp.dma_start(craw[:, par], n.ctx[ds(b, 1)].rearrange("o c d -> c (o d)")).then_inc(ctx_in[par], 16)
                sp.dma_start(ctraw[:, par], n.ctxT[:, :, ds(b * C, C)]).then_inc(ctx_in[par], 16)

            def run(s, back, mid, front, par):
                if mid:
                    if loads(s):
                        sp.wait_ge(comb, (s + 1) * 2 * TB)
                        load(s + 2, par)
                    sp.wait_ge(x3_done, (s + 1) * TB)
                    sp.dma_start(n.tile_rows(n.x3_d, s * TB, TB), x3[:]).then_inc(x3_out, 16)
                    if loads(s):
                        load_ctx(s + 2, par)
                if back:
                    sp.wait_ge(xd_done, s * TB)
                    sp.dma_start(n.tile_rows(n.xd_d, (s - 1) * TB, TB), xd[:]).then_inc(xd_out, 16)

            for b in range(2):
                load(b, b)
                load_ctx(b, b)
            sp.dma_start(cwr[:], n.conv_w).then_inc(cwr_in, 16)
            sp.dma_start(n.cb[:], n.conv_b).then_inc(cwr_in, 16)
            steps(sp, run)
            sp.wait_ge(x3_out, B * 16)
            sp.wait_ge(xd_out, B * 16)

        @block.gpsimd
        def _(pool):
            def gather(b, par):
                pool.tensor_copy(ycol[:, par], slot[:, :, ds(b * TB, TB)]).then_inc(ycol_done, 1)
                hold(pool, ycol_done, b + 1, n.passed_pool)
                for i, y in enumerate((y1, y2)):
                    for j in range(TB):
                        pool.indirect_dma_start(out=y[:, par, j], out_offset=None, in_=n.ys_d[:, :],
                                                in_offset=bass.IndirectOffsetOnAxis(ap=ycol[:, par, i, j:j + 1], axis=0)
                                                ).then_inc(y_in[par], 16)

            def rstd(which, mv_sem, count, out_sem, ve_count):
                pool.wait_ge(mv_sem, count)
                pool.tensor_tensor(ve[:, which], mv[:, which, :, 1], eps[:], ALU.add).then_inc(ve_done, 1)
                pool.wait_ge(ve_done, ve_count)
                pool.tensor_tensor(rs[:, which], ve[:, which], half[:], ALU.pow).then_inc(out_sem, 1)

            def run(s, back, mid, front, par):
                if loads(s):
                    hold(pool, comb, (s + 1) * 2 * TB, n.passed_pool)
                    gather(s + 2, par)
                if isinstance(s, int) and s == 0:
                    pool.dma_start(n.w1q[:].rearrange("p k f -> p (k f)"), n.w1q_d[:, :]).then_inc(fw_in, 16)
                    pool.dma_start(n.w2q[:].rearrange("p k f -> p (k f)"), n.w2q_d[:, :]).then_inc(fw_in, 16)
                if front:
                    if mid:
                        pool.wait_ge(xn_done, (s + 1) * TB)
                    rstd(0, mv1_done, (s + 2) * TB, rs1_done, s * 2 + 2 if mid else 1)
                if mid:
                    rstd(1, mv2_done, (s + 1) * TB, rs2_done, s * 2 + (3 if front else 2))

            pool.memset(half[:], -0.5)
            pool.memset(eps[:], EPS_LN)
            gather(0, 0)
            gather(1, 1)
            pool.wait_ge(cwr_in, 32)
            pool.tensor_scalar(n.cw[:], cwr[:], n.mean[:, 0:1], None, ALU.mult)
            pool.tensor_scalar(n.g2[:], n.mean[:, 1:2], tg[:, 3:4], 1.0 / 127.0, ALU.mult, ALU.mult)
            steps(pool, run)
            pool.wait_ge(fw_in, 32)

        @block.scalar
        def _(act):
            def run(s, back, mid, front, par):
                if mid:
                    for j in range(TB):
                        act.wait_ge(t_full, s * TB + j + 1)
                        act.activation(xT[:, j], t_ps[:, j % 2], ACT.Copy).then_inc(t_copied, 1)
                if back:
                    act.wait_ge(nmr2_done, s)
                    if not (isinstance(s, int) and s == 1):
                        act.wait_ge(xd_done, (s - 1) * TB)
                    for j in range(TB):
                        act.activation(xq[:, j], x3[:, j], ACT.Identity, bias=nmr[:, 1, j:j + 1],
                                       scale=rs[:, 1, j:j + 1]).then_inc(x4_done, 1)
                if mid:
                    act.wait_ge(nm_done, s + 1)
                    for j in range(TB):
                        act.activation(pr[:, j], s_ps[:, j, 0:C], ACT.Exp, bias=nm[:, j:j + 1],
                                       accum_out=su[:, j:j + 1]).then_inc(e_done, 1)
                    act.wait_ge(p_full, s + 1)
                    act.activation(prT[:], p_ps[0:C], ACT.Copy).then_inc(p_copied, 1)
                if back:
                    act.wait_ge(sc_done, s)
                    for j in range(TB):
                        act.activation(xq[:, j], xq[:, j], ACT.Copy, bias=MAGIC, scale=sc[:, j:j + 1]).then_inc(q_done, 1)
                if front:
                    act.wait_ge(nmr1_done, s + 2)
                    for j in range(TB):
                        act.activation(xn[:, j], x1[:, 1 - par, j], ACT.Identity, bias=nmr[:, 0, j:j + 1],
                                       scale=rs[:, 0, j:j + 1]).then_inc(xn_done, 1)

            whole(act, run)

        @block.vector
        def _(dve):
            def stats(which, src, mv_sem, base):
                for j in range(TB):
                    dve.bn_stats(st[:, which, j], src[:, j]).then_inc(st_done, 1)
                aggregate(which, mv_sem, base)

            def aggregate(which, mv_sem, base):
                for j in range(TB):
                    hold(dve, st_done, base + j + 1, n.passed_dve)
                    dve.bn_aggr(mv[:, which, j], st[:, which, j]).then_inc(mv_sem, 1)

            def dequantise(s, j):
                if j == 0 and not (isinstance(s, int) and s == 1):
                    dve.wait_ge(xd_out, (s - 1) * 16)
                dve.wait_ge(q_done, (s - 1) * TB + j + 1)
                dve.tensor_scalar(xd[:, j], xq[:, j], MAGIC, dq[:, j:j + 1], ALU.subtract, ALU.mult).then_inc(xd_done, 1)

            def combine_first(o):
                for j in range(TB):
                    dve.scalar_tensor_tensor(out=y1[:, o, j], in0=y1[:, o, j], scalar=gcol[:, o, 0, j:j + 1],
                                             in1=x2[:, o, j], op0=ALU.mult, op1=ALU.add).then_inc(comb, 1)

            def combine_second(s, o):
                for j in range(TB):
                    dve.wait_ge(comb, (s + 1) * 2 * TB + j + 1)
                    dve.scalar_tensor_tensor(out=x1[:, o, j], in0=y2[:, o, j], scalar=gcol[:, o, 1, j:j + 1],
                                             in1=y1[:, o, j], op0=ALU.mult, op1=ALU.add).then_inc(comb, 1)

            def run(s, back, mid, front, par):
                o = 1 - par
                if front:
                    dve.tensor_copy(gcol[:, o], gate[:, :, ds((s + 1) * TB, TB)]).then_inc(gcol_done, 1)
                    dve.wait_ge(gcol_done, s + 2)
                    dve.wait_ge(y_in[o], half_of(s) * 32 * TB + 32 * TB)
                    dve.wait_ge(x2_in[o], half_of(s) * 16 + 16)
                    combine_first(o)
                if back:
                    dve.wait_ge(rs2_done, s)
                    dve.scalar_tensor_tensor(out=nmr[:, 1], in0=mv[:, 1, :, 0], scalar=-1.0, in1=rs[:, 1], op0=ALU.mult,
                                             op1=ALU.mult).then_inc(nmr2_done, 1)
                if front:
                    combine_second(s, o)
                if back:
                    for j in range(TB):
                        dve.wait_ge(x4_done, (s - 1) * TB + j + 1)
                        dve.tensor_reduce(am[:, j:j + 1], xq[:, j], AX.X, ALU.max, apply_absolute_value=True).then_inc(am_done, 1)
                    dve.wait_ge(am_done, s * TB)
                    dve.tensor_scalar(am[:], am[:], EPS_Q, None, ALU.max).then_inc(amc_done, 1)
                    dve.wait_ge(amc_done, s)
                    dve.reciprocal(ami[:], am[:]).then_inc(ami_done, 1)
                    dve.tensor_scalar(dq[:], am[:], 1.0 / 127.0, None, ALU.mult)
                    dve.wait_ge(ami_done, s)
                    dve.tensor_scalar(sc[:], ami[:], 127.0, None, ALU.mult).then_inc(sc_done, 1)
                if mid:
                    dve.wait_ge(s_full, s + 1)
                    dve.tensor_reduce(nm[:], s_ps[:, :, 0:C], AX.X, ALU.max, negate=True).then_inc(nm_done, 1)
                if front:
                    dve.wait_ge(comb, (s + 2) * 2 * TB)
                    stats(0, x1[:, o], mv1_done, s * 2 * TB + TB if mid else 0)
                if front:
                    dve.wait_ge(rs1_done, s + 2)
                    dve.scalar_tensor_tensor(out=nmr[:, 0], in0=mv[:, 0, :, 0], scalar=-1.0, in1=rs[:, 0], op0=ALU.mult,
                                             op1=ALU.mult).then_inc(nmr1_done, 1)
                if mid:
                    dve.wait_ge(e_done, s * TB + TB)
                    dve.reciprocal(ri[:], su[:]).then_inc(ri_done, 1)
                    dve.wait_ge(ri_done, s + 1)
                    dve.tensor_scalar(rt[:], ri[:], tg[:, 1:2], None, ALU.mult).then_inc(rt_done, 1)
                    dve.wait_ge(rt_done, s + 1)
                    if not (isinstance(s, int) and s == 0):
                        dve.wait_ge(x3_out, s * 16)
                    for j in range(TB):
                        dve.wait_ge(o_full, s * TB + j + 1)
                        dve.scalar_tensor_tensor(out=x3[:, j], in0=o_ps[:, j % 2], scalar=rt[:, j:j + 1], in1=x1[:, par, j],
                                                 op0=ALU.mult, op1=ALU.add).then_inc(x3_done, 1)
                        if back:
                            dequantise(s, j)
                        dve.wait_ge(x3_done, s * TB + j + 1)
                        dve.bn_stats(st[:, 1, j], x3[:, j]).then_inc(st_done, 1)
                    aggregate(1, mv2_done, s * 2 * TB + (2 * TB if front else TB))
                elif back:
                    for j in range(TB):
                        dequantise(s, j)

            whole(dve, run)

        @block.tensor
        def _(pe):
            def run(s, back, mid, front, par):
                if not mid:
                    return
                for j in range(TB):
                    pe.wait_ge(xn_done, s * TB + j + 1)
                    if not (isinstance(s, int) and s * TB + j < 2):
                        pe.wait_ge(t_copied, s * TB + j - 1)
                    for k in range(KD):
                        mm = pe.transpose(t_ps[:, j % 2, k], xn[:, j, k * P:(k + 1) * P], ident[:])
                    mm.then_inc(t_full, 1)
                pe.wait_ge(ctx_in[par], half_of(s - 1) * 32 + 32)
                for j in range(TB):
                    pe.wait_ge(t_copied, s * TB + j + 1)
                    for k in range(KD):
                        mm = pe.matmul(s_ps[:, j, 0:C], xT[:, j, k], ctraw[:, par, k], start=(k == 0), stop=(k == KD - 1))
                mm.then_inc(s_full, 1)
                pe.wait_ge(e_done, s * TB + TB)
                for j in range(TB):
                    mm = pe.transpose(p_ps[0:C, j], pr[:, j], ident[:])
                mm.then_inc(p_full, 1)
                pe.wait_ge(p_copied, s + 1)
                for j in range(TB):
                    if not (isinstance(s, int) and s * TB + j < 2):
                        pe.wait_ge(x3_done, s * TB + j - 1)
                    pe.matmul(o_ps[:, j % 2], prT[:, j], craw[:, par], start=True, stop=True).then_inc(o_full, 1)

            whole(pe, run)


def ffn(nc, n):
    B, S, D, KD, NT, TB, DH, KF = n.B, n.S, n.D, n.KD, n.NT, n.TB, n.DH, n.KF
    ident, w1q, w2q, cw, cb, g2 = n.ident, n.w1q, n.w2q, n.cw, n.cb, n.g2
    RING = 4

    with ExitStack() as ctx:
        def sb(name, shape, dt=F32, c=ctx):
            return c.enter_context(nc.sbuf_tensor("b_" + name, shape, dt))

        def sem(name, c=ctx):
            return c.enter_context(nc.semaphore("b_" + name))

        xd = sb("xd", [P, TB, D])
        xdT = sb("xdT", [P, 2, KD, TB, P], FR)
        av = sb("av", [P, RING, S])
        h = sb("h", [P, 2, KF, S])
        hq = sb("hq", [P, KF, S], BF16)
        am = sb("am", [P, S])
        mx = sb("mx", [P, TB])
        mxc = sb("mxc", [P, TB])
        mi = sb("mi", [P, TB])
        s2 = sb("s2", [P, TB])
        d2 = sb("d2", [P, 2, TB])
        srow = sb("srow", [P, S])
        x3 = sb("x3", [P, 2, TB, D])
        f_ps = ctx.enter_context(nc.psum_tensor("b_f_ps", [P, RING, 512], F32))
        t_ps = ctx.enter_context(nc.psum_tensor("b_t_ps", [P, 512], F32))
        q_ps = ctx.enter_context(nc.psum_tensor("b_q_ps", [P, TB, P], F32))
        o_ps = ctx.enter_context(nc.psum_tensor("b_o_ps", [P, 2, D], F32))

        xd_in = sem("xd_in")
        x3_in = [sem("x3_in0"), sem("x3_in1")]
        t_full = sem("t_full")
        t_hi = sem("t_hi")
        t_lo = sem("t_lo")
        f_full = sem("f_full")
        mid_tap = sem("mid_tap")
        prev_tap = sem("prev_tap")
        conv_done = sem("conv_done")
        h_done = sem("h_done")
        am_done = sem("am_done")
        amt_full = sem("amt_full")
        scale_steps = sem("scale_steps")
        row_full = sem("row_full")
        row_done = sem("row_done")
        u_done = sem("u_done")
        own_u = sem("own_u")
        hq_done = sem("hq_done")
        o_full = sem("o_full")
        o_done = sem("o_done")
        out_done = sem("out_done")

        def whole(run):
            def steps(eng):
                run(-1, False, False, False, True, 1)
                run(0, True, False, False, True, 0)
                run(1, True, True, False, True, 1)
                run(2, True, True, True, True, 0)
                run(3, True, True, True, B > 4, 1)
                if B > 4:
                    with eng.Fori(2, B // 2 - 1) as i:
                        run(i * 2, True, True, True, True, 0)
                        run(i * 2 + 1, True, True, True, True, 1)
                    run(B - 2, True, True, True, True, 0)
                    run(B - 1, True, True, True, False, 1)
                run(B, False, True, True, False, 0)
                run(B + 1, False, False, True, False, 1)
            return steps

        def transposed(j):
            return (f_ps[:, j - 1] if j else t_ps[:]).rearrange("p (k t) -> p k t", t=P)

        assert B % 2 == 0 and B >= 4 and KF == 16 and TB == RING
        rounds = {6: (0,), 7: (1,), 8: (2,), 9: (3, 4), 10: (5,), 11: (6, 7), 12: (8,), 13: (9, 10), 14: (11, 12),
                  15: (13, 14, 15)}
        block = ctx.enter_context(nc.Block())

        @block.sync
        def _(sp):
            def run(s, f1, quant, f2, front, par):
                if front:
                    if not (isinstance(s, int) and s < 0):
                        sp.wait_ge(t_full, (s + 1) * TB)
                    sp.dma_start(xd[:], n.tile_rows(n.xd_d, (s + 1) * TB, TB)).then_inc(xd_in, 16)
                if quant:
                    if not (isinstance(s, int) and s < 3):
                        sp.wait_ge(out_done, (s - 2) * 16)
                    sp.dma_start(x3[:, 1 - par], n.tile_rows(n.x3_d, (s - 1) * TB, TB)).then_inc(x3_in[1 - par], 16)
                if f2:
                    sp.wait_ge(o_done, (s - 1) * TB)
                    sp.dma_start(n.tile_rows(n.out, (s - 2) * TB, TB), x3[:, par]).then_inc(out_done, 16)

            whole(run)(sp)
            sp.wait_ge(out_done, B * 16)

        @block.gpsimd
        def _(pool):
            def run(s, f1, quant, f2, front, par):
                if not quant:
                    return
                for m in range(0, KF, 1 if f1 else 2):
                    if m == 0:
                        pool.wait_ge(row_done, s)
                    pool.tensor_tensor(h[:, 1 - par, m], h[:, 1 - par, m], srow[:], ALU.mult).then_inc(u_done, 1)

            whole(run)(pool)

        @block.scalar
        def _(act):
            def run(s, f1, quant, f2, front, par):
                def silu(m):
                    act.wait_ge(conv_done, s * KF + m + 1)
                    if not (isinstance(s, int) and s < 2):
                        act.wait_ge(hq_done, (s - 2) * KF + m + 1)
                    act.activation(h[:, par, m], av[:, m % RING], ACT.Silu).then_inc(h_done, 1)

                for m in range(KF):
                    if f1:
                        act.wait_ge(f_full, s * KF + m + 1)
                        if m >= RING or not (isinstance(s, int) and s == 0):
                            act.wait_ge(h_done, s * KF + m + 1 - RING)
                        act.activation(av[:, m % RING], f_ps[:, m % RING], ACT.Identity, bias=cb[:, m:m + 1],
                                       scale=cw[:, m, 1:2]).then_inc(mid_tap, 1)
                        if m >= 1:
                            silu(m - 1)
                    if quant and m == 5:
                        act.wait_ge(row_full, s)
                        if not (isinstance(s, int) and s == 1):
                            act.wait_ge(u_done, (s - 1) * KF)
                        act.activation(srow[:], q_ps[:], ACT.Copy).then_inc(row_done, 1)
                if f1:
                    silu(KF - 1)
                if front:
                    for j in range(TB):
                        act.wait_ge(t_full, (s + 1) * TB + j + 1)
                        act.activation(xdT[:, 0, :, j], transposed(j), ACT.Copy).then_inc(t_hi, 1)

            whole(run)(act)

        @block.vector
        def _(dve):
            def run(s, f1, quant, f2, front, par):
                def outputs(j):
                    dve.wait_ge(o_full, (s - 2) * TB + j + 1)
                    dve.wait_ge(x3_in[par], s // 2 * 16)
                    dve.scalar_tensor_tensor(out=x3[:, par, j], in0=o_ps[:, j % 2] if quant else f_ps[:, j], scalar=d2[:, par, j:j + 1],
                                             in1=x3[:, par, j], op0=ALU.mult, op1=ALU.add).then_inc(o_done, 1)

                def round_tile(m):
                    if f1:
                        dve.wait_ge(u_done, (s - 1) * KF + m + 1)
                    elif m % 2:
                        dve.wait_ge(own_u, m // 2 + 1)
                    else:
                        dve.wait_ge(row_done, s)
                        dve.tensor_tensor(h[:, 1 - par, m + 1], h[:, 1 - par, m + 1], srow[:], ALU.mult).then_inc(own_u, 1)
                        dve.wait_ge(u_done, (s - 1) * KF + m // 2 + 1)
                    if m == 0 and not (isinstance(s, int) and s == 1):
                        dve.wait_ge(o_full, (s - 1) * TB)
                    dve.tensor_scalar(hq[:, m], h[:, 1 - par, m], MAGIC, MAGIC, ALU.add, ALU.subtract).then_inc(hq_done, 1)

                if quant:
                    dve.wait_ge(h_done, s * KF)
                    dve.tensor_reduce(am[:], h[:, 1 - par].rearrange("p m t -> p t m"), AX.X, ALU.max,
                                      apply_absolute_value=True).then_inc(am_done, 1)
                if f2:
                    outputs(0)
                    outputs(1)
                for m in range(KF + 1):
                    if f1 and m < KF:
                        u = s * KF + m + 1
                        dve.wait_ge(mid_tap, u)
                        a, f = av[:, m % RING], f_ps[:, m % RING]
                        dve.scalar_tensor_tensor(out=a[:, 1:S], in0=f[:, 0:S - 1], scalar=cw[:, m, 0:1], in1=a[:, 1:S],
                                                 op0=ALU.mult, op1=ALU.add).then_inc(prev_tap, 1)
                        dve.wait_ge(prev_tap, u)
                        dve.scalar_tensor_tensor(out=a[:, 0:S - 1], in0=f[:, 1:S], scalar=cw[:, m, 2:3], in1=a[:, 0:S - 1],
                                                 op0=ALU.mult, op1=ALU.add).then_inc(conv_done, 1)
                    if f2 and m in (1, 3):
                        outputs(2 + m // 2)
                    if quant and m == 2:
                        dve.wait_ge(amt_full, s)
                        dve.tensor_reduce(mx[:], q_ps[:], AX.X, ALU.max).then_inc(scale_steps, 1)
                        dve.wait_ge(scale_steps, s * 4 - 3)
                        dve.tensor_scalar(mxc[:], mx[:], EPS_Q, None, ALU.max).then_inc(scale_steps, 1)
                        dve.wait_ge(scale_steps, s * 4 - 2)
                        dve.reciprocal(mi[:], mxc[:]).then_inc(scale_steps, 1)
                        dve.tensor_scalar(d2[:, 1 - par], mxc[:], g2[:], None, ALU.mult)
                        dve.wait_ge(scale_steps, s * 4 - 1)
                        dve.tensor_scalar(s2[:], mi[:], 127.0, None, ALU.mult).then_inc(scale_steps, 1)
                    if m == KF and front:
                        transposed_low(s + 1)
                    if quant:
                        for r in rounds.get(m, ()):
                            round_tile(r)

            def transposed_low(b):
                for j in range(TB):
                    dve.wait_ge(t_hi, b * TB + j + 1)
                    dve.tensor_tensor(xdT[:, 1, :, j], transposed(j), xdT[:, 0, :, j].bitcast(F32),
                                      ALU.subtract).then_inc(t_lo, 1)

            whole(run)(dve)

        @block.tensor
        def _(pe):
            def run(s, f1, quant, f2, front, par):
                def down(j):
                    u = (s - 2) * TB + j
                    if j == 0:
                        pe.wait_ge(hq_done, (s - 1) * KF)
                    if not (isinstance(s, int) and s == 2 and j < 2):
                        pe.wait_ge(o_done, u - 1)
                    for k in range(KF):
                        mm = pe.matmul(o_ps[:, j % 2], hq[:, k, j * P:(j + 1) * P], w2q[:, k, :], start=(k == 0),
                                       stop=(k == KF - 1))
                    mm.then_inc(o_full, 1)

                if f2 and not quant:
                    for k in range(KF):
                        pe.wait_ge(hq_done, (s - 2) * KF + k + 1)
                        for j in range(TB):
                            mm = pe.matmul(f_ps[:, j], hq[:, k, j * P:(j + 1) * P], w2q[:, k, :], start=(k == 0),
                                           stop=(k == KF - 1))
                            if k == KF - 1:
                                mm.then_inc(o_full, 1)
                    return
                if f2:
                    down(0)
                    down(1)
                for m in range(KF):
                    if f1:
                        if m == 0:
                            pe.wait_ge(t_lo, (s + 1) * TB)
                        if m >= RING:
                            pe.wait_ge(conv_done, s * KF + m + 1 - RING)
                        for k in range(KD):
                            for part in range(2):
                                mm = pe.matmul(f_ps[:, m % RING], w1q[:, k, m * P:(m + 1) * P], xdT[:, part, k],
                                               start=(k == 0 and part == 0), stop=(k == KD - 1 and part == 1))
                        mm.then_inc(f_full, 1)
                    if f2 and m in (1, 3):
                        down(2 + m // 2)
                    if quant and m == 2:
                        pe.wait_ge(am_done, s)
                        if not (isinstance(s, int) and s == 1):
                            pe.wait_ge(row_done, s - 1)
                        for j in range(TB):
                            mm = pe.transpose(q_ps[:, j], am[:, j * P:(j + 1) * P], ident[:])
                        mm.then_inc(amt_full, 1)
                    if quant and m == 4:
                        pe.wait_ge(scale_steps, s * 4)
                        for j in range(TB):
                            mm = pe.matmul(q_ps[:, j], s2[:, j:j + 1].to_broadcast([P, P]), ident[:], start=True, stop=True)
                        mm.then_inc(row_full, 1)
                if front:
                    pe.wait_ge(xd_in, (s + 2) * 16)
                    for j in range(TB):
                        if f1 and j:
                            pe.wait_ge(conv_done, (s + 1) * KF - RING + j)
                        for k in range(KD):
                            mm = pe.transpose(transposed(j)[:, k], xd[:, j, k * P:(k + 1) * P], ident[:])
                        mm.then_inc(t_full, 1)

            whole(run)(pe)


def kernel(x, ctx_1024, g_xattn, g_ffn, L0_xattn_Wq, L0_xattn_bq, L0_xattn_Wk, L0_xattn_bk, L0_xattn_Wv,
           L0_xattn_bv, L0_xattn_Wo, L0_xattn_bo, L0_ffn_router_w, L0_ffn_router_b, L0_ffn_routed_w1,
           L0_ffn_routed_w3, L0_ffn_routed_w2, L0_ffn_shared_w1, L0_ffn_shared_w3, L0_ffn_shared_w2,
           L1_ffn_w1, L1_ffn_conv_w, L1_ffn_conv_b, L1_ffn_w2):
    import numpy as np
    import concourse.bacc as bacc
    from concourse.bass_utils import run_bass_kernel_spmd

    def rows(w):
        w = np.asarray(w)
        return np.swapaxes(w.reshape(*w.shape[:-2], w.shape[-2] // P, P, w.shape[-1]), -3, -2)

    def columns(v):
        return np.asarray(v).reshape(-1, P).T

    x, c = np.asarray(x), np.asarray(ctx_1024)
    B, S, D = x.shape
    w13 = np.concatenate([np.concatenate([L0_ffn_shared_w1, L0_ffn_shared_w3], -1),
                          np.concatenate([L0_ffn_routed_w1, L0_ffn_routed_w3], -1)])
    w2 = np.concatenate([L0_ffn_shared_w2, L0_ffn_routed_w2])
    w1 = np.asarray(L1_ffn_w1)
    ins = {
        "x": x.reshape(B * S, D),
        "ctx": c,
        "ctxT": rows(c.reshape(-1, D).T),
        "gates": np.concatenate([g_xattn, g_ffn]),
        "wqT": rows(np.asarray(L0_xattn_Wq).T),
        "wkT": rows(np.asarray(L0_xattn_Wk).T),
        "wvT": rows(np.asarray(L0_xattn_Wv).T),
        "woT": rows(np.asarray(L0_xattn_Wo).T),
        "bq": columns(L0_xattn_bq),
        "bk": columns(L0_xattn_bk),
        "bv": np.asarray(L0_xattn_bv),
        "bo": np.asarray(L0_xattn_bo),
        "router_w": rows(L0_ffn_router_w),
        "router_b": np.asarray(L0_ffn_router_b),
        "w13": rows(w13),
        "w2e": rows(w2),
        "w1T": rows(w1.T),
        "conv_w": np.asarray(L1_ffn_conv_w).reshape(-1, P, 3).swapaxes(0, 1),
        "conv_b": columns(L1_ffn_conv_b),
        "w2T": rows(np.asarray(L1_ffn_w2).T),
    }
    nc = bacc.Bacc("TRN2", target_bir_lowering=False, num_devices=1)
    arrays, aps = {}, {}
    for name, a in ins.items():
        a = np.ascontiguousarray(a)
        arrays[f"in_{name}"] = a
        aps[name] = nc.dram_tensor(f"in_{name}", a.shape, mybir.dt.from_np(a.dtype), kind="ExternalInput").ap()
    out = nc.dram_tensor("out", (B * S, D), F32, kind="ExternalOutput").ap()
    flamingo(nc, **aps, out=out)
    r = run_bass_kernel_spmd(nc, [arrays], core_ids=[0])
    return r.results[0]["out"].reshape(B, S, D)
```
